# Optimizing a Trainium2 kernel written in Bass

```python
import numpy as np
import jax
import jax.numpy as jnp

def _softmax(x, axis=-1):
    return jax.nn.softmax(x, axis=axis)

def _gelu(x):
    return jax.nn.gelu(x, approximate=True)

def _silu(x):
    return jax.nn.silu(x)

def _sigmoid(x):
    return jax.nn.sigmoid(x)

def _layernorm(x, axis=-1, eps=1e-05):
    m = jnp.mean(x, axis=axis, keepdims=True)
    v = jnp.var(x, axis=axis, keepdims=True)
    return (x - m) / jnp.sqrt(v + eps)

def _scatter_add(tgt, idx, src, axis=0):
    return tgt.at[idx].add(src)

def _segment_sum(src, seg, n):
    return jax.ops.segment_sum(src, seg, n)
kernel_name = 'mk_flamingo_gated_d4_seqx_r8_90d912'

def setup_inputs(seed: int=0):
    np.random.seed(seed)
    _w = jnp.asarray

    def _rec_inputs():
        import jax
        import jax.numpy as jnp
        _rk = jax.random.key(seed)
        x = -0.0002928 + 1 * jax.random.normal(jax.random.fold_in(_rk, 1), (8, 256, 128), jnp.float32)
        _lenS = 256 - jax.random.randint(jax.random.fold_in(_rk, 7), (8,), 0, max(1, 256 // 4) + 1, jnp.int32)
        _lenS2 = 256 - jax.random.randint(jax.random.fold_in(_rk, 8), (8,), 0, max(1, 256 // 4) + 1, jnp.int32)
        _ctx_1024P = jax.random.normal(jax.random.fold_in(_rk, 11), (8, 16, 128), jnp.float32)
        _ctx_1024c = jax.random.dirichlet(jax.random.fold_in(_rk, 511), 0.3 * jnp.ones((16,), jnp.float32), (8, 256))
        _ctx_1024t = jnp.einsum('bsk,bkd->bsd', _ctx_1024c, _ctx_1024P)
        _ctx_1024t = _ctx_1024t * jax.lax.rsqrt(jnp.mean(jnp.square(_ctx_1024t)) + 1e-12) * 0.953939
        ctx_1024 = -1.39393e-06 + 0.999914 * (_ctx_1024t + 0.3 * jax.random.normal(jax.random.fold_in(_rk, 611), (8, 256, 128), jnp.float32))
        _validS = jnp.arange(256)[None, :] < _lenS[:, None]
        _validS2 = jnp.arange(256)[None, :] < _lenS2[:, None]
        _causal = jnp.tril(jnp.ones((256, 256), dtype=bool))
        mask_Bx1xSxS2_ik1 = jnp.where(jnp.broadcast_to(_validS2[:, None, None, :], (8, 1, 256, 256)), 1, 0).astype(jnp.int32)
        mask_BxS2_bk0 = jnp.logical_not(jnp.broadcast_to(_validS2[:, :], (8, 256)))
        _g = jax.random.normal(jax.random.fold_in(_rk, 9001), (2, 4), jnp.float32)
        _g = jnp.sign(_g) * jnp.maximum(jnp.abs(_g), 1.0) + (_g == 0) * 1.0
        g_xattn = _g[0]
        g_ffn = _g[1]
        return (x, ctx_1024, mask_Bx1xSxS2_ik1, mask_BxS2_bk0, g_xattn, g_ffn)
    x, ctx_1024, mask_Bx1xSxS2_ik1, mask_BxS2_bk0, g_xattn, g_ffn = _rec_inputs()

    def _L0_xattn_setup():
        import jax, jax.numpy as jnp
        import numpy as np
        B, S, E, H = (2, 256, 128, 16)
        D = E // H
        key = jax.random.key(seed)
        ks = jax.random.split(key, 14)
        inp = {'query': jax.random.normal(ks[0], (B, S, E), jnp.float32), 'key': jax.random.normal(ks[1], (B, S, E), jnp.float32), 'value': jax.random.normal(ks[2], (B, S, E), jnp.float32), 'adj': jax.random.normal(ks[3], (S, S), jnp.float32), 'mask': jax.random.randint(ks[4], (B, 1, S, S), 0, 2, jnp.int32)}
        sc = 1.0 / np.sqrt(E)
        inp['Wq'] = jax.random.normal(ks[5], (E, E), jnp.float32) * sc
        inp['bq'] = jax.random.normal(ks[6], (E,), jnp.float32) * sc
        inp['Wk'] = jax.random.normal(ks[7], (E, E), jnp.float32) * sc
        inp['bk'] = jax.random.normal(ks[8], (E,), jnp.float32) * sc
        inp['Wv'] = jax.random.normal(ks[9], (E, E), jnp.float32) * sc
        inp['bv'] = jax.random.normal(ks[10], (E,), jnp.float32) * sc
        inp['Wo'] = jax.random.normal(ks[11], (E, E), jnp.float32) * sc
        inp['bo'] = jax.random.normal(ks[12], (E,), jnp.float32) * sc
        return inp
    _L0_xattn_all = _L0_xattn_setup()
    _L0_xattn_in = {k: v for k, v in _L0_xattn_all.items() if k in ('adj', 'Wq', 'bq', 'Wk', 'bk', 'Wv', 'bv', 'Wo', 'bo')}
    del _L0_xattn_all

    def _L0_ffn_setup():
        import jax, jax.numpy as jnp
        import numpy as np
        B, S, D, T = (4, 512, 128, 8)
        key = jax.random.key(seed)
        k1, k2, k3, k4 = jax.random.split(key, 4)
        x = jax.random.normal(k1, (B, S, D), dtype=jnp.float32)
        tile_sigs = jax.random.normal(k2, (T, D), dtype=jnp.float32)
        bound = 1.0 / np.sqrt(D)
        W = jax.random.uniform(k3, (T, D, D), minval=-bound, maxval=bound, dtype=jnp.float32)
        b = jax.random.uniform(k4, (T, D), minval=-bound, maxval=bound, dtype=jnp.float32)
        return {'x': x, 'tile_sigs': tile_sigs, 'W': W, 'b': b}
    _L0_ffn_all = _L0_ffn_setup()
    _L0_ffn_in = {k: v for k, v in _L0_ffn_all.items() if k in ('tile_sigs', 'W', 'b')}
    del _L0_ffn_all

    def _L1_xattn_setup():
        import jax, jax.numpy as jnp
        import numpy as np
        B, S, D, H = (2, 256, 128, 16)
        DK = D // H
        EPS = 1e-10
        ROPE_BASE = 500000.0

        def _rms_norm(x, w):
            return w * x * jax.lax.rsqrt(jnp.mean(x * x, axis=-1, keepdims=True) + EPS)

        def _rope_tables(seq_len, dk):
            inv_freq = 1.0 / ROPE_BASE ** (jnp.arange(0, dk, 2, dtype=jnp.float32) / dk)
            t = jnp.arange(seq_len, dtype=jnp.float32)
            freqs = jnp.outer(t, inv_freq)
            emb = jnp.concatenate([freqs, freqs], -1)
            return (jnp.cos(emb), jnp.sin(emb))

        def _rotate_half(x):
            x1, x2 = jnp.split(x, 2, axis=-1)
            return jnp.concatenate([-x2, x1], axis=-1)
        key = jax.random.key(seed)
        ks = jax.random.split(key, 8)
        scale = 1.0 / np.sqrt(D)
        return {'q': jax.random.normal(ks[0], (B, S, D), jnp.float32), 'k': jax.random.normal(ks[1], (B, S, D), jnp.float32), 'v': jax.random.normal(ks[2], (B, S, D), jnp.float32), 'Wq': jax.random.normal(ks[3], (D, D), jnp.float32) * scale, 'Wk': jax.random.normal(ks[4], (D, D), jnp.float32) * scale, 'Wv': jax.random.normal(ks[5], (D, D), jnp.float32) * scale, 'Wo': jax.random.normal(ks[6], (D, D), jnp.float32) * scale, 'q_norm_w': jnp.ones((DK,), jnp.float32) + 0.02 * jax.random.normal(ks[7], (DK,), jnp.float32), 'k_norm_w': jnp.ones((DK,), jnp.float32)}
    _L1_xattn_all = _L1_xattn_setup()
    _L1_xattn_in = {k: v for k, v in _L1_xattn_all.items() if k in ('Wq', 'Wk', 'Wv', 'Wo', 'q_norm_w', 'k_norm_w')}
    del _L1_xattn_all

    def _L1_ffn_setup():
        import jax, jax.numpy as jnp
        import numpy as np
        B, S, D_MODEL, D_FF, E, R, TOP_K = (4, 256, 128, 512, 8, 16, 2)
        key = jax.random.key(seed)
        ks = jax.random.split(key, 9)
        sd = 1.0 / np.sqrt(D_MODEL)
        return {'hidden_states': jax.random.normal(ks[0], (B, S, D_MODEL), jnp.float32), 'wi': jax.random.normal(ks[1], (D_FF, D_MODEL), jnp.float32) * sd, 'bi': jax.random.normal(ks[2], (D_FF,), jnp.float32) * 0.01, 'wo': jax.random.normal(ks[3], (D_MODEL, D_FF), jnp.float32) * (1.0 / np.sqrt(D_FF)), 'bo': jax.random.normal(ks[4], (D_MODEL,), jnp.float32) * 0.01, 'lora_A': jax.random.normal(ks[5], (E, R, D_MODEL), jnp.float32) * sd, 'lora_B': jax.random.normal(ks[6], (E, D_FF, R), jnp.float32) * 0.02, 'gate_w': jax.random.normal(ks[7], (E, D_MODEL), jnp.float32) * sd, 'gate_b': jax.random.normal(ks[8], (E,), jnp.float32) * 0.01}
    _L1_ffn_all = _L1_ffn_setup()
    _L1_ffn_in = {k: v for k, v in _L1_ffn_all.items() if k in ('wi', 'bi', 'wo', 'bo', 'lora_A', 'lora_B', 'gate_w', 'gate_b')}
    del _L1_ffn_all

    def _L2_xattn_setup():
        import jax, jax.numpy as jnp
        import numpy as np
        NUM_HEADS, NUM_KV, HEAD_DIM, WIDTH = (4, 1, 32, 128)
        MASK_FILL = -2.3819763e+38

        def _apply_rope(x, positions, max_wavelength=10000.0):
            d = x.shape[-1]
            freq_exp = 2.0 / d * jnp.arange(d // 2, dtype=jnp.float32)
            timescale = max_wavelength ** freq_exp
            radians = positions[..., None].astype(jnp.float32) / timescale
            radians = radians[..., None, :]
            sin, cos = (jnp.sin(radians), jnp.cos(radians))
            x1, x2 = jnp.split(x, 2, axis=-1)
            out = jnp.concatenate([x1 * cos - x2 * sin, x2 * cos + x1 * sin], axis=-1)
            return out.astype(x.dtype)

        def _rmsnorm(x, scale):
            var = jnp.mean(jnp.square(x.astype(jnp.float32)), axis=-1, keepdims=True)
            normed = x * jax.lax.rsqrt(var + 1e-06)
            return (normed * (1 + scale)).astype(x.dtype)
        key = jax.random.key(seed)
        ks = jax.random.split(key, 7)
        B, T, S = (8, 64, 256)
        return {'x': jax.random.normal(ks[0], (B, T, WIDTH), jnp.float32), 'mem_seq': jax.random.normal(ks[1], (B, S, WIDTH), jnp.float32), 'mem_mask': jax.random.randint(ks[2], (B, S), 0, 2).astype(bool), 'rms_scale': jax.random.normal(ks[3], (WIDTH,), jnp.float32) * 0.02, 'q_w': jax.random.normal(ks[4], (NUM_HEADS, WIDTH, HEAD_DIM), jnp.float32) / np.sqrt(WIDTH), 'kv_w': jax.random.normal(ks[5], (2, NUM_KV, WIDTH, HEAD_DIM), jnp.float32) / np.sqrt(WIDTH), 'out_w': jax.random.normal(ks[6], (NUM_HEADS, HEAD_DIM, WIDTH), jnp.float32) / np.sqrt(NUM_HEADS * HEAD_DIM)}
    _L2_xattn_all = _L2_xattn_setup()
    _L2_xattn_in = {k: v for k, v in _L2_xattn_all.items() if k in ('rms_scale', 'q_w', 'kv_w', 'out_w')}
    del _L2_xattn_all

    def _L2_ffn_setup():
        import jax, jax.numpy as jnp
        import numpy as np
        LN_EPS = 1e-12
        key = jax.random.key(seed)
        ks = jax.random.split(key, 8)
        B, S, H, I, E = (4, 256, 128, 512, 8)
        sH = 1.0 / np.sqrt(H)
        sI = 1.0 / np.sqrt(I)
        return {'hidden_states': jax.random.normal(ks[0], (B, S, H), dtype=jnp.float32), 'Wr': jax.random.uniform(ks[1], (E, H), jnp.float32, -sH, sH), 'W1': jax.random.uniform(ks[2], (E, H, I), jnp.float32, -sH, sH), 'b1': jax.random.uniform(ks[3], (E, I), jnp.float32, -sH, sH), 'Wo': jax.random.uniform(ks[4], (I, H), jnp.float32, -sI, sI), 'bo': jax.random.uniform(ks[5], (H,), jnp.float32, -sI, sI), 'gamma': jnp.ones((H,), jnp.float32), 'beta': jnp.zeros((H,), jnp.float32)}
    _L2_ffn_all = _L2_ffn_setup()
    _L2_ffn_in = {k: v for k, v in _L2_ffn_all.items() if k in ('Wr', 'W1', 'b1', 'Wo', 'bo', 'gamma', 'beta')}
    del _L2_ffn_all

    def _L3_xattn_setup():
        import jax, jax.numpy as jnp
        import numpy as np
        DIM = 128
        NUM_HEADS = 16
        HEAD_DIM = DIM // NUM_HEADS
        key = jax.random.key(seed)
        ks = jax.random.split(key, 11)
        B, N, C = (2, 256, DIM)
        s = 1.0 / np.sqrt(C)
        inp = {'q': jax.random.normal(ks[0], (B, N, C), jnp.float32), 'k': jax.random.normal(ks[1], (B, N, C), jnp.float32), 'v': jax.random.normal(ks[2], (B, N, C), jnp.float32), 'Wq': jax.random.normal(ks[3], (C, C), jnp.float32) * s, 'bq': jnp.zeros((C,), jnp.float32), 'Wk': jax.random.normal(ks[4], (C, C), jnp.float32) * s, 'bk': jnp.zeros((C,), jnp.float32), 'Wv': jax.random.normal(ks[5], (C, C), jnp.float32) * s, 'bv': jnp.zeros((C,), jnp.float32), 'Wo': jax.random.normal(ks[6], (C, C), jnp.float32) * s, 'bo': jnp.zeros((C,), jnp.float32)}
        return inp
    _L3_xattn_all = _L3_xattn_setup()
    _L3_xattn_in = {k: v for k, v in _L3_xattn_all.items() if k in ('Wq', 'bq', 'Wk', 'bk', 'Wv', 'bv', 'Wo', 'bo')}
    del _L3_xattn_all

    def _L3_ffn_setup():
        import jax, jax.numpy as jnp
        import numpy as np
        NUM_EXPERTS = 8
        TOP_K = 2
        HIDDEN = 128
        INTER_TOTAL = 1024
        B, S = (2, 256)
        key = jax.random.key(seed)
        k1, k2, k3, k4, k5, k6 = jax.random.split(key, 6)
        T = B * S
        x = jax.random.normal(k1, (B, S, HIDDEN), dtype=jnp.float32)
        scores = jax.random.uniform(k2, (T, NUM_EXPERTS), dtype=jnp.float32)
        expert_weights = jax.random.uniform(k3, (T, TOP_K), dtype=jnp.float32)
        top_experts = jax.random.randint(k4, (T, TOP_K), 0, NUM_EXPERTS, dtype=jnp.int32)
        w1 = jax.random.normal(k5, (HIDDEN, INTER_TOTAL), dtype=jnp.float32) * 0.02
        w2 = jax.random.normal(k6, (INTER_TOTAL, HIDDEN), dtype=jnp.float32) * 0.02
        return {'x': x, 'scores': scores, 'expert_weights': expert_weights, 'top_experts': top_experts, 'w1': w1, 'w2': w2}
    _L3_ffn_all = _L3_ffn_setup()
    _L3_ffn_in = {k: v for k, v in _L3_ffn_all.items() if k in ('scores', 'expert_weights', 'top_experts', 'w1', 'w2')}
    del _L3_ffn_all
    return {'x': x, 'ctx_1024': ctx_1024, 'mask_Bx1xSxS2_ik1': mask_Bx1xSxS2_ik1, 'mask_BxS2_bk0': mask_BxS2_bk0, 'g_xattn': g_xattn, 'g_ffn': g_ffn, 'L0_xattn_adj': _L0_xattn_in['adj'], 'L0_xattn_Wq': _L0_xattn_in['Wq'], 'L0_xattn_bq': _L0_xattn_in['bq'], 'L0_xattn_Wk': _L0_xattn_in['Wk'], 'L0_xattn_bk': _L0_xattn_in['bk'], 'L0_xattn_Wv': _L0_xattn_in['Wv'], 'L0_xattn_bv': _L0_xattn_in['bv'], 'L0_xattn_Wo': _L0_xattn_in['Wo'], 'L0_xattn_bo': _L0_xattn_in['bo'], 'L0_ffn_tile_sigs': _L0_ffn_in['tile_sigs'], 'L0_ffn_W': _L0_ffn_in['W'], 'L0_ffn_b': _L0_ffn_in['b'], 'L1_xattn_Wq': _L1_xattn_in['Wq'], 'L1_xattn_Wk': _L1_xattn_in['Wk'], 'L1_xattn_Wv': _L1_xattn_in['Wv'], 'L1_xattn_Wo': _L1_xattn_in['Wo'], 'L1_xattn_q_norm_w': _L1_xattn_in['q_norm_w'], 'L1_xattn_k_norm_w': _L1_xattn_in['k_norm_w'], 'L1_ffn_wi': _L1_ffn_in['wi'], 'L1_ffn_bi': _L1_ffn_in['bi'], 'L1_ffn_wo': _L1_ffn_in['wo'], 'L1_ffn_bo': _L1_ffn_in['bo'], 'L1_ffn_lora_A': _L1_ffn_in['lora_A'], 'L1_ffn_lora_B': _L1_ffn_in['lora_B'], 'L1_ffn_gate_w': _L1_ffn_in['gate_w'], 'L1_ffn_gate_b': _L1_ffn_in['gate_b'], 'L2_xattn_rms_scale': _L2_xattn_in['rms_scale'], 'L2_xattn_q_w': _L2_xattn_in['q_w'], 'L2_xattn_kv_w': _L2_xattn_in['kv_w'], 'L2_xattn_out_w': _L2_xattn_in['out_w'], 'L2_ffn_Wr': _L2_ffn_in['Wr'], 'L2_ffn_W1': _L2_ffn_in['W1'], 'L2_ffn_b1': _L2_ffn_in['b1'], 'L2_ffn_Wo': _L2_ffn_in['Wo'], 'L2_ffn_bo': _L2_ffn_in['bo'], 'L2_ffn_gamma': _L2_ffn_in['gamma'], 'L2_ffn_beta': _L2_ffn_in['beta'], 'L3_xattn_Wq': _L3_xattn_in['Wq'], 'L3_xattn_bq': _L3_xattn_in['bq'], 'L3_xattn_Wk': _L3_xattn_in['Wk'], 'L3_xattn_bk': _L3_xattn_in['bk'], 'L3_xattn_Wv': _L3_xattn_in['Wv'], 'L3_xattn_bv': _L3_xattn_in['bv'], 'L3_xattn_Wo': _L3_xattn_in['Wo'], 'L3_xattn_bo': _L3_xattn_in['bo'], 'L3_ffn_scores': _L3_ffn_in['scores'], 'L3_ffn_expert_weights': _L3_ffn_in['expert_weights'], 'L3_ffn_top_experts': _L3_ffn_in['top_experts'], 'L3_ffn_w1': _L3_ffn_in['w1'], 'L3_ffn_w2': _L3_ffn_in['w2']}

def reference(x, ctx_1024, mask_Bx1xSxS2_ik1, mask_BxS2_bk0, g_xattn, g_ffn, L0_xattn_adj, L0_xattn_Wq, L0_xattn_bq, L0_xattn_Wk, L0_xattn_bk, L0_xattn_Wv, L0_xattn_bv, L0_xattn_Wo, L0_xattn_bo, L0_ffn_tile_sigs, L0_ffn_W, L0_ffn_b, L1_xattn_Wq, L1_xattn_Wk, L1_xattn_Wv, L1_xattn_Wo, L1_xattn_q_norm_w, L1_xattn_k_norm_w, L1_ffn_wi, L1_ffn_bi, L1_ffn_wo, L1_ffn_bo, L1_ffn_lora_A, L1_ffn_lora_B, L1_ffn_gate_w, L1_ffn_gate_b, L2_xattn_rms_scale, L2_xattn_q_w, L2_xattn_kv_w, L2_xattn_out_w, L2_ffn_Wr, L2_ffn_W1, L2_ffn_b1, L2_ffn_Wo, L2_ffn_bo, L2_ffn_gamma, L2_ffn_beta, L3_xattn_Wq, L3_xattn_bq, L3_xattn_Wk, L3_xattn_bk, L3_xattn_Wv, L3_xattn_bv, L3_xattn_Wo, L3_xattn_bo, L3_ffn_scores, L3_ffn_expert_weights, L3_ffn_top_experts, L3_ffn_w1, L3_ffn_w2):
    import jax
    import jax.numpy as jnp

    def _L0_xattn_ref(query, key, value, adj, mask, Wq, bq, Wk, bk, Wv, bv, Wo, bo):
        import jax, jax.numpy as jnp
        import numpy as np
        B, S, E, H = (2, 256, 128, 16)
        D = E // H
        b, s, _ = query.shape

        def heads(x, W, bias):
            y = jnp.einsum('bse,ef->bsf', x, W.T) + bias
            return y.reshape(b, s, H, D).transpose(0, 2, 1, 3)
        Q = heads(query, Wq, bq)
        K = heads(key, Wk, bk)
        V = heads(value, Wv, bv)
        scores = jnp.einsum('bhqd,bhkd->bhqk', Q, K) / jnp.sqrt(jnp.float32(D))
        scores = scores + adj[None, None, :, :]
        scores = jnp.where(mask == 0, jnp.float32(-jnp.inf), scores)
        weights = jax.nn.softmax(scores, axis=-1)
        out = jnp.einsum('bhqk,bhkd->bhqd', weights, V)
        out = out.transpose(0, 2, 1, 3).reshape(b, s, E)
        return jnp.einsum('bse,ef->bsf', out, Wo.T) + bo

    def _L0_ffn_ref(x, tile_sigs, W, b):
        import jax, jax.numpy as jnp
        import numpy as np
        B, S, D, T = (4, 512, 128, 8)
        scores = jnp.einsum('bsd,td->bst', x, jnp.sign(tile_sigs))
        idx = jnp.argmax(scores, axis=-1)
        all_out = jnp.einsum('bsd,tde->bste', x, W) + b[None, None]
        out = jnp.take_along_axis(all_out, idx[:, :, None, None], axis=2)
        return out[:, :, 0, :]

    def _L1_xattn_ref(q, k, v, Wq, Wk, Wv, Wo, q_norm_w, k_norm_w):
        import jax, jax.numpy as jnp
        import numpy as np
        B, S, D, H = (2, 256, 128, 16)
        DK = D // H
        EPS = 1e-10
        ROPE_BASE = 500000.0

        def _rms_norm(x, w):
            return w * x * jax.lax.rsqrt(jnp.mean(x * x, axis=-1, keepdims=True) + EPS)

        def _rope_tables(seq_len, dk):
            inv_freq = 1.0 / ROPE_BASE ** (jnp.arange(0, dk, 2, dtype=jnp.float32) / dk)
            t = jnp.arange(seq_len, dtype=jnp.float32)
            freqs = jnp.outer(t, inv_freq)
            emb = jnp.concatenate([freqs, freqs], -1)
            return (jnp.cos(emb), jnp.sin(emb))

        def _rotate_half(x):
            x1, x2 = jnp.split(x, 2, axis=-1)
            return jnp.concatenate([-x2, x1], axis=-1)
        Bq, Sq, _ = q.shape

        def proj(x, W):
            return (x @ W.T).reshape(Bq, Sq, H, DK).transpose(0, 2, 1, 3)
        query, key_, value = (proj(q, Wq), proj(k, Wk), proj(v, Wv))
        query = _rms_norm(query, q_norm_w)
        key_ = _rms_norm(key_, k_norm_w)
        cos, sin = _rope_tables(Sq, DK)
        query = query * cos + _rotate_half(query) * sin
        key_ = key_ * cos + _rotate_half(key_) * sin
        scale = 1.0 / np.sqrt(DK)
        scores = jnp.einsum('bhqd,bhkd->bhqk', query, key_) * scale
        causal = jnp.tril(jnp.ones((Sq, Sq), bool))
        scores = jnp.where(causal, scores, -jnp.inf)
        probs = jax.nn.softmax(scores, axis=-1)
        attn = jnp.einsum('bhqk,bhkd->bhqd', probs, value)
        attn = attn.transpose(0, 2, 1, 3).reshape(Bq, Sq, D)
        return attn @ Wo.T

    def _L1_ffn_ref(hidden_states, wi, bi, wo, bo, lora_A, lora_B, gate_w, gate_b):
        import jax, jax.numpy as jnp
        import numpy as np
        B, S, D_MODEL, D_FF, E, R, TOP_K = (4, 256, 128, 512, 8, 16, 2)
        logits = jnp.einsum('bsd,ed->bse', hidden_states, gate_w) + gate_b
        scores = jax.nn.softmax(logits, axis=-1)
        top_v, top_i = jax.lax.top_k(scores, TOP_K)
        val_sum = top_v.sum(axis=-1)
        out = jnp.zeros_like(hidden_states)
        for e in range(E):
            count = (top_i == e).sum(axis=-1).astype(hidden_states.dtype)
            gate = count * val_sum
            inter = jnp.einsum('bsd,fd->bsf', hidden_states, wi) + bi + jnp.einsum('bsr,fr->bsf', jnp.einsum('bsd,rd->bsr', hidden_states, lora_A[e]), lora_B[e])
            h = jax.nn.relu(inter)
            expert_out = jnp.einsum('bsf,df->bsd', h, wo) + bo
            out = out + gate[..., None] * expert_out
        return out

    def _L2_xattn_ref(x, mem_seq, mem_mask, rms_scale, q_w, kv_w, out_w):
        import jax, jax.numpy as jnp
        import numpy as np
        NUM_HEADS, NUM_KV, HEAD_DIM, WIDTH = (4, 1, 32, 128)
        MASK_FILL = -2.3819763e+38

        def _apply_rope(x, positions, max_wavelength=10000.0):
            d = x.shape[-1]
            freq_exp = 2.0 / d * jnp.arange(d // 2, dtype=jnp.float32)
            timescale = max_wavelength ** freq_exp
            radians = positions[..., None].astype(jnp.float32) / timescale
            radians = radians[..., None, :]
            sin, cos = (jnp.sin(radians), jnp.cos(radians))
            x1, x2 = jnp.split(x, 2, axis=-1)
            out = jnp.concatenate([x1 * cos - x2 * sin, x2 * cos + x1 * sin], axis=-1)
            return out.astype(x.dtype)

        def _rmsnorm(x, scale):
            var = jnp.mean(jnp.square(x.astype(jnp.float32)), axis=-1, keepdims=True)
            normed = x * jax.lax.rsqrt(var + 1e-06)
            return (normed * (1 + scale)).astype(x.dtype)
        B, S, _ = mem_seq.shape
        T = x.shape[1]
        G = NUM_HEADS // NUM_KV
        xn = _rmsnorm(x, rms_scale)
        mn = _rmsnorm(mem_seq, rms_scale)
        q = jnp.einsum('BTD,NDH->BTNH', xn, q_w)
        kv = jnp.einsum('BSD,cKDH->cBSKH', mn, kv_w)
        k, v = (kv[0], kv[1])
        q_pos = jnp.broadcast_to(jnp.arange(S, T + S), (B, T))
        k_pos = jnp.broadcast_to(jnp.arange(S), (B, S))
        q = _apply_rope(q, q_pos) * HEAD_DIM ** (-0.5)
        k = _apply_rope(k, k_pos)
        q = q.reshape(B, T, NUM_KV, G, HEAD_DIM)
        logits = jnp.einsum('BTKGH,BSKH->BKGTS', q, k, preferred_element_type=jnp.float32)
        masked = jnp.where(mem_mask[:, None, None, None, :], logits, MASK_FILL)
        probs = jax.nn.softmax(masked, axis=-1).astype(x.dtype)
        enc = jnp.einsum('BKGTS,BSKH->BTKGH', probs, v).reshape(B, T, NUM_HEADS, HEAD_DIM)
        return jnp.einsum('BTNH,NHD->BTD', enc, out_w)

    def _L2_ffn_ref(hidden_states, Wr, W1, b1, Wo, bo, gamma, beta):
        import jax, jax.numpy as jnp
        import numpy as np
        LN_EPS = 1e-12
        B, S, H = hidden_states.shape
        E = Wr.shape[0]
        x = hidden_states.reshape(-1, H)
        router_logits = x @ Wr.T
        expert_idx = jnp.argmax(jax.nn.softmax(router_logits, axis=-1), axis=-1)
        inter = jnp.zeros((x.shape[0], W1.shape[2]), dtype=x.dtype)
        for e in range(E):
            mask = (expert_idx == e)[:, None].astype(x.dtype)
            inter = inter + mask * jax.nn.gelu(x @ W1[e] + b1[e], approximate=False)
        y = inter @ Wo + bo + x
        mu = jnp.mean(y, axis=-1, keepdims=True)
        var = jnp.mean(jnp.square(y - mu), axis=-1, keepdims=True)
        out = (y - mu) * jax.lax.rsqrt(var + LN_EPS) * gamma + beta
        return out.reshape(B, S, H)

    def _L3_xattn_ref(q, k, v, Wq, bq, Wk, bk, Wv, bv, Wo, bo):
        import jax, jax.numpy as jnp
        import numpy as np
        DIM = 128
        NUM_HEADS = 16
        HEAD_DIM = DIM // NUM_HEADS
        B, Nq, C = q.shape
        Nkv = k.shape[1]
        H, D = (NUM_HEADS, HEAD_DIM)
        qh = (q @ Wq.T + bq).reshape(B, Nq, H, D).transpose(0, 2, 1, 3)
        kh = (k @ Wk.T + bk).reshape(B, Nkv, H, D).transpose(0, 2, 1, 3)
        vh = (v @ Wv.T + bv).reshape(B, Nkv, H, D).transpose(0, 2, 1, 3)
        scale = D ** (-0.5)
        attn = jax.nn.softmax(jnp.einsum('bhqd,bhkd->bhqk', qh, kh) * scale, axis=-1)
        out = jnp.einsum('bhqk,bhkd->bhqd', attn, vh)
        out = out.transpose(0, 2, 1, 3).reshape(B, Nq, C)
        return out @ Wo.T + bo

    def _L3_ffn_ref(x, scores, expert_weights, top_experts, w1, w2):
        import jax, jax.numpy as jnp
        import numpy as np
        NUM_EXPERTS = 8
        TOP_K = 2
        HIDDEN = 128
        INTER_TOTAL = 1024
        B, S = (2, 256)
        in_shape = x.shape
        T = in_shape[0] * in_shape[1]
        H = in_shape[-1]
        x_flat = x.reshape(T, H)
        flat_experts = top_experts.reshape(-1)
        flat_weights = expert_weights.reshape(-1)
        order = jnp.argsort(flat_experts, stable=True)
        token_idx = order // TOP_K
        xg = x_flat[token_idx]
        h = jax.nn.gelu(xg @ w1, approximate=True)
        y = h @ w2
        w_sorted = flat_weights[order]
        out = jnp.zeros((T, H), dtype=x.dtype).at[token_idx].add(w_sorted[:, None] * y)
        return out.reshape(in_shape)
    x = x + jnp.tanh(g_xattn[0]) * _L0_xattn_ref(_layernorm(x, axis=-1), ctx_1024, ctx_1024, L0_xattn_adj, mask_Bx1xSxS2_ik1, L0_xattn_Wq, L0_xattn_bq, L0_xattn_Wk, L0_xattn_bk, L0_xattn_Wv, L0_xattn_bv, L0_xattn_Wo, L0_xattn_bo)
    x = x + jnp.tanh(g_ffn[0]) * _L0_ffn_ref(_layernorm(x, axis=-1), L0_ffn_tile_sigs, L0_ffn_W, L0_ffn_b)
    x = x + jnp.tanh(g_xattn[1]) * _L1_xattn_ref(_layernorm(x, axis=-1), ctx_1024, ctx_1024, L1_xattn_Wq, L1_xattn_Wk, L1_xattn_Wv, L1_xattn_Wo, L1_xattn_q_norm_w, L1_xattn_k_norm_w)
    x = x + jnp.tanh(g_ffn[1]) * _L1_ffn_ref(_layernorm(x, axis=-1), L1_ffn_wi, L1_ffn_bi, L1_ffn_wo, L1_ffn_bo, L1_ffn_lora_A, L1_ffn_lora_B, L1_ffn_gate_w, L1_ffn_gate_b)
    x = x + jnp.tanh(g_xattn[2]) * _L2_xattn_ref(_layernorm(x, axis=-1), ctx_1024, mask_BxS2_bk0, L2_xattn_rms_scale, L2_xattn_q_w, L2_xattn_kv_w, L2_xattn_out_w)
    x = x + jnp.tanh(g_ffn[2]) * _L2_ffn_ref(_layernorm(x, axis=-1), L2_ffn_Wr, L2_ffn_W1, L2_ffn_b1, L2_ffn_Wo, L2_ffn_bo, L2_ffn_gamma, L2_ffn_beta)
    x = x + jnp.tanh(g_xattn[3]) * _L3_xattn_ref(_layernorm(x, axis=-1), ctx_1024, ctx_1024, L3_xattn_Wq, L3_xattn_bq, L3_xattn_Wk, L3_xattn_bk, L3_xattn_Wv, L3_xattn_bv, L3_xattn_Wo, L3_xattn_bo)
    x = x + jnp.tanh(g_ffn[3]) * _L3_ffn_ref(_layernorm(x, axis=-1), L3_ffn_scores, L3_ffn_expert_weights, L3_ffn_top_experts, L3_ffn_w1, L3_ffn_w2)
    return x

_drawn_inputs = setup_inputs


def setup_inputs(seed=0):
    import zlib

    import numpy as np

    out = dict(_drawn_inputs(seed))
    spreads = {'L1_xattn_k_norm_w': (1.0, 0.2),
     'L2_ffn_gamma': (1.0, 0.2),
     'L2_ffn_beta': (0.0, 0.1),
     'L3_xattn_bq': (0.0, 0.483),
     'L3_xattn_bk': (0.0, 2.0),
     'L3_xattn_bv': (0.0, 0.1),
     'L3_xattn_bo': (0.0, 0.1)}
    factors = {'L0_xattn_bk': 64.0,
     'L1_xattn_q_norm_w': 6.166,
     'L1_ffn_bi': 5.015,
     'L1_ffn_bo': 4.882,
     'L1_ffn_gate_b': 7.308,
     'L2_xattn_rms_scale': 4.318,
     'L2_ffn_b1': 4.037,
     'L3_ffn_expert_weights': 4.277,
     'L2_ffn_bo': 2.897}
    for name, (base, spread) in spreads.items():
        noise = np.random.default_rng([zlib.crc32(name.encode()), seed]).standard_normal(out[name].shape)
        drawn = base * np.exp(spread * noise) if base else spread * noise
        out[name] = jnp.asarray(drawn.astype(out[name].dtype))
    for name, factor in factors.items():
        out[name] = (out[name] * factor).astype(out[name].dtype)
    return out
```

```python
from contextlib import ExitStack

import concourse.bass as bass
from concourse import mybir

F32 = mybir.dt.float32
BF16 = mybir.dt.bfloat16
I32 = mybir.dt.int32
U32 = mybir.dt.uint32
U8 = mybir.dt.uint8
ALU = mybir.AluOpType
ACT = mybir.ActivationFunctionType
AX = mybir.AxisListType

P = 128
BATCH = 8
SEQ = 256
NT = SEQ // P
ROWS = 2
TURNS = BATCH // ROWS
HEADS = 16
HD = P // HEADS
MQ, MD = 4, 32
E = 8
RANK = 16
FF = 512
FT = FF // P
FF3 = 1024
FT3 = FF3 // P
STK = 64
TERMS = 6
KD = TERMS * HD
NEG = -1.0e30
FILL = -2.3819763e+38
SUBLAYERS = 8


def columns(parts):
    at, out = 0, {}
    for name, n in parts:
        out[name] = (at, n)
        at += n
    return out, at


PACKS = {
    "c0": [("ident", P), ("tri", P), ("triT", P), ("iota", E), ("g", 8),
           ("wq0", P), ("wk0", P), ("wv0", P), ("wo0", P), ("bq0", P), ("bk0", P), ("bv0", P), ("bo0", P),
           ("adj", NT * SEQ)],
    "c1": [("sig", E), ("wf0", E * P),
           ("wq1", P), ("wk1", P), ("wv1", P), ("wo1", P), ("qnw", HD), ("knw", HD),
           ("cos1", NT * HD), ("sin1", NT * HD)],
    "c2": [("wi", FF), ("bi", FT), ("wo_f1", FF), ("bo_f1", P), ("loraA", P), ("loraB", FF), ("gate", E),
           ("gateb", E),
           ("rms", 1), ("qw2", P), ("kvw2", 2 * MD), ("ow2", P),
           ("cq2", NT * MD), ("sq2", NT * MD), ("ck2", NT * MD), ("sk2", NT * MD)],
    "c3": [("wr", E), ("w1_f2", E * FF), ("wo_f2", FF), ("bo_f2", P), ("gamma", P), ("beta", P)],
    "c4": [("wq3", P), ("wk3", P), ("wv3", P), ("wo3", P), ("bq3", P), ("bk3", P), ("bv3", P), ("bo3", P),
           ("w1_f3", FF3), ("w2_f3", FF3), ("ew", 2 * NT * ROWS)],
}
SMALL = [("sel", E * P), ("pick1", P), ("pick2", P), ("bf0", P), ("b1_f2", FF)]
WHERE = {}
WIDTH = {}
for _pack, _parts in PACKS.items():
    _cols, WIDTH[_pack] = columns(_parts)
    WHERE.update({_n: (_pack, *_c) for _n, _c in _cols.items()})
SMALL_COLS, SMALL_W = columns(SMALL)



def row_steps(b):
    out = [("load", 0, b)]
    for l in range(4):
        parts_a, parts_b = (8, 8) if l != 2 else (2, 2)
        if 2 * l < SUBLAYERS:
            out += [("kv", l, b), ("stats", l, b), ("norm", l, b), ("query", l, b)]
            out += [("max", l, b, p) for p in range(parts_a)]
            out += [("shift", l, b)]
            out += [("attend", l, b, p) for p in range(parts_b)]
            out += [("mix", l, b)]
        if 2 * l + 1 < SUBLAYERS and l < 3:
            out += [("stats", 4 + l, b), ("norm", 4 + l, b), ("route", l, b), ("experts", l, b)]
    return out + [("store", 0, b)]


WEIGHT = {"load": 1, "kv": 4, "stats": 2, "norm": 2, "query": 5, "max": 1.3, "shift": 4, "attend": 1.8, "mix": 4,
          "route": 6, "experts": 9, "store": 1}
LAG = 25


def turn_order():
    rows, at, time, out, holder = [row_steps(b) for b in range(ROWS)], [0] * ROWS, [0, LAG], [], None
    while any(at[b] < len(rows[b]) for b in range(ROWS)):
        free = [b for b in range(ROWS) if at[b] < len(rows[b])
                and not (rows[b][at[b]][0] == "attend" and holder not in (None, b))]
        b = min(free, key=lambda b: time[b])
        s = rows[b][at[b]]
        if s[0] == "attend":
            holder = b
        if s[0] == "mix":
            holder = None
        out.append(s)
        at[b] += 1
        time[b] = max(time[b], min(time)) + WEIGHT[s[0]]
    return out


def psum_uses(s):
    kind, l, b = s[:3]
    if kind == "load":
        return [("ctxT_ps", "one", "ctxT"), ("biasT_ps", "one", "biasT")]
    if kind == "kv":
        uses = [("kv_ps", "one", "k_in")]
        if l == 2:
            return uses + [("kT2_ps", "one", "kT0")]
        return uses + [("kT0_ps", "one", "kT0"), ("kT1_ps", "one", "kT1")]
    if kind == "norm":
        return [("xT_ps", "one", "xT")]
    if kind == "query":
        uses = [("q_ps", "one", "q_in")]
        if l == 2:
            return uses + [("qT2_ps", "two", "qT1")]
        return uses + [("qT0_ps", "one", "qT0"), ("qT1_ps", "one", "qT1")]
    if kind == "max":
        return [("max0_ps", "one", "max0"), ("max1_ps", "one", "max1")]
    if kind == "shift":
        return [("shift_ps", "one", "shiftT")]
    if kind == "attend":
        return [("scores_ps", "two", "biased" if l == 0 else "probs")]
    if kind == "mix":
        return [("oT_ps", "one", "oT"), ("y_ps", "one", "x_new")]
    if kind == "route":
        uses = [("logits_ps", "one", "logits"), ("onehotT_ps", "one", "onehotT")]
        if l == 1:
            return uses + [("u_ps", "one", "u"), ("pick_ps", "one", "picked")]
        return uses + [("spread0_ps", "two", "spread0"), ("spread1_ps", "two", "spread1")]
    if kind == "experts":
        if l == 0:
            return [("f_ps", "one", "x_new")]
        if l == 1:
            return [("h0_ps", "two", "h0"), ("h1_ps", "two", "h1"), ("f_ps", "one", "f_in")]
        return [("h0_ps", "two", "h0"), ("f_ps", "one", "f_in")]
    if kind == "tail":
        return [("h0_ps", "two", "h0"), ("h1_ps", "two", "h1"), ("f_ps", "one", "x_new")]
    return []


def stages(s):
    kind, l, b = s[:3]
    out = [u[0] for u in psum_uses(s)]
    out += {
        "load": ["bias", "bias_hi", "ctxT", "biasT", "ctx_var", "ctx_rms", "mask_row"],
        "kv": ["k_in", "v"] + (["kT0", "k_var", "k_rms", "k_rot"] if l == 2 else ["kT0", "kT1", "k_stack", "k_in"][:3]),
        "stats": ["var", "rstd"] + (["rms"] if l == 2 else []) + ["x_bias"],
        "norm": ["x_normed", "xT"],
        "query": ["q_in", "q_stack", "qT0", "qT1"] + (["q_hi", "q_rest", "q_mid"] if l != 2 else [])
                 + (["q_var", "q_rms", "q_ready"] if l == 1 else []),
        "max": ["max0", "max1"],
        "shift": ["shift", "shiftT"],
        "attend": (["biased"] if l == 0 else []) + ["probs", "weighed"],
        "mix": ["o", "oT", "x_new"],
        "route": ["logits", "onehot", "onehotT"] + (["gate_in", "gate_exp", "u", "picked"] if l == 1
                                                     else ["onehotF", "spread0", "spread1"]),
        "experts": ["x_new"] + ([] if l == 0 else ["h0", "f_in"] if l == 2 else ["h0", "h1", "f_in"])
                   + (["y_var", "y_rstd", "y_res"] if l == 2 else []),
        "tail": ["h0", "h1", "x_new"],
        "store": [],
    }[kind]
    return out


class Plan:

    def __init__(self, order, slots):
        self.value, self.slot, self.before, self.nth = {}, {}, {}, {}
        count, at, last, steps = {}, {ring: 0 for ring in slots}, {}, {}
        for s in order:
            for stage in stages(s):
                count[stage] = count.get(stage, 0) + 1
                self.value[stage, s] = count[stage]
            for use, ring, reader in psum_uses(s):
                slot = (ring, at[ring] % slots[ring])
                at[ring] += 1
                self.slot[use, s] = slot
                self.before[use, s] = last.get(slot)
                last[slot] = (reader, s)
            steps[s[0]] = steps.get(s[0], 0) + 1
            self.nth[s] = steps[s[0]] - 1
        self.names = sorted(count)


def build(nc, dram, out):
    turn = turn_order()
    rings = {"one": 3, "two": 2}
    plan = Plan(turn, rings)
    tail = [("stats", 7, b) for b in range(ROWS)] + [("norm", 7, b) for b in range(ROWS)] + \
           [("tail", 3, b) for b in range(ROWS)]
    tail_plan = Plan(tail, rings)

    with ExitStack() as ctx:
        def sb(name, shape, dt=F32):
            return ctx.enter_context(nc.sbuf_tensor(name, shape, dt))

        def pair(name, shape, dt=F32):
            return [sb(f"{name}_row{b}", shape, dt) for b in range(ROWS)]

        pack = {n: sb(n, [P, w]) for n, w in WIDTH.items()}
        small = sb("small", [16, SMALL_W])

        def W(name):
            n, a, w = WHERE[name]
            return pack[n][:, a:a + w]

        def S16(name, rows):
            a, w = SMALL_COLS[name]
            return small[0:rows, a:a + w]

        identb = sb("identb", [P, P], BF16)
        trib = sb("trib", [P, P], BF16)
        triTb = sb("triTb", [P, P], BF16)
        selb = sb("selb", [E, E * P], BF16)
        pickb = sb("pickb", [16, 2 * P], BF16)
        wq0s = sb("wq0s", [P, P])
        bq0s = sb("bq0s", [P, P])
        sgn = sb("sgn", [P, E])
        wc = {"q": sb("wcq", [P, NT, HD]), "k": sb("wck", [P, NT, HD])}
        ws = {"q": sb("wsq", [P, NT, HD]), "k": sb("wsk", [P, NT, HD])}
        qw2 = sb("qw2s", [P, P])
        kvw2 = sb("kvw2s", [P, 2 * MD])
        rms1 = sb("rms1", [P, 1])
        tg = sb("tg", [P, 8])
        tbo = {0: sb("tbo0", [P, P]), 3: sb("tbo3", [P, P])}
        tgam = sb("tgam", [P, P])
        tbeta = sb("tbeta", [P, P])
        bo2x = sb("bo2x", [P, P])
        wsum = sb("wsum", [P, ROWS * NT])
        neghalf = sb("neghalf", [P, NT * HEADS])

        x = pair("x", [P, NT, P])
        cx = pair("cx", [P, NT, P])
        mrow8 = pair("mrow8", [MD + 1, SEQ], U8)
        bias = pair("bias", [P, NT, SEQ])
        bias_hi = pair("bias_hi", [P, NT, SEQ], BF16)
        biasT = pair("biasT", [P, NT, SEQ])
        ctxT = pair("ctxT", [P, SEQ])
        cst = pair("cst", [P, NT, 6])
        cmv = pair("cmv", [P, NT, 2])
        crms = pair("crms", [P, NT])
        st = pair("st", [P, NT, 6])
        mv = pair("mv", [P, NT, 2])
        rstd = pair("rstd", [P, NT])
        rms = pair("rms", [P, NT])
        xn = pair("xn", [P, NT, P])
        xT = pair("xT", [P, SEQ])
        xb = pair("xb", [P, NT, P])
        qf = pair("qf", [P, NT, P])
        qr = pair("qr", [P, NT, P])
        qt2 = pair("qt2", [P, NT, P])
        qss = pair("qss", [P, NT * HEADS])
        kf = pair("kf", [P, NT, P])
        kr = pair("kr", [P, NT, P])
        kt2 = pair("kt2", [P, NT, P])
        kss = pair("kss", [P, NT * HEADS])
        qs = pair("qs", [P, NT * HEADS, 8, HD], BF16)
        ks = pair("ks", [P, NT * HEADS, 8, HD], BF16)
        qT = pair("qT", [P, 8, SEQ], BF16)
        kT = pair("kT", [P, 8, SEQ], BF16)
        v = pair("v", [P, NT, HEADS, HD + 1])
        nm = pair("nm", [P, NT, 2, 8])
        mp = pair("mp", [P, NT, 2, 2, 8], BF16)
        mT = pair("mT", [32, SEQ], BF16)
        k2 = pair("k2", [P, NT, MD])
        q2 = pair("q2", [P, NT, MQ, MD])
        q2T = pair("q2T", [MD + 2, MQ, SEQ])
        k2T = pair("k2T", [MD + 2, SEQ])
        v2 = pair("v2", [P, NT, MD + 1])
        nm2 = pair("nm2", [P, NT, MQ])
        mT2 = pair("mT2", [8, P])
        probs = [sb(f"probs{i}", [P, 2, 512]) for i in range(4)]
        rec = pair("rec", [P, NT * HEADS])
        o = pair("o", [P, NT, P])
        oT = pair("oT", [P, SEQ])
        lg = pair("lg", [P, NT, E])
        ge = pair("ge", [P, NT, E])
        gm = pair("gm", [P, NT])
        gs = pair("gs", [P, NT])
        gv = pair("gv", [P, NT])
        mx = pair("mx", [P, NT, 8])
        ix = pair("ix", [P, NT, 8], U32)
        ixf = pair("ixf", [P, NT, 8])
        oh = pair("oh", [P, NT, 2, E], BF16)
        ohT = pair("ohT", [16, SEQ], BF16)
        ohF = pair("ohF", [16, SEQ])
        uT = pair("uT", [P, SEQ])
        um = pair("um", [P, 2, SEQ])
        xm = pair("xm", [P, E, SEQ])
        h = [t[:, :, :].rearrange("p (i f) q -> p i f q", i=2) for t in xm]
        msk = [t[:, 0:NT, :].bitcast(I32) for t in xm]
        y = pair("y", [P, NT, P])
        yr = pair("yr", [P, NT, P])

        banks = {("one", i): ctx.enter_context(nc.psum_tensor(f"one{i}", [P, 512], F32)) for i in range(rings["one"])}
        banks |= {("two", i): ctx.enter_context(nc.psum_tensor(f"two{i}", [P, 1024], F32)) for i in range(rings["two"])}
        pv = ctx.enter_context(nc.psum_tensor("pv", [P, 512], F32))

        const_in = ctx.enter_context(nc.semaphore("const_in"))
        setup_act = ctx.enter_context(nc.semaphore("setup_act"))
        setup_pool = ctx.enter_context(nc.semaphore("setup_pool"))
        setup_dve = ctx.enter_context(nc.semaphore("setup_dve"))
        sem = {}
        for name in plan.names:
            sem[name] = ctx.enter_context(nc.semaphore(name))
        for b in range(ROWS):
            for name in ("x_in", "ctx_in", "mask_in", "row_in", "shift_in"):
                sem[name, b] = ctx.enter_context(nc.semaphore(f"{name}{b}"))
        sem["stored"] = ctx.enter_context(nc.semaphore("stored"))
        sem["dve"] = ctx.enter_context(nc.semaphore("dve_done"))
        sem["act"] = ctx.enter_context(nc.semaphore("act_done"))
        sem["pool"] = ctx.enter_context(nc.semaphore("pool_done"))
        nums = [s.num for s in sem.values()]
        all_sems = range(min(nums), max(nums) + 1)

        class Chain:

            def __init__(self, eng, s):
                self.eng, self.s, self.n = eng, s, 0

            def mark(self, ins):
                ins.then_inc(self.s, 1)
                self.n += 1

            def link(self, ins):
                self.mark(ins)
                self.eng.wait_ge(self.s, self.n)

        def shifted(b):
            n, got = 0, {}
            for s in turn:
                if s[0] == "shift" and s[2] == b:
                    n += 16 * (2 if s[1] == 2 else 4)
                    got[s[1]] = n
            return got

        shift_at = [shifted(b) for b in range(ROWS)]

        def x_ready_from(s, p):
            prev = None
            for t in p:
                if t == s:
                    break
                if t[2] == s[2] and t[0] in ("mix", "experts", "tail"):
                    prev = t
            return prev

        with nc.Block() as block:
            @block.sync
            def _(sp):
                for n in WIDTH:
                    sp.dma_start(pack[n][:, :], dram[n]).then_inc(const_in, 16)
                sp.dma_start(small[:, :], dram["small"]).then_inc(const_in, 16)

            n_consts = 16 * (len(WIDTH) + 1)

            @block.scalar
            def _(act):
                act.wait_ge(const_in, n_consts)
                act.activation(tg[:, :], W("g"), ACT.Tanh).then_inc(setup_act, 1)
                act.activation(sgn[:, :], W("sig"), ACT.Sign).then_inc(setup_act, 1)
                act.activation(wq0s[:, :], W("wq0"), ACT.Copy, scale=HD ** -0.5)
                act.activation(bq0s[:, :], W("bq0"), ACT.Copy, scale=HD ** -0.5)
                act.activation(bo2x[:, :], W("bo_f1"), ACT.Copy, scale=2.0)
                act.activation(selb[:, :], S16("sel", E), ACT.Copy)
                act.activation(pickb[:, 0:P], S16("pick1", 16), ACT.Copy)
                act.activation(pickb[:, P:2 * P], S16("pick2", 16), ACT.Copy)
                act.activation(rms1[:, :], W("rms"), ACT.Copy, bias=1.0).then_inc(setup_act, 1)

            @block.gpsimd
            def _(pool):
                pool.memset(neghalf[:, :], -0.5)
                for b in range(ROWS):
                    pool.memset(v[b][:, :, :, HD:HD + 1], 1.0)
                    pool.memset(v2[b][:, :, MD:MD + 1], 1.0)
                    pool.memset(qs[b][:, :, TERMS:8, :], 0.0)
                    pool.memset(ks[b][:, :, TERMS:8, :], 0.0).then_inc(setup_pool, 1)
                    pool.wait_ge(setup_pool, b + 1)
                    pool.memset(ks[b][:, :, TERMS, 0:2], 1.0)

            @block.vector
            def _(dve):
                for b in range(ROWS):
                    nc.vector.memset(q2T[b][MD:MD + 2, :, :], 1.0)
                    nc.vector.memset(k2T[b][MD:MD + 2, :], 1.0)
                dve.wait_ge(const_in, n_consts)
                nc.vector.tensor_copy(identb[:, :], W("ident"))
                nc.vector.tensor_copy(trib[:, :], W("tri"))
                nc.vector.tensor_copy(triTb[:, :], W("triT"))
                for n in "qk":
                    c = W("cos1").rearrange("p (t d) -> p t d", t=NT)
                    sn = W("sin1").rearrange("p (t d) -> p t d", t=NT)
                    w = W(f"{n}nw")
                    H2 = HD // 2
                    nc.vector.tensor_tensor(wc[n][:, :, :], c, w[:, None, :].to_broadcast([P, NT, HD]), ALU.mult)
                    nc.vector.scalar_tensor_tensor(out=ws[n][:, :, 0:H2], in0=sn[:, :, 0:H2], scalar=-1.0,
                                                   in1=w[:, None, H2:HD].to_broadcast([P, NT, H2]),
                                                   op0=ALU.mult, op1=ALU.mult)
                    nc.vector.tensor_tensor(ws[n][:, :, H2:HD], sn[:, :, H2:HD],
                                            w[:, None, 0:H2].to_broadcast([P, NT, H2]), ALU.mult)
                ew = W("ew").rearrange("p (n k) -> p n k", k=2)
                nc.vector.tensor_tensor(wsum[:, :], ew[:, :, 0], ew[:, :, 1], ALU.add).then_inc(setup_dve, 1)
                dve.wait_ge(setup_act, 3)
                dve.wait_ge(setup_dve, 1)
                nc.vector.tensor_scalar(wsum[:, :], wsum[:, :], tg[:, 7:8], None, ALU.mult)
                nc.vector.tensor_scalar(tbo[0][:, :], W("bo0"), tg[:, 0:1], None, ALU.mult)
                nc.vector.tensor_scalar(tbo[3][:, :], W("bo3"), tg[:, 3:4], None, ALU.mult)
                nc.vector.tensor_scalar(tgam[:, :], W("gamma"), tg[:, 6:7], None, ALU.mult)
                nc.vector.tensor_scalar(tbeta[:, :], W("beta"), tg[:, 6:7], None, ALU.mult)
                nc.vector.tensor_scalar(qw2[:, :], W("qw2"), rms1[:, 0:1], None, ALU.mult)
                nc.vector.tensor_scalar(kvw2[:, :], W("kvw2"), rms1[:, 0:1], None, ALU.mult)

        def programs(block, order, plan, first_row, in_loop):
            def at(stage, s):
                return plan.value[stage, s]

            def bank(use, s):
                return banks[plan.slot[use, s]]

            def claim(pe, use, s):
                before = plan.before[use, s]
                if before:
                    pe.wait_ge(sem[before[0]], plan.value[before])

            def prev_on(kind, s, back):
                same = [t for t in order if t[0] == kind]
                i = same.index(s) - back
                return same[i] if i >= 0 else None

            def rope(eng, ch, n, b, f, r, t2, ss, wait_power):
                N = NT * HEADS
                H2 = HD // 2
                g = f[:, :, :].rearrange("p t (h d) -> p (t h) d", d=HD)
                rg = r[:, :, :].rearrange("p t (h d) -> p (t h) d", d=HD)
                f4 = f[:, :, :].rearrange("p t (h d) -> p t h d", d=HD)
                r4 = r[:, :, :].rearrange("p t (h d) -> p t h d", d=HD)
                t4 = t2[:, :, :].rearrange("p t (h d) -> p t h d", d=HD)
                ch.link(eng.tensor_tensor(rg, g, g, ALU.mult))
                if n == "q":
                    ch.link(eng.tensor_reduce(ss[:, :], rg, AX.X, ALU.add))
                else:
                    t3 = t2[:, :, :].rearrange("p t (h d) -> p (t h) d", d=HD)
                    ch.link(eng.tensor_tensor(t3[:, :, 0:4], rg[:, :, 0:4], rg[:, :, 4:8], ALU.add))
                    ch.link(eng.tensor_tensor(t3[:, :, 4:6], t3[:, :, 0:2], t3[:, :, 2:4], ALU.add))
                    ch.link(eng.tensor_tensor(ss[:, :], t3[:, :, 4], t3[:, :, 5], ALU.add))
                var = eng.tensor_scalar(ss[:, :], ss[:, :], 1.0 / HD, 1e-10, ALU.mult, ALU.add)
                if n == "q":
                    var.then_inc(sem["q_var"], 1)
                else:
                    ch.link(var)
                    ch.mark(eng.tensor_tensor(ss[:, :], ss[:, :], neghalf[:, 0:N], ALU.pow))
                ch.mark(eng.tensor_tensor(r4, f4, wc[n][:, :, None, :].to_broadcast([P, NT, HEADS, HD]), ALU.mult))
                ch.mark(eng.tensor_tensor(t4[:, :, :, 0:H2], f4[:, :, :, H2:HD], ws[n][:, :, None, 0:H2].to_broadcast([P, NT, HEADS, H2]), ALU.mult))
                ch.link(eng.tensor_tensor(t4[:, :, :, H2:HD], f4[:, :, :, 0:H2], ws[n][:, :, None, H2:HD].to_broadcast([P, NT, HEADS, H2]), ALU.mult))
                ch.link(eng.tensor_tensor(r[:, :, :], r[:, :, :], t2[:, :, :], ALU.add))
                if wait_power:
                    eng.wait_ge(*wait_power)
                ch.link(eng.tensor_tensor(g, rg, ss[:, :, None].to_broadcast([P, N, HD]), ALU.mult))

            def stack_transposes(pe, ps, src, g):
                dst = ps[:, :].bitcast(BF16)
                for jj in range(4):
                    for t in range(NT):
                        hh = t * HEADS + 2 * (4 * g + jj)
                        ins = pe.transpose(dst[:, jj * SEQ + t * P:jj * SEQ + (t + 1) * P],
                                           src[:, hh:hh + 2, :, :].rearrange("p h g d -> p (h g d)"), identb[:, :])
                return ins

            def half_turn(dve, ch, f, tmp, dst, cname, sname, nh):
                c = W(cname).rearrange("p (t d) -> p t d", t=NT)
                sn = W(sname).rearrange("p (t d) -> p t d", t=NT)
                H2 = MD // 2
                V = nc.vector
                shape = [P, NT, nh, H2]
                ch.mark(V.tensor_tensor(dst, f, c[:, :, None, :].to_broadcast([P, NT, nh, MD]), ALU.mult))
                ch.mark(V.tensor_tensor(tmp[:, :, :, 0:H2], f[:, :, :, H2:MD], sn[:, :, None, 0:H2].to_broadcast(shape), ALU.mult))
                ch.link(V.tensor_tensor(tmp[:, :, :, H2:MD], f[:, :, :, 0:H2], sn[:, :, None, H2:MD].to_broadcast(shape), ALU.mult))
                return V.tensor_tensor(dst, dst, tmp, ALU.add)

            @block.sync
            def _(sp):
                for s in order:
                    kind, l, b = s[:3]
                    if kind == "load":
                        row = first_row + b
                        sp.dma_start(cx[b][:, :, :], dram["ctx"][bass.ds(row, 1)].rearrange("o (t p) d -> p (o t) d", p=P)).then_inc(sem["ctx_in", b], 16)
                        sp.dma_start(msk[b][:, :, :], dram["mask"][bass.ds(row, 1)].rearrange("o (t p) k -> p (o t) k", p=P)).then_inc(sem["mask_in", b], 16)
                        sp.dma_start(x[b][:, :, :], dram["x"][bass.ds(row, 1)].rearrange("o (t p) d -> p (o t) d", p=P)).then_inc(sem["x_in", b], 16)
                        sp.dma_start(mrow8[b][MD:MD + 1, :], dram["mrow"][bass.ds(row, 1)]).then_inc(sem["row_in", b], 16)
                    if kind == "shift":
                        sp.wait_ge(sem["shiftT"], at("shiftT", s))
                        if l == 2:
                            for t in range(NT):
                                sp.dma_start(q2T[b][MD + 1:MD + 2, :, t * P:(t + 1) * P], mT2[b][MQ * t:MQ * t + MQ, :]).then_inc(sem["shift_in", b], 16)
                        else:
                            for r in range(2):
                                for part in range(2):
                                    row = STK * r + KD + part
                                    n = 16 * r + 8 * part
                                    sp.dma_start(qT[b][row:row + 1, :, :], mT[b][n:n + 8, :]).then_inc(sem["shift_in", b], 16)
                    if kind == "store" or kind == "tail":
                        last = s if kind == "tail" else x_ready_from(s, order)
                        if last:
                            sp.wait_ge(sem["x_new"], at("x_new", last))
                        row = first_row + b
                        dst = out[bass.ds(row, 1)] if in_loop else out[row:row + 1]
                        sp.dma_start(dst.rearrange("o (t p) d -> p (o t) d", p=P), x[b][:, :, :]).then_inc(sem["stored"], 16)
                sp.wait_ge(sem["stored"], 16 * ROWS)

            @block.gpsimd
            def _(pool):
                ch = Chain(pool, sem["pool"])

                def power(t, n):
                    return pool.tensor_tensor(t, t, neghalf[:, 0:n], ALU.pow)

                for s in order:
                    kind, l, b = s[:3]
                    if kind == "load":
                        pool.wait_ge(sem["mask_in", b], 16)
                        ch.link(pool.tensor_scalar(bias[b][:, :, :], msk[b][:, :, :], 0.0, NEG, ALU.is_equal, ALU.mult))
                        adj = W("adj").rearrange("p (t k) -> p t k", t=NT)
                        pool.tensor_tensor(bias[b][:, :, :], bias[b][:, :, :], adj, ALU.add).then_inc(sem["bias"], 1)
                        pool.wait_ge(sem["bias"], at("bias", s))
                        pool.tensor_copy(bias_hi[b][:, :, :], bias[b][:, :, :]).then_inc(sem["bias_hi"], 1)
                        pool.wait_ge(sem["ctx_var"], at("ctx_var", s))
                        power(crms[b][:, :], NT).then_inc(sem["ctx_rms"], 1)
                    if kind == "kv" and l != 2:
                        pool.wait_ge(sem["k_in"], at("k_in", s))
                        k3 = kf[b][:, :, :].rearrange("p t (h d) -> p t h d", d=HD)
                        if l == 1:
                            rope(pool, ch, "k", b, kf[b], kr[b], kt2[b], kss[b], None)
                        kk = kf[b][:, :, :].rearrange("p t (h d) -> p (t h) d", d=HD)
                        rr = kr[b][:, :, :].rearrange("p t (h d) -> p (t h) d", d=HD)
                        n = NT * HEADS
                        prev = [t for t in order[:order.index(s)] if t[0] == "kv" and t[2] == b and t[1] != 2]
                        if prev:
                            pool.wait_ge(sem["kT1_ps"], at("kT1_ps", prev[-1]))
                        ch.link(pool.tensor_copy(ks[b][:, :, 3:6, :], kk[:, :, None, :].to_broadcast([P, n, 3, HD])))
                        ch.link(pool.tensor_tensor(rr, kk, ks[b][:, :, 3, :], ALU.subtract))
                        ch.link(pool.tensor_copy(ks[b][:, :, 0:2, :], rr[:, :, None, :].to_broadcast([P, n, 2, HD])))
                        pool.tensor_tensor(ks[b][:, :, 2, :], rr, ks[b][:, :, 0, :], ALU.subtract).then_inc(sem["k_stack"], 1)
                    if kind == "stats":
                        pool.wait_ge(sem["var"], at("var", s))
                        power(rstd[b][:, :], NT).then_inc(sem["rstd"], 1)
                        if l == 2:
                            pool.wait_ge(sem["rstd"], at("rstd", s))
                            ch.link(pool.tensor_tensor(rms[b][:, :], rstd[b][:, :], rstd[b][:, :], ALU.mult))
                            ch.link(pool.tensor_tensor(rms[b][:, :], rms[b][:, :], mv[b][:, :, 1], ALU.mult))
                            ch.link(pool.tensor_scalar(rms[b][:, :], rms[b][:, :], 1e-6, 0.0, ALU.add, ALU.add))
                            ch.link(power(rms[b][:, :], NT))
                            pool.tensor_tensor(rstd[b][:, :], rms[b][:, :], rstd[b][:, :], ALU.mult).then_inc(sem["rms"], 1)
                        add = {0: tbo[0], 3: tbo[3], 6: tbeta}.get(l)
                        src = add if add is not None else tbeta
                        pool.tensor_tensor(xb[b][:, :, :], x[b][:, :, :], src[:, None, :].to_broadcast([P, NT, P]), ALU.add).then_inc(sem["x_bias"], 1)
                    if kind == "query" and l == 1:
                        pool.wait_ge(sem["q_var"], at("q_var", s))
                        power(qss[b][:, :], NT * HEADS).then_inc(sem["q_rms"], 1)
                    if kind == "experts" and l == 2:
                        pool.wait_ge(sem["x_normed"], at("x_normed", ("norm", 6, b)))
                        pool.tensor_tensor(yr[b][:, :, :], xn[b][:, :, :], W("bo_f2")[:, None, :].to_broadcast([P, NT, P]), ALU.add).then_inc(sem["y_res"], 1)
                        pool.wait_ge(sem["y_var"], at("y_var", s))
                        power(rstd[b][:, :], NT).then_inc(sem["y_rstd"], 1)

            @block.scalar
            def _(act):
                for s in order:
                    kind, l, b = s[:3]

                    def evac(dst, use, cols, stage, **kw):
                        act.wait_ge(sem[use], at(use, s))
                        act.activation(dst, cols, ACT.Copy, **kw).then_inc(sem[stage], 1)

                    if kind == "load":
                        evac(ctxT[b][:, :], "ctxT_ps", bank("ctxT_ps", s)[:, 0:SEQ], "ctxT")
                        evac(biasT[b][:, :, :], "biasT_ps", bank("biasT_ps", s)[:, :].rearrange("p (t q) -> p t q", t=NT), "biasT")
                    if kind == "kv" and l != 2:
                        for g in range(2):
                            src = bank(f"kT{g}_ps", s)[:, :].bitcast(BF16).rearrange("p (j k) -> p j k", j=4)
                            evac(kT[b][:, 4 * g:4 * g + 4, :], f"kT{g}_ps", src, f"kT{g}")
                    if kind == "kv" and l == 2:
                        evac(k2T[b][0:MD, :], "kT2_ps", bank("kT2_ps", s)[0:MD, 0:SEQ], "kT0")
                    if kind == "norm":
                        evac(xT[b][:, :], "xT_ps", bank("xT_ps", s)[:, 0:SEQ], "xT")
                    if kind == "query" and l != 2:
                        n = NT * HEADS
                        act.wait_ge(sem["q_ready" if l == 1 else "q_in"], at("q_ready" if l == 1 else "q_in", s))
                        qq = qf[b][:, :, :].rearrange("p t (h d) -> p (t h) d", d=HD)
                        rr = qr[b][:, :, :].rearrange("p t (h d) -> p (t h) d", d=HD)
                        act.activation(qs[b][:, :, 1:4, :], qq[:, :, None, :].to_broadcast([P, n, 3, HD]), ACT.Copy).then_inc(sem["q_hi"], 1)
                        act.wait_ge(sem["q_rest"], at("q_rest", s))
                        act.activation(qs[b][:, :, 0:5:4, :], rr[:, :, None, :].to_broadcast([P, n, 2, HD]), ACT.Copy).then_inc(sem["q_mid"], 1)
                        for g in range(2):
                            src = bank(f"qT{g}_ps", s)[:, :].bitcast(BF16).rearrange("p (j k) -> p j k", j=4)
                            evac(qT[b][:, 4 * g:4 * g + 4, :], f"qT{g}_ps", src, f"qT{g}")
                    if kind == "query" and l == 2:
                        src = bank("qT2_ps", s)[0:MD, :].rearrange("p (h q) -> p h q", h=MQ)
                        act.wait_ge(sem["qT2_ps"], at("qT2_ps", s))
                        act.activation(q2T[b][0:MD, 0:2, :], src[:, 0:2, :], ACT.Copy).then_inc(sem["qT0"], 1)
                        act.activation(q2T[b][0:MD, 2:4, :], src[:, 2:4, :], ACT.Copy).then_inc(sem["qT1"], 1)
                    if kind == "shift":
                        if l == 2:
                            evac(mT2[b][:, :], "shift_ps", bank("shift_ps", s)[0:8, 0:P], "shiftT")
                        else:
                            evac(mT[b][:, :], "shift_ps", bank("shift_ps", s)[0:32, 0:P].bitcast(BF16), "shiftT")
                    if kind == "attend":
                        n = plan.nth[s]
                        before = prev_on("attend", s, 4)
                        if before:
                            act.wait_ge(sem["weighed"], at("weighed", before))
                        dst = probs[n % 4]
                        if l == 0:
                            act.wait_ge(sem["biased"], at("biased", s))
                            act.activation(dst[:, :, :], dst[:, :, :], ACT.Exp).then_inc(sem["probs"], 1)
                        else:
                            act.wait_ge(sem["scores_ps"], at("scores_ps", s))
                            w = 384 if l == 1 else 512
                            src = bank("scores_ps", s)[:, :].rearrange("p (r n) -> p r n", r=2)
                            act.activation(dst[:, :, 0:w], src[:, :, 0:w], ACT.Exp,
                                           scale=1.0 if l == 2 else HD ** -0.5).then_inc(sem["probs"], 1)
                    if kind == "mix":
                        evac(oT[b][:, :], "oT_ps", bank("oT_ps", s)[:, 0:SEQ], "oT")
                    if kind == "route":
                        if l == 1:
                            act.wait_ge(sem["gate_in"], at("gate_in", s))
                            act.activation(ge[b][:, :, :], lg[b][:, :, :], ACT.Exp).then_inc(sem["gate_exp"], 1)
                        rows = 16 if l == 1 else 8
                        src = bank("onehotT_ps", s)[0:rows, 0:P].bitcast(BF16)
                        evac(ohT[b][0:rows, :], "onehotT_ps", src, "onehotT")
                        if l == 1:
                            evac(uT[b][:, :], "u_ps", bank("u_ps", s)[:, 0:SEQ], "u")
                        else:
                            act.wait_ge(sem["onehotT"], at("onehotT", s))
                            act.activation(ohF[b][0:rows, :], ohT[b][0:rows, :], ACT.Copy).then_inc(sem["onehotF"], 1)
                    if kind == "experts" and l == 1:
                        for i in range(2):
                            act.wait_ge(sem[f"h{i}_ps"], at(f"h{i}_ps", s))
                            for ft in range(FT):
                                ins = act.activation(h[b][:, i, ft, :], bank(f"h{i}_ps", s)[:, ft * SEQ:(ft + 1) * SEQ],
                                                     ACT.Relu, bias=W("bi")[:, ft:ft + 1])
                            ins.then_inc(sem[f"h{i}"], 1)
                    if kind == "experts" and l == 2:
                        act.wait_ge(sem["h0_ps"], at("h0_ps", s))
                        act.activation(h[b][:, 0, :, :], bank("h0_ps", s)[:, :].rearrange("p (f q) -> p f q", f=FT), ACT.Gelu).then_inc(sem["h0"], 1)
                    if kind == "tail":
                        for i in range(2):
                            act.wait_ge(sem[f"h{i}_ps"], at(f"h{i}_ps", s))
                            act.activation(h[b][:, i, :, :], bank(f"h{i}_ps", s)[:, :].rearrange("p (f q) -> p f q", f=FT), ACT.Gelu_apprx_tanh).then_inc(sem[f"h{i}"], 1)

            @block.tensor
            def _(pe):
                ident = W("ident")

                def mm(dst, lhsT, rhs, start=True, stop=True, **kw):
                    return pe.matmul(dst, lhsT, rhs, start=start, stop=stop, **kw)

                for s in order:
                    kind, l, b = s[:3]
                    if kind == "load":
                        pe.wait_ge(sem["ctx_in", b], 16)
                        claim(pe, "ctxT_ps", s)
                        for t in range(NT):
                            ins = pe.transpose(bank("ctxT_ps", s)[:, t * P:(t + 1) * P], cx[b][:, t, :], ident)
                        ins.then_inc(sem["ctxT_ps"], 1)
                        pe.wait_ge(sem["bias"], at("bias", s))
                        claim(pe, "biasT_ps", s)
                        for k in range(NT):
                            for q in range(NT):
                                ins = pe.transpose(bank("biasT_ps", s)[:, k * SEQ + q * P:k * SEQ + (q + 1) * P],
                                                   bias[b][:, q, k * P:(k + 1) * P], ident)
                        ins.then_inc(sem["biasT_ps"], 1)
                    if kind == "kv":
                        load = ("load", 0, b)
                        pe.wait_ge(sem["ctxT"], at("ctxT", load))
                        claim(pe, "kv_ps", s)
                        ps = bank("kv_ps", s)
                        for t in range(NT):
                            c = ctxT[b][:, t * P:(t + 1) * P]
                            if l == 2:
                                ins = mm(ps[:, t * 2 * MD:(t + 1) * 2 * MD], c, kvw2[:, :])
                            else:
                                mm(ps[:, t * P:(t + 1) * P], c, W(f"wk{l}"))
                                ins = mm(ps[:, SEQ + t * P:SEQ + (t + 1) * P], c, W(f"wv{l}"))
                        ins.then_inc(sem["kv_ps"], 1)
                        if l == 2:
                            pe.wait_ge(sem["k_rot"], at("k_rot", s))
                            claim(pe, "kT2_ps", s)
                            for t in range(NT):
                                ins = pe.transpose(bank("kT2_ps", s)[0:MD, t * P:(t + 1) * P], k2[b][:, t, :], ident)
                            ins.then_inc(sem["kT2_ps"], 1)
                        else:
                            pe.wait_ge(sem["k_stack"], at("k_stack", s))
                            for g in range(2):
                                claim(pe, f"kT{g}_ps", s)
                                stack_transposes(pe, bank(f"kT{g}_ps", s), ks[b], g).then_inc(sem[f"kT{g}_ps"], 1)
                    if kind == "norm":
                        pe.wait_ge(sem["x_normed"], at("x_normed", s))
                        claim(pe, "xT_ps", s)
                        for t in range(NT):
                            ins = pe.transpose(bank("xT_ps", s)[:, t * P:(t + 1) * P], xn[b][:, t, :], ident)
                        ins.then_inc(sem["xT_ps"], 1)
                    if kind == "query":
                        normed = ("norm", l, b)
                        pe.wait_ge(sem["xT"], at("xT", normed))
                        claim(pe, "q_ps", s)
                        wq = {0: wq0s[:, :], 1: W("wq1"), 2: qw2[:, :], 3: W("wq3")}[l]
                        for t in range(NT):
                            ins = mm(bank("q_ps", s)[:, t * P:(t + 1) * P], xT[b][:, t * P:(t + 1) * P], wq)
                        ins.then_inc(sem["q_ps"], 1)
                        pe.wait_ge(sem["q_stack"], at("q_stack", s))
                        if l == 2:
                            claim(pe, "qT2_ps", s)
                            for hh in range(MQ):
                                for t in range(NT):
                                    ins = pe.transpose(bank("qT2_ps", s)[0:MD, hh * SEQ + t * P:hh * SEQ + (t + 1) * P],
                                                       q2[b][:, t, hh, :], ident)
                            ins.then_inc(sem["qT2_ps"], 1)
                        else:
                            for g in range(2):
                                claim(pe, f"qT{g}_ps", s)
                                stack_transposes(pe, bank(f"qT{g}_ps", s), qs[b], g).then_inc(sem[f"qT{g}_ps"], 1)
                    if kind == "max":
                        part = s[3]
                        if part == 0:
                            q, k = ("query", l, b), ("kv", l, b)
                            pe.wait_ge(sem["qT1"], at("qT1", q))
                            if l == 2:
                                pe.wait_ge(sem["kT0"], at("kT0", k))
                                pe.wait_ge(sem["mask_row"], at("mask_row", ("load", 0, b)))
                            else:
                                pe.wait_ge(sem["kT1"], at("kT1", k))
                            if l == 0:
                                pe.wait_ge(sem["bias_hi"], at("bias_hi", ("load", 0, b)))
                        for i in range(2):
                            claim(pe, f"max{i}_ps", s)
                            ps = bank(f"max{i}_ps", s)
                            if l == 2:
                                t = part
                                for hh in range(2):
                                    ins = mm(ps[:, hh * SEQ:(hh + 1) * SEQ], q2T[b][0:MD + 1, 2 * i + hh, t * P:(t + 1) * P],
                                             k2T[b][0:MD + 1, :])
                                ins.then_inc(sem[f"max{i}_ps"], 1)
                                continue
                            t, jp, r = part // 4, part % 4, i
                            rows = slice(STK * r, STK * r + KD)
                            ps2 = ps[:, :].rearrange("p (h k) -> p h k", h=2)
                            kn = P if l == 1 and t == 0 else SEQ
                            if l == 0:
                                mm(ps2, identb[:, :], bias_hi[b][:, t, None, :].to_broadcast([P, 2, SEQ]), skip_group_check=True)
                            for hh in range(2):
                                j = 2 * jp + hh
                                ins = mm(ps2[:, hh, 0:kn], qT[b][rows, j, t * P:(t + 1) * P], kT[b][rows, j, 0:kn],
                                         start=(l == 3 or (l == 1 and hh == 0)), skip_group_check=True)
                            if l == 1:
                                ins = mm(ps2[:, :, t * P:(t + 1) * P], identb[:, :],
                                         trib[:, None, :].to_broadcast([P, 2, P]), start=False, skip_group_check=True)
                            ins.then_inc(sem[f"max{i}_ps"], 1)
                    if kind == "shift":
                        pe.wait_ge(sem["shift"], at("shift", s))
                        claim(pe, "shift_ps", s)
                        if l == 2:
                            ins = pe.transpose(bank("shift_ps", s)[0:8, 0:P], nm2[b][:, :, :].rearrange("p t h -> p (t h)"), ident)
                        else:
                            ps = bank("shift_ps", s)[:, 0:P].bitcast(BF16)
                            for t in range(NT):
                                ins = pe.transpose(ps[0:32, t * P:(t + 1) * P], mp[b][:, t, :, :, :].rearrange("p r m j -> p (r m j)"), identb[:, :])
                        ins.then_inc(sem["shift_ps"], 1)
                    if kind == "attend":
                        part = s[3]
                        if part == 0:
                            pe.wait_ge(sem["shift_in", b], shift_at[b][l])
                        claim(pe, "scores_ps", s)
                        ps = bank("scores_ps", s)
                        for r in range(2):
                            for k in range(NT):
                                if l == 2:
                                    ins = mm(ps[:, r * 512 + k * SEQ:r * 512 + (k + 1) * SEQ], k2T[b][:, k * P:(k + 1) * P],
                                             q2T[b][:, 2 * part + r, :])
                                    continue
                                rows = slice(STK * r, STK * r + KD + 2)
                                q0 = P if l == 1 and k == 1 else 0
                                ins = mm(ps[:, r * 512 + k * SEQ:r * 512 + k * SEQ + SEQ - q0],
                                         kT[b][rows, part, k * P:(k + 1) * P], qT[b][rows, part, q0:SEQ],
                                         start=(l != 1 or k == 0), skip_group_check=True)
                            if l == 1:
                                diag = ps[:, r * 512:(r + 1) * 512].rearrange("p (k q) -> p k q", k=2)[:, :, 0:P]
                                ins = mm(diag, identb[:, :], triTb[:, None, :].to_broadcast([P, 2, P]),
                                         start=False, skip_group_check=True)
                        ins.then_inc(sem["scores_ps"], 1)
                        if part == 0:
                            pe.wait_ge(sem["v"], at("v", ("kv", l, b)))
                            mixed = [t for t in order[:order.index(s)] if t[0] == "mix"]
                            if mixed:
                                pe.wait_ge(sem["o"], at("o", mixed[-1]))
                        pe.wait_ge(sem["probs"], at("probs", s))
                        pr = probs[plan.nth[s] % 4]
                        for r in range(2):
                            hh = 2 * part + r
                            for t in range(NT):
                                ks_ = [0] if l == 1 and t == 0 else [0, 1]
                                for k in ks_:
                                    c = k * SEQ + t * P - (P if l == 1 and k == 1 else 0)
                                    if l == 2:
                                        dst = pv[:, (t * MQ + hh) * (MD + 1):(t * MQ + hh + 1) * (MD + 1)]
                                        w = v2[b][:, k, :]
                                    else:
                                        dst = pv[:, (t * HEADS + hh) * (HD + 1):(t * HEADS + hh + 1) * (HD + 1)]
                                        w = v[b][:, k, hh, :]
                                    ins = mm(dst, pr[:, r, c:c + P], w, start=(k == 0), stop=(k == ks_[-1]))
                        ins.then_inc(sem["weighed"], 1)
                    if kind == "mix":
                        pe.wait_ge(sem["o"], at("o", s))
                        claim(pe, "oT_ps", s)
                        for t in range(NT):
                            ins = pe.transpose(bank("oT_ps", s)[:, t * P:(t + 1) * P], o[b][:, t, :], ident)
                        ins.then_inc(sem["oT_ps"], 1)
                        pe.wait_ge(sem["oT"], at("oT", s))
                        claim(pe, "y_ps", s)
                        for t in range(NT):
                            ins = mm(bank("y_ps", s)[:, t * P:(t + 1) * P], oT[b][:, t * P:(t + 1) * P], W("ow2" if l == 2 else f"wo{l}"))
                        ins.then_inc(sem["y_ps"], 1)
                    if kind == "route":
                        pe.wait_ge(sem["xT"], at("xT", ("norm", 4 + l, b)))
                        claim(pe, "logits_ps", s)
                        for t in range(NT):
                            w = {0: sgn[:, :], 1: W("gate"), 2: W("wr")}[l]
                            ins = mm(bank("logits_ps", s)[:, t * E:(t + 1) * E], xT[b][:, t * P:(t + 1) * P], w)
                        ins.then_inc(sem["logits_ps"], 1)
                        n = 16 if l == 1 else 8
                        pe.wait_ge(sem["onehot"], at("onehot", s))
                        claim(pe, "onehotT_ps", s)
                        ps = bank("onehotT_ps", s)[:, 0:P].bitcast(BF16)
                        for t in range(NT):
                            ins = pe.transpose(ps[0:n, t * P:(t + 1) * P], oh[b][:, t, :, :].rearrange("p s e -> p (s e)")[:, 0:n], identb[:, :])
                        ins.then_inc(sem["onehotT_ps"], 1)
                        if l == 1:
                            claim(pe, "u_ps", s)
                            mm(bank("u_ps", s)[:, 0:SEQ], W("loraA"), xT[b][:, :]).then_inc(sem["u_ps"], 1)
                            pe.wait_ge(sem["onehotT"], at("onehotT", s))
                            claim(pe, "pick_ps", s)
                            for i in range(2):
                                ins = mm(bank("pick_ps", s)[:, i * SEQ:(i + 1) * SEQ], pickb[:, i * P:(i + 1) * P], ohT[b][:, :])
                            ins.then_inc(sem["pick_ps"], 1)
                        else:
                            pe.wait_ge(sem["onehotT"], at("onehotT", s))
                            for i in range(2):
                                claim(pe, f"spread{i}_ps", s)
                                for e in range(4):
                                    ins = mm(bank(f"spread{i}_ps", s)[:, e * SEQ:(e + 1) * SEQ],
                                             selb[:, (4 * i + e) * P:(4 * i + e + 1) * P], ohT[b][0:E, :])
                                ins.then_inc(sem[f"spread{i}_ps"], 1)
                    if kind == "experts":
                        r = ("route", l, b)
                        if l == 0:
                            pe.wait_ge(sem["spread1"], at("spread1", r))
                            pe.wait_ge(sem["onehotF"], at("onehotF", r))
                            claim(pe, "f_ps", s)
                            for t in range(NT):
                                dst = bank("f_ps", s)[:, t * P:(t + 1) * P]
                                mm(dst, ohF[b][0:E, t * P:(t + 1) * P], S16("bf0", E), stop=False)
                                for e in range(E):
                                    ins = mm(dst, xm[b][:, e, t * P:(t + 1) * P], W("wf0")[:, e * P:(e + 1) * P], start=False, stop=(e == E - 1))
                            ins.then_inc(sem["f_ps"], 1)
                        if l == 1:
                            for i in range(2):
                                if i == 0:
                                    pe.wait_ge(sem["picked"], at("picked", r))
                                claim(pe, f"h{i}_ps", s)
                                for ft in range(FT):
                                    dst = bank(f"h{i}_ps", s)[:, ft * SEQ:(ft + 1) * SEQ]
                                    mm(dst, W("wi")[:, ft * P:(ft + 1) * P], xT[b][:, :], stop=False)
                                    ins = mm(dst, W("loraB")[:, ft * P:(ft + 1) * P], um[b][:, i, :], start=False)
                                ins.then_inc(sem[f"h{i}_ps"], 1)
                        if l == 2:
                            pe.wait_ge(sem["spread1"], at("spread1", r))
                            pe.wait_ge(sem["onehotF"], at("onehotF", r))
                            claim(pe, "h0_ps", s)
                            for ft in range(FT):
                                dst = bank("h0_ps", s)[:, ft * SEQ:(ft + 1) * SEQ]
                                mm(dst, S16("b1_f2", E)[:, ft * P:(ft + 1) * P], ohF[b][0:E, :], stop=False)
                                for e in range(E):
                                    ins = mm(dst, W("w1_f2")[:, e * FF + ft * P:e * FF + (ft + 1) * P], xm[b][:, e, :], start=False, stop=(e == E - 1))
                            ins.then_inc(sem["h0_ps"], 1)
                        if l > 0:
                            claim(pe, "f_ps", s)
                            for i in range(3 - l):
                                pe.wait_ge(sem[f"h{i}"], at(f"h{i}", s))
                            for t in range(NT):
                                for i in range(3 - l):
                                    for ft in range(FT):
                                        w = W(f"wo_f{l}")[:, ft * P:(ft + 1) * P]
                                        ins = mm(bank("f_ps", s)[:, t * P:(t + 1) * P], h[b][:, i, ft, t * P:(t + 1) * P], w,
                                                 start=(i == 0 and ft == 0), stop=(i == 2 - l and ft == FT - 1))
                            ins.then_inc(sem["f_ps"], 1)
                    if kind == "tail":
                        pe.wait_ge(sem["xT"], at("xT", ("norm", 7, b)))
                        for i in range(2):
                            claim(pe, f"h{i}_ps", s)
                            for ft in range(FT):
                                n = FT * i + ft
                                ins = mm(bank(f"h{i}_ps", s)[:, ft * SEQ:(ft + 1) * SEQ], W("w1_f3")[:, n * P:(n + 1) * P], xT[b][:, :])
                            ins.then_inc(sem[f"h{i}_ps"], 1)
                        claim(pe, "f_ps", s)
                        for i in range(2):
                            pe.wait_ge(sem[f"h{i}"], at(f"h{i}", s))
                        for t in range(NT):
                            for n in range(FT3):
                                ins = mm(bank("f_ps", s)[:, t * P:(t + 1) * P], h[b][:, n // FT, n % FT, t * P:(t + 1) * P],
                                         W("w2_f3")[:, n * P:(n + 1) * P], start=(n == 0), stop=(n == FT3 - 1))
                        ins.then_inc(sem["f_ps"], 1)

            @block.vector
            def _(dve):
                ch = Chain(dve, sem["dve"])
                V = nc.vector

                def half(ap):
                    return ap.rearrange("p (t d) -> p t d", t=NT)

                def layer_stats(src, b, m, sums):
                    for t in range(NT):
                        ch.link(V.bn_stats(sums[b][:, t, :], src[:, t, :]))
                    for t in range(NT):
                        ch.link(V.bn_aggr(m[b][:, t, :], sums[b][:, t, :]))

                for s in order:
                    kind, l, b = s[:3]
                    if kind == "load":
                        dve.wait_ge(sem["ctx_in", b], 16)
                        layer_stats(cx[b], b, cmv, cst)
                        ch.link(V.tensor_tensor(crms[b][:, :], cmv[b][:, :, 0], cmv[b][:, :, 0], ALU.mult))
                        ch.link(V.tensor_tensor(crms[b][:, :], crms[b][:, :], cmv[b][:, :, 1], ALU.add))
                        V.tensor_scalar(crms[b][:, :], crms[b][:, :], 1e-6, None, ALU.add).then_inc(sem["ctx_var"], 1)
                        dve.wait_ge(sem["row_in", b], 16)
                        V.tensor_scalar(k2T[b][MD:MD + 1, :], mrow8[b][MD:MD + 1, :], 0.0, FILL, ALU.is_equal, ALU.mult).then_inc(sem["mask_row"], 1)
                    if kind == "kv":
                        dve.wait_ge(sem["kv_ps"], at("kv_ps", s))
                        ps = bank("kv_ps", s)
                        if l == 2:
                            dve.wait_ge(sem["ctx_rms"], at("ctx_rms", ("load", 0, b)))
                            for t in range(NT):
                                V.tensor_scalar(v2[b][:, t, 0:MD], ps[:, t * 2 * MD + MD:(t + 1) * 2 * MD], crms[b][:, t:t + 1], None, ALU.mult)\
                                 .then_inc(sem["v"] if t == NT - 1 else sem["dve"], 1)
                                if t < NT - 1:
                                    ch.n += 1
                            kk = kf[b][:, :, 0:MD]
                            for t in range(NT):
                                ins = V.tensor_scalar(kk[:, t, :], ps[:, t * 2 * MD:t * 2 * MD + MD], crms[b][:, t:t + 1], None, ALU.mult)
                                if t < NT - 1:
                                    ch.mark(ins)
                            ins.then_inc(sem["k_in"], 1)
                            dve.wait_ge(sem["k_in"], at("k_in", s))
                            half_turn(dve, ch, kk[:, :, None, :], kr[b][:, :, 0:MD].unsqueeze(2), k2[b][:, :, None, :], "ck2", "sk2", 1).then_inc(sem["k_rot"], 1)
                        else:
                            vin = half(ps[:, SEQ:2 * SEQ])
                            vd = v[b][:, :, :, 0:HD]
                            if l == 1:
                                V.tensor_copy(vd, vin.rearrange("p t (h d) -> p t h d", d=HD)).then_inc(sem["v"], 1)
                                V.tensor_copy(kf[b][:, :, :], half(ps[:, 0:SEQ])).then_inc(sem["k_in"], 1)
                            else:
                                bv = W(f"bv{l}").rearrange("p (h d) -> p h d", d=HD)
                                for t in range(NT):
                                    ins = V.tensor_tensor(vd[:, t], vin[:, t].rearrange("p (h d) -> p h d", d=HD), bv, ALU.add)
                                    if t < NT - 1:
                                        ch.mark(ins)
                                ins.then_inc(sem["v"], 1)
                                V.tensor_tensor(kf[b][:, :, :], half(ps[:, 0:SEQ]), W(f"bk{l}")[:, None, :].to_broadcast([P, NT, P]), ALU.add).then_inc(sem["k_in"], 1)
                    if kind == "stats":
                        prev = x_ready_from(s, order)
                        if prev:
                            dve.wait_ge(sem["x_new"], at("x_new", prev))
                        elif in_loop:
                            dve.wait_ge(sem["x_in", b], 16)
                        layer_stats(x[b], b, mv, st)
                        V.tensor_scalar(rstd[b][:, :], mv[b][:, :, 1], 1e-5, None, ALU.add).then_inc(sem["var"], 1)
                    if kind == "norm":
                        n = "rms" if l == 2 else "rstd"
                        dve.wait_ge(sem[n], at(n, ("stats", l, b)))
                        for t in range(NT):
                            ins = V.tensor_scalar(xn[b][:, t, :], x[b][:, t, :], mv[b][:, t, 0:1], rstd[b][:, t:t + 1], ALU.subtract, ALU.mult)
                            if t < NT - 1:
                                ch.mark(ins)
                        ins.then_inc(sem["x_normed"], 1)
                    if kind == "query":
                        dve.wait_ge(sem["q_ps"], at("q_ps", s))
                        ps = half(bank("q_ps", s)[:, 0:SEQ])
                        if l in (0, 3):
                            bq = bq0s[:, :] if l == 0 else W("bq3")
                            V.tensor_tensor(qf[b][:, :, :], ps, bq[:, None, :].to_broadcast([P, NT, P]), ALU.add).then_inc(sem["q_in"], 1)
                            dve.wait_ge(sem["q_in"], at("q_in", s))
                        else:
                            V.tensor_copy(qf[b][:, :, :], ps).then_inc(sem["q_in"], 1)
                            dve.wait_ge(sem["q_in"], at("q_in", s))
                        if l == 1:
                            rope(V, ch, "q", b, qf[b], qr[b], qt2[b], qss[b], (sem["q_rms"], at("q_rms", s)))
                            V.tensor_copy(qt2[b][:, 0, 0:1], qf[b][:, 0, 0:1]).then_inc(sem["q_ready"], 1)
                        if l == 2:
                            q4 = qf[b][:, :, :].rearrange("p t (h d) -> p t h d", d=MD)
                            r4 = qr[b][:, :, :].rearrange("p t (h d) -> p t h d", d=MD)
                            half_turn(dve, ch, q4, r4, q2[b][:, :, :, :], "cq2", "sq2", MQ).then_inc(sem["q_stack"], 1)
                        else:
                            qq = qf[b][:, :, :].rearrange("p t (h d) -> p (t h) d", d=HD)
                            rr = qr[b][:, :, :].rearrange("p t (h d) -> p (t h) d", d=HD)
                            dve.wait_ge(sem["q_hi"], at("q_hi", s))
                            V.tensor_tensor(rr, qq, qs[b][:, :, 1, :], ALU.subtract).then_inc(sem["q_rest"], 1)
                            dve.wait_ge(sem["q_mid"], at("q_mid", s))
                            V.tensor_tensor(qs[b][:, :, 5, :], rr, qs[b][:, :, 0, :], ALU.subtract).then_inc(sem["q_stack"], 1)
                    if kind == "max":
                        part = s[3]
                        for i in range(2):
                            dve.wait_ge(sem[f"max{i}_ps"], at(f"max{i}_ps", s))
                            ps = bank(f"max{i}_ps", s)[:, :].rearrange("p (h k) -> p h k", h=2)
                            if l == 2:
                                dst, kn = nm2[b][:, part, 2 * i:2 * i + 2], SEQ
                            else:
                                t, jp = part // 4, part % 4
                                dst, kn = nm[b][:, t, i, 2 * jp:2 * jp + 2], (P if l == 1 and t == 0 else SEQ)
                            V.tensor_reduce(dst, ps[:, :, 0:kn], AX.X, ALU.max, negate=True).then_inc(sem[f"max{i}"], 1)
                    if kind == "shift":
                        lastp = ("max", l, b, 7 if l != 2 else 1)
                        dve.wait_ge(sem["max0"], at("max0", lastp))
                        dve.wait_ge(sem["max1"], at("max1", lastp))
                        if l == 2:
                            V.tensor_copy(nm2[b][:, 0, 0:1], nm2[b][:, 0, 0:1]).then_inc(sem["shift"], 1)
                        else:
                            for t in range(NT):
                                ch.link(V.tensor_copy(mp[b][:, t, :, 0, :], nm[b][:, t, :, :]))
                            for t in range(NT):
                                ins = V.tensor_tensor(mp[b][:, t, :, 1, :], nm[b][:, t, :, :], mp[b][:, t, :, 0, :], ALU.subtract)
                                if t < NT - 1:
                                    ch.mark(ins)
                            ins.then_inc(sem["shift"], 1)
                    if kind == "attend" and l == 0:
                        n = plan.nth[s]
                        before = prev_on("attend", s, 4)
                        if before:
                            dve.wait_ge(sem["weighed"], at("weighed", before))
                        if s[3] == 0:
                            dve.wait_ge(sem["biasT"], at("biasT", ("load", 0, b)))
                        dve.wait_ge(sem["scores_ps"], at("scores_ps", s))
                        bt = biasT[b][:, :, :].rearrange("p k q -> p (k q)")
                        V.tensor_tensor(probs[n % 4][:, :, :], bank("scores_ps", s)[:, :].rearrange("p (r n) -> p r n", r=2),
                                        bt[:, None, :].to_broadcast([P, 2, 512]), ALU.add).then_inc(sem["biased"], 1)
                    if kind == "mix":
                        lastp = ("attend", l, b, 7 if l != 2 else 1)
                        dve.wait_ge(sem["weighed"], at("weighed", lastp))
                        nh, d = (MQ, MD) if l == 2 else (HEADS, HD)
                        n = NT * nh
                        z = pv[:, 0:n * (d + 1)].rearrange("p (n d) -> p n d", d=d + 1)
                        ch.link(V.reciprocal(rec[b][:, 0:n], z[:, :, d]))
                        V.tensor_tensor(o[b][:, :, :].rearrange("p t (h d) -> p (t h) d", d=d), z[:, :, 0:d],
                                        rec[b][:, 0:n, None].to_broadcast([P, n, d]), ALU.mult).then_inc(sem["o"], 1)
                        dve.wait_ge(sem["y_ps"], at("y_ps", s))
                        res = x
                        dve.wait_ge(sem["x_bias"], at("x_bias", ("stats", l, b)))
                        if l in (0, 3):
                            res = xb
                        V.scalar_tensor_tensor(out=x[b][:, :, :], in0=half(bank("y_ps", s)[:, 0:SEQ]), scalar=tg[:, l:l + 1],
                                               in1=res[b][:, :, :], op0=ALU.mult, op1=ALU.add).then_inc(sem["x_new"], 1)
                    if kind == "route":
                        dve.wait_ge(sem["logits_ps"], at("logits_ps", s))
                        ps = bank("logits_ps", s)[:, 0:NT * E].rearrange("p (t e) -> p t e", t=NT)
                        vals = lg
                        if l == 1:
                            V.tensor_tensor(lg[b][:, :, :], ps, W("gateb")[:, None, :].to_broadcast([P, NT, E]), ALU.add).then_inc(sem["logits"], 1)
                            dve.wait_ge(sem["logits"], at("logits", s))
                            ch.link(V.tensor_reduce(gm[b][:, :], lg[b][:, :, :], AX.X, ALU.max))
                            V.tensor_tensor(lg[b][:, :, :], lg[b][:, :, :], gm[b][:, :, None].to_broadcast([P, NT, E]), ALU.subtract).then_inc(sem["gate_in"], 1)
                            dve.wait_ge(sem["gate_exp"], at("gate_exp", s))
                            vals = ge
                        else:
                            V.tensor_copy(lg[b][:, :, :], ps).then_inc(sem["logits"], 1)
                            dve.wait_ge(sem["logits"], at("logits", s))
                        for t in range(NT):
                            ch.link(V.max(mx[b][:, t, :], vals[b][:, t, :]))
                        for t in range(NT):
                            ch.link(V.max_index(ix[b][:, t, :], mx[b][:, t, :], vals[b][:, t, :]))
                        ch.link(V.tensor_copy(ixf[b][:, :, :], ix[b][:, :, :]))
                        ns = 2 if l == 1 else 1
                        for t in range(NT):
                            for i in range(ns):
                                ins = V.tensor_scalar(oh[b][:, t, i, :], W("iota"), ixf[b][:, t, i:i + 1], None, ALU.is_equal)
                                if (t, i) != (NT - 1, ns - 1):
                                    ch.mark(ins)
                        ins.then_inc(sem["onehot"], 1)
                        if l == 1:
                            ch.link(V.tensor_reduce(gs[b][:, :], ge[b][:, :, :], AX.X, ALU.add))
                            ch.link(V.reciprocal(gs[b][:, :], gs[b][:, :]))
                            ch.link(V.tensor_tensor(gv[b][:, :], mx[b][:, :, 0], mx[b][:, :, 1], ALU.add))
                            ch.link(V.scalar_tensor_tensor(out=gv[b][:, :], in0=gv[b][:, :], scalar=tg[:, 5:6], in1=gs[b][:, :], op0=ALU.mult, op1=ALU.mult))
                            dve.wait_ge(sem["u"], at("u", s))
                            dve.wait_ge(sem["pick_ps"], at("pick_ps", s))
                            V.tensor_tensor(um[b][:, :, :], bank("pick_ps", s)[:, :].rearrange("p (i q) -> p i q", i=2),
                                            uT[b][:, None, :].to_broadcast([P, 2, SEQ]), ALU.mult).then_inc(sem["picked"], 1)
                        else:
                            for i in range(2):
                                dve.wait_ge(sem[f"spread{i}_ps"], at(f"spread{i}_ps", s))
                                V.tensor_tensor(xm[b][:, 4 * i:4 * i + 4, :], bank(f"spread{i}_ps", s)[:, :].rearrange("p (e q) -> p e q", e=4),
                                                xT[b][:, None, :].to_broadcast([P, 4, SEQ]), ALU.mult).then_inc(sem[f"spread{i}"], 1)
                    if kind == "experts":
                        dve.wait_ge(sem["f_ps"], at("f_ps", s))
                        dve.wait_ge(sem["x_bias"], at("x_bias", ("stats", 4 + l, b)))
                        ps = half(bank("f_ps", s)[:, 0:SEQ])
                        if l == 0:
                            V.scalar_tensor_tensor(out=x[b][:, :, :], in0=ps, scalar=tg[:, 4:5], in1=x[b][:, :, :],
                                                   op0=ALU.mult, op1=ALU.add).then_inc(sem["x_new"], 1)
                        if l == 1:
                            V.tensor_tensor(y[b][:, :, :], ps, bo2x[:, None, :].to_broadcast([P, NT, P]), ALU.add).then_inc(sem["f_in"], 1)
                            dve.wait_ge(sem["f_in"], at("f_in", s))
                            for t in range(NT):
                                ins = V.scalar_tensor_tensor(out=x[b][:, t, :], in0=y[b][:, t, :], scalar=gv[b][:, t:t + 1], in1=x[b][:, t, :],
                                                             op0=ALU.mult, op1=ALU.add)
                                if t < NT - 1:
                                    ch.mark(ins)
                            ins.then_inc(sem["x_new"], 1)
                        if l == 2:
                            dve.wait_ge(sem["y_res"], at("y_res", s))
                            V.tensor_tensor(y[b][:, :, :], ps, yr[b][:, :, :], ALU.add).then_inc(sem["f_in"], 1)
                            dve.wait_ge(sem["f_in"], at("f_in", s))
                            layer_stats(y[b], b, mv, st)
                            V.tensor_scalar(rstd[b][:, :], mv[b][:, :, 1], 1e-12, None, ALU.add).then_inc(sem["y_var"], 1)
                            dve.wait_ge(sem["y_rstd"], at("y_rstd", s))
                            for t in range(NT):
                                ch.link(V.tensor_scalar(y[b][:, t, :], y[b][:, t, :], mv[b][:, t, 0:1], rstd[b][:, t:t + 1], ALU.subtract, ALU.mult))
                            ch.link(V.tensor_tensor(y[b][:, :, :], y[b][:, :, :], tgam[:, None, :].to_broadcast([P, NT, P]), ALU.mult))
                            V.tensor_tensor(x[b][:, :, :], y[b][:, :, :], xb[b][:, :, :], ALU.add).then_inc(sem["x_new"], 1)
                    if kind == "tail":
                        dve.wait_ge(sem["f_ps"], at("f_ps", s))
                        dve.wait_ge(sem["x_bias"], at("x_bias", ("stats", 7, b)))
                        for t in range(NT):
                            n = b * NT + t
                            ins = V.scalar_tensor_tensor(out=x[b][:, t, :], in0=bank("f_ps", s)[:, t * P:(t + 1) * P], scalar=wsum[:, n:n + 1],
                                                         in1=x[b][:, t, :], op0=ALU.mult, op1=ALU.add)
                            if t < NT - 1:
                                ch.mark(ins)
                        ins.then_inc(sem["x_new"], 1)

        with nc.Fori(0, TURNS) as i:
            with nc.Block() as block:
                programs(block, turn, plan, (TURNS - 1 - i) * ROWS, True)
            nc.all_engine_barrier(sems_to_clear=all_sems)

        if SUBLAYERS == 8:
            with nc.Block() as block:
                programs(block, tail, tail_plan, 0, False)



def kernel(**inputs):
    import numpy as np
    import concourse.bacc as _bacc
    from concourse import mybir as _mybir
    from concourse.bass_utils import run_bass_kernel_spmd as _run

    a = {k: np.asarray(v) for k, v in inputs.items()}
    f = np.float32

    def rows(n):
        return np.broadcast_to(a[n].reshape(1, -1), (P, a[n].size))

    def tiles(w):
        return w.reshape(-1, P, w.shape[-1]).transpose(1, 0, 2).reshape(P, -1)

    pos = np.arange(SEQ, dtype=f)

    def spread(t):
        return tiles(np.ascontiguousarray(t.astype(f)))

    inv1 = (1.0 / np.power(f(500000.0), np.arange(0, HD, 2, dtype=f) / f(HD))).astype(f)
    ang1 = np.outer(pos, inv1).astype(f)
    emb1 = np.concatenate([ang1, ang1], -1)
    ts2 = np.power(f(10000.0), f(2.0 / MD) * np.arange(MD // 2, dtype=f)).astype(f)
    angk = (pos[:, None] / ts2).astype(f)
    angq = ((pos + SEQ)[:, None] / ts2).astype(f)
    sc = MD ** -0.5
    cos2, sin2 = (lambda g: np.concatenate([np.cos(g), np.cos(g)], -1)), (lambda g: np.concatenate([-np.sin(g), np.sin(g)], -1))
    i, j = np.arange(P)[:, None], np.arange(P)[None, :]
    tri = np.where(j <= i, 0.0, NEG).astype(f)
    ex = {
        "ident": np.eye(P, dtype=f), "tri": tri, "triT": np.ascontiguousarray(tri.T),
        "iota": np.broadcast_to(np.arange(E, dtype=f), (P, E)),
        "g": np.broadcast_to(np.concatenate([a["g_xattn"], a["g_ffn"]])[None], (P, 8)),
        "adj": tiles(a["L0_xattn_adj"]),
        "sig": a["L0_ffn_tile_sigs"].T, "wf0": a["L0_ffn_W"].transpose(1, 0, 2).reshape(P, -1),
        "qnw": rows("L1_xattn_q_norm_w"), "knw": rows("L1_xattn_k_norm_w"),
        "cos1": spread(np.cos(emb1)), "sin1": spread(np.sin(emb1)),
        "wi": a["L1_ffn_wi"].T, "bi": a["L1_ffn_bi"].reshape(FT, P).T, "wo_f1": tiles(a["L1_ffn_wo"].T), "bo_f1": rows("L1_ffn_bo"),
        "loraA": a["L1_ffn_lora_A"].reshape(P, P).T, "loraB": a["L1_ffn_lora_B"].transpose(0, 2, 1).reshape(P, FF),
        "gate": a["L1_ffn_gate_w"].T, "gateb": rows("L1_ffn_gate_b"),
        "rms": a["L2_xattn_rms_scale"].reshape(P, 1), "qw2": a["L2_xattn_q_w"].transpose(1, 0, 2).reshape(P, P),
        "kvw2": a["L2_xattn_kv_w"][:, 0].transpose(1, 0, 2).reshape(P, 2 * MD), "ow2": a["L2_xattn_out_w"].reshape(P, P),
        "cq2": spread(cos2(angq) * sc), "sq2": spread(sin2(angq) * sc), "ck2": spread(cos2(angk)), "sk2": spread(sin2(angk)),
        "wr": a["L2_ffn_Wr"].T, "w1_f2": a["L2_ffn_W1"].transpose(1, 0, 2).reshape(P, -1), "wo_f2": tiles(a["L2_ffn_Wo"]),
        "bo_f2": rows("L2_ffn_bo"), "gamma": rows("L2_ffn_gamma"), "beta": rows("L2_ffn_beta"),
        "w1_f3": a["L3_ffn_w1"], "w2_f3": tiles(a["L3_ffn_w2"]), "ew": tiles(a["L3_ffn_expert_weights"]),
    }
    for l in (0, 1, 3):
        for n in "qkvo":
            ex[f"w{n}{l}"] = a[f"L{l}_xattn_W{n}"].T
            if l != 1:
                ex[f"b{n}{l}"] = rows(f"L{l}_xattn_b{n}")
    arrays = {n: np.concatenate([ex[m] for m, _ in parts], axis=1) for n, parts in PACKS.items()}
    sel = np.zeros((16, E, P), f)
    for e in range(E):
        sel[e, e, :] = 1.0
    pick = np.zeros((2, 16, P), f)
    for c in range(2):
        for e in range(E):
            pick[c, c * E + e, e * RANK:(e + 1) * RANK] = 1.0
    small = np.zeros((16, SMALL_W), f)
    for n, w, r in (("sel", sel.reshape(16, -1), 16), ("pick1", pick[0], 16), ("pick2", pick[1], 16),
                    ("bf0", a["L0_ffn_b"], E), ("b1_f2", a["L2_ffn_b1"], E)):
        c, k = SMALL_COLS[n]
        small[0:r, c:c + k] = w
    arrays |= {"small": small, "x": a["x"], "ctx": a["ctx_1024"], "mask": a["mask_Bx1xSxS2_ik1"][:, 0],
               "mrow": a["mask_BxS2_bk0"]}
    arrays = {n: np.ascontiguousarray(v) for n, v in arrays.items()}

    nc = _bacc.Bacc("TRN2", target_bir_lowering=False, num_devices=1)
    dram = {n: nc.dram_tensor(f"in_{n}", v.shape, _mybir.dt.from_np(v.dtype), kind="ExternalInput").ap() for n, v in arrays.items()}
    out = nc.dram_tensor("out", (BATCH, SEQ, P), _mybir.dt.float32, kind="ExternalOutput").ap()
    build(nc, dram, out)
    r = _run(nc, [{f"in_{n}": v for n, v in arrays.items()}], core_ids=[0])
    return r.results[0]["out"]
```

```python
from contextlib import ExitStack

import concourse.bass as bass
from concourse import mybir

F32 = mybir.dt.float32
BF16 = mybir.dt.bfloat16
I32 = mybir.dt.int32
U32 = mybir.dt.uint32
U8 = mybir.dt.uint8
ALU = mybir.AluOpType
ACT = mybir.ActivationFunctionType
AX = mybir.AxisListType

P = 128
BATCH = 8
SEQ = 256
NT = SEQ // P
ROWS = 2
TURNS = BATCH // ROWS
HEADS = 16
HD = P // HEADS
MQ, MD = 4, 32
E = 8
RANK = 16
FF = 512
FT = FF // P
FF3 = 1024
FT3 = FF3 // P
STK = 64
TERMS = 6
KD = TERMS * HD
NEG = -1.0e30
FILL = -2.3819763e+38
SUBLAYERS = 8


def columns(parts):
    at, out = 0, {}
    for name, n in parts:
        out[name] = (at, n)
        at += n
    return out, at


PACKS = {
    "c0": [("ident", P), ("tri", P), ("triT", P), ("iota", E), ("g", 8),
           ("wq0", P), ("wk0", P), ("wv0", P), ("wo0", P), ("bq0", P), ("bk0", P), ("bv0", P), ("bo0", P),
           ("adj", NT * SEQ)],
    "c1": [("sig", E), ("wf0", E * P),
           ("wq1", P), ("wk1", P), ("wv1", P), ("wo1", P), ("qnw", HD), ("knw", HD),
           ("cos1", NT * HD), ("sin1", NT * HD)],
    "c2": [("wi", FF), ("bi", FT), ("wo_f1", FF), ("bo_f1", P), ("loraA", P), ("loraB", FF), ("gate", E),
           ("gateb", E),
           ("rms", 1), ("qw2", P), ("kvw2", 2 * MD), ("ow2", P),
           ("cq2", NT * MD), ("sq2", NT * MD), ("ck2", NT * MD), ("sk2", NT * MD)],
    "c3": [("wr", E), ("w1_f2", E * FF), ("wo_f2", FF), ("bo_f2", P), ("gamma", P), ("beta", P)],
    "c4": [("wq3", P), ("wk3", P), ("wv3", P), ("wo3", P), ("bq3", P), ("bk3", P), ("bv3", P), ("bo3", P),
           ("w1_f3", FF3), ("w2_f3", FF3), ("ew", 2 * NT * ROWS)],
}
SMALL = [("sel", E * P), ("pick1", P), ("pick2", P), ("bf0", P), ("b1_f2", FF)]
WHERE = {}
WIDTH = {}
for _pack, _parts in PACKS.items():
    _cols, WIDTH[_pack] = columns(_parts)
    WHERE.update({_n: (_pack, *_c) for _n, _c in _cols.items()})
SMALL_COLS, SMALL_W = columns(SMALL)



def row_steps(b):
    def keys(l):
        if 2 * l >= SUBLAYERS or l > 3:
            return [None] * 5
        steps = [("kv", l, b), ("k_turn", l, b) if l == 1 else None]
        return steps + ([("k_mid", l, b), ("k_low", l, b)] if l != 2 else [None, None]) + [("k_flip", l, b)]

    out = [("load", 0, b), ("bias", 0, b)] + keys(0)
    for l in range(4):
        parts_a, parts_b = (8, 8) if l != 2 else (2, 2)
        if 2 * l < SUBLAYERS:
            out += [("stats", l, b), ("norm", l, b), ("flip", l, b), ("query", l, b)]
            out += [("q_turn", l, b)] if l == 1 else []
            out += [("q_mid", l, b), ("q_low", l, b)] if l != 2 else []
            out += [("q_flip", l, b)]
            out += [("max", l, b, p) for p in range(parts_a)]
            out += [("shift", l, b), ("shift_flip", l, b)]
            for p in range(parts_b + AHEAD):
                out += [("attend", l, b, p)] if p < parts_b else []
                out += [("weigh", l, b, p - AHEAD)] if p >= AHEAD else []
            out += [("divide", l, b), ("o_flip", l, b), ("mix", l, b)]
        k = keys(l + 1)
        if 2 * l + 1 < SUBLAYERS and l < 3:
            out += [k[0], ("stats", 4 + l, b), k[1], ("norm", 4 + l, b), ("flip", 4 + l, b), k[2], ("route", l, b), k[3],
                    ("choose", l, b), k[4], ("spread", l, b), ("inner", l, b), ("outer", l, b)]
            out += [("finish", l, b)] if l == 2 else []
        else:
            out += k
    return [t for t in out if t] + [("store", 0, b)]


AHEAD = 2
COST = {"kv": (.9, .9), "k_turn": (0, 0), "k_mid": (0, 0), "k_low": (0, 0), "k_flip": (.9, .9),
        "stats": (0, 4), "norm": (0, 1), "flip": (.3, 1), "query": (.4, 1.5), "q_turn": (0, 2), "q_mid": (0, 1.5),
        "q_low": (0, .6), "q_flip": (.9, 2), "max": (.8, 1.1), "shift": (0, 1), "shift_flip": (.2, 4),
        "attend": (.5, 1), "weigh": (.5, .5), "divide": (0, 1.5), "o_flip": (.3, 1), "mix": (.4, .8),
        "route": (.1, 3), "choose": (.1, 1), "spread": (.8, 3), "inner": (8, 9), "outer": (3, 3.5), "finish": (0, 4),
        "load": (.3, 1), "bias": (.5, 1), "store": (0, 0)}
LAG = 45


def turn_order():
    rows, at, ready, out, holder = [row_steps(b) for b in range(ROWS)], [0] * ROWS, [LAG * b for b in range(ROWS)], [], None
    now = 0.0
    while any(at[b] < len(rows[b]) for b in range(ROWS)):
        free = [b for b in range(ROWS) if at[b] < len(rows[b])
                and not (rows[b][at[b]][0] == "attend" and holder not in (None, b))]
        b = min(free, key=lambda b: ready[b])
        s = rows[b][at[b]]
        if s[0] == "attend":
            holder = b
        if s[0] == "divide":
            holder = None
        out.append(s)
        at[b] += 1
        busy, delay = COST[s[0]]
        now = max(now, ready[b])
        ready[b] = now + max(delay, busy)
        now += busy
    return out


def psum_uses(s):
    kind, l, b = s[:3]
    wide = l != 2
    uses = {
        "load": [("ctxT_ps", "one", "ctxT")],
        "bias": [("biasT_ps", "one", "biasT")],
        "kv": [("kv_ps", "one", "k_in")],
        "k_flip": [("kT0_ps", "one", "kT0"), ("kT1_ps", "one", "kT1")] if wide else [("kT2_ps", "one", "kT0")],
        "flip": [("xT_ps", "one", "xT")],
        "query": [("q_ps", "one", "q_in")],
        "q_flip": [("qT0_ps", "one", "qT0"), ("qT1_ps", "one", "qT1")] if wide else [("qT2_ps", "two", "qT1")],
        "max": [("max0_ps", "one", "max0"), ("max1_ps", "one", "max1")],
        "shift_flip": [("shift_ps", "one", "shiftT")],
        "attend": [("scores_ps", "two", "biased" if l == 0 else "probs")],
        "o_flip": [("oT_ps", "one", "oT")],
        "mix": [("y_ps", "one", "x_mixed")],
        "route": [("logits_ps", "one", "logits")],
        "choose": [("onehotT_ps", "one", "onehotT")] + ([("u_ps", "one", "u")] if l == 1 else []),
        "spread": [("pick_ps", "one", "picked")] if l == 1 else
                  [("spread0_ps", "two", "spread0"), ("spread1_ps", "two", "spread1")],
        "inner": [] if l == 0 else [("h0_ps", "two", "h0"), ("h1_ps", "two", "h1")][:3 - l],
        "outer": [("f_ps", "one", "f_in" if l else "x_fed")],
        "tail": [("h0_ps", "two", "h0"), ("h1_ps", "two", "h1"), ("f_ps", "one", "x_fed")],
    }
    return uses.get(kind, [])


def stages(s):
    kind, l, b = s[:3]
    wide = l != 2
    more = {
        "load": ["ctxT", "ctx_var", "ctx_rms", "mask_row"],
        "bias": ["bias", "bias_hi", "biasT"],
        "kv": ["k_in", "v"] + (["k_var", "k_rms", "k_prod"] if l == 1 else ["k_hi"] if wide else ["k_rot"]),
        "k_turn": ["k_ready", "k_hi"],
        "k_mid": ["k_rest", "k_mid"],
        "k_low": ["k_stack"],
        "k_flip": ["kT0", "kT1"] if wide else ["kT0"],
        "stats": ["var", "rstd"] + (["rms"] if l == 2 else []) + ["x_bias"],
        "norm": ["x_normed"],
        "flip": ["xT"],
        "query": ["q_in"] + (["q_var", "q_rms", "q_prod"] if l == 1 else ["q_hi"] if wide else ["q_stack"]),
        "q_turn": ["q_ready", "q_hi"],
        "q_mid": ["q_rest", "q_mid"],
        "q_low": ["q_stack"],
        "q_flip": ["qT0", "qT1"],
        "max": ["max0", "max1"],
        "shift": ["shift"],
        "shift_flip": ["shiftT"],
        "attend": (["biased"] if l == 0 else []) + ["probs"],
        "weigh": ["weighed"],
        "divide": ["o"],
        "o_flip": ["oT"],
        "mix": ["x_mixed"],
        "route": ["logits", "onehot"] + (["gate_in", "gate_exp"] if l == 1 else []),
        "choose": ["onehotT"] + (["u"] if l == 1 else ["onehotF"]),
        "spread": ["picked"] if l == 1 else ["spread0", "spread1"],
        "inner": [] if l == 0 else ["h0", "h1"][:3 - l],
        "outer": (["f_in"] if l else []) + (["y_res", "y_var", "y_rstd"] if l == 2 else ["x_fed"]),
        "finish": ["x_fed"],
        "tail": ["h0", "h1", "x_fed"],
        "store": [],
    }[kind]
    return [u[0] for u in psum_uses(s)] + more


class Plan:

    def __init__(self, order, slots):
        self.value, self.slot, self.before, self.nth = {}, {}, {}, {}
        count, at, last, steps = {}, {ring: 0 for ring in slots}, {}, {}
        for s in order:
            for stage in stages(s):
                count[stage] = count.get(stage, 0) + 1
                self.value[(stage, *s[1:])] = count[stage]
            for use, ring, reader in psum_uses(s):
                slot = (ring, at[ring] % slots[ring])
                key = (use, *s[1:])
                at[ring] += 1
                self.slot[key] = slot
                self.before[key] = last.get(slot)
                last[slot] = (reader, *s[1:])
            steps[s[0]] = steps.get(s[0], 0) + 1
            self.nth[s] = steps[s[0]] - 1
        self.names = sorted(count)


def build(nc, dram, out):
    turn = turn_order()
    rings = {"one": 3, "two": 2}
    plan = Plan(turn, rings)
    tail = [("stats", 7, b) for b in range(ROWS)] + [("norm", 7, b) for b in range(ROWS)] + \
           [("flip", 7, b) for b in range(ROWS)] + \
           [("tail", 3, b) for b in range(ROWS)]
    tail_plan = Plan(tail, rings)

    with ExitStack() as ctx:
        def sb(name, shape, dt=F32):
            return ctx.enter_context(nc.sbuf_tensor(name, shape, dt))

        def pair(name, shape, dt=F32):
            return [sb(f"{name}_row{b}", shape, dt) for b in range(ROWS)]

        pack = {n: sb(n, [P, w]) for n, w in WIDTH.items()}
        small = sb("small", [16, SMALL_W])

        def W(name):
            n, a, w = WHERE[name]
            return pack[n][:, a:a + w]

        def S16(name, rows):
            a, w = SMALL_COLS[name]
            return small[0:rows, a:a + w]

        identb = sb("identb", [P, P], BF16)
        trib = sb("trib", [P, P], BF16)
        triTb = sb("triTb", [P, P], BF16)
        selb = sb("selb", [E, E * P], BF16)
        pickb = sb("pickb", [16, 2 * P], BF16)
        wq0s = sb("wq0s", [P, P])
        bq0s = sb("bq0s", [P, P])
        sgn = sb("sgn", [P, E])
        wc = {"q": sb("wcq", [P, NT, HD]), "k": sb("wck", [P, NT, HD])}
        ws = {"q": sb("wsq", [P, NT, HD]), "k": sb("wsk", [P, NT, HD])}
        qw2 = sb("qw2s", [P, P])
        kvw2 = sb("kvw2s", [P, 2 * MD])
        rms1 = sb("rms1", [P, 1])
        tg = sb("tg", [P, 8])
        tbo = {0: sb("tbo0", [P, P]), 3: sb("tbo3", [P, P])}
        tgam = sb("tgam", [P, P])
        tbeta = sb("tbeta", [P, P])
        bo2x = sb("bo2x", [P, P])
        wsum = sb("wsum", [P, ROWS * NT])
        neghalf = sb("neghalf", [P, NT * HEADS])

        x = pair("x", [P, NT, P])
        cx = pair("cx", [P, NT, P])
        mrow8 = pair("mrow8", [MD + 1, SEQ], U8)
        bias = pair("bias", [P, NT, SEQ])
        bias_hi = pair("bias_hi", [P, NT, SEQ], BF16)
        biasT = pair("biasT", [P, NT, SEQ])
        ctxT = pair("ctxT", [P, SEQ])
        cst = pair("cst", [P, NT, 6])
        cmv = pair("cmv", [P, NT, 2])
        crms = pair("crms", [P, NT])
        st = pair("st", [P, NT, 6])
        mv = pair("mv", [P, NT, 2])
        rstd = pair("rstd", [P, NT])
        rms = pair("rms", [P, NT])
        xn = pair("xn", [P, NT, P])
        xT = pair("xT", [P, SEQ])
        xb = pair("xb", [P, NT, P])
        qf = pair("qf", [P, NT, P])
        qr = pair("qr", [P, NT, P])
        qt2 = pair("qt2", [P, NT, P])
        qss = pair("qss", [P, NT * HEADS])
        kf = pair("kf", [P, NT, P])
        kr = pair("kr", [P, NT, P])
        kt2 = pair("kt2", [P, NT, P])
        kss = pair("kss", [P, NT * HEADS])
        qs = pair("qs", [P, NT * HEADS, 8, HD], BF16)
        ks = pair("ks", [P, NT * HEADS, 8, HD], BF16)
        qT = pair("qT", [P, 8, SEQ], BF16)
        kT = pair("kT", [P, 8, SEQ], BF16)
        v = pair("v", [P, NT, HEADS, HD + 1])
        nm = pair("nm", [P, NT, 2, 8])
        mp = pair("mp", [P, NT, 2, 2, 8], BF16)
        mT = pair("mT", [32, SEQ], BF16)
        k2 = pair("k2", [P, NT, MD])
        q2 = pair("q2", [P, NT, MQ, MD])
        q2T = pair("q2T", [MD + 2, MQ, SEQ])
        k2T = pair("k2T", [MD + 2, SEQ])
        v2 = pair("v2", [P, NT, MD + 1])
        nm2 = pair("nm2", [P, NT, MQ])
        mT2 = pair("mT2", [8, P])
        probs = [sb(f"probs{i}", [P, 2, 512]) for i in range(4)]
        rec = pair("rec", [P, NT * HEADS])
        o = pair("o", [P, NT, P])
        oT = pair("oT", [P, SEQ])
        lg = pair("lg", [P, NT, E])
        ge = pair("ge", [P, NT, E])
        gm = pair("gm", [P, NT])
        gs = pair("gs", [P, NT])
        gv = pair("gv", [P, NT])
        mx = pair("mx", [P, NT, 8])
        ix = pair("ix", [P, NT, 8], U32)
        ixf = pair("ixf", [P, NT, 8])
        oh = pair("oh", [P, NT, 2, E], BF16)
        ohT = pair("ohT", [16, SEQ], BF16)
        ohF = pair("ohF", [16, SEQ])
        uT = pair("uT", [P, SEQ])
        um = pair("um", [P, 2, SEQ])
        xm = pair("xm", [P, E, SEQ])
        h = [t[:, :, :].rearrange("p (i f) q -> p i f q", i=2) for t in xm]
        msk = [t[:, 0:NT, :].bitcast(I32) for t in xm]
        y = pair("y", [P, NT, P])
        yr = pair("yr", [P, NT, P])

        banks = {("one", i): ctx.enter_context(nc.psum_tensor(f"one{i}", [P, 512], F32)) for i in range(rings["one"])}
        banks |= {("two", i): ctx.enter_context(nc.psum_tensor(f"two{i}", [P, 1024], F32)) for i in range(rings["two"])}
        pv = ctx.enter_context(nc.psum_tensor("pv", [P, 512], F32))

        const_in = ctx.enter_context(nc.semaphore("const_in"))
        setup_act = ctx.enter_context(nc.semaphore("setup_act"))
        setup_pool = ctx.enter_context(nc.semaphore("setup_pool"))
        setup_dve = ctx.enter_context(nc.semaphore("setup_dve"))
        sem = {}
        for name in plan.names:
            sem[name] = ctx.enter_context(nc.semaphore(name))
        for b in range(ROWS):
            for name in ("x_in", "ctx_in", "mask_in", "row_in", "shift_in"):
                sem[name, b] = ctx.enter_context(nc.semaphore(f"{name}{b}"))
        sem["stored"] = ctx.enter_context(nc.semaphore("stored"))
        sem["dve"] = ctx.enter_context(nc.semaphore("dve_done"))
        sem["act"] = ctx.enter_context(nc.semaphore("act_done"))
        sem["pool"] = ctx.enter_context(nc.semaphore("pool_done"))
        nums = [s.num for s in sem.values()]
        all_sems = range(min(nums), max(nums) + 1)

        class Chain:

            def __init__(self, eng, s):
                self.eng, self.s, self.n = eng, s, 0

            def mark(self, ins):
                ins.then_inc(self.s, 1)
                self.n += 1

            def link(self, ins):
                self.mark(ins)
                self.eng.wait_ge(self.s, self.n)

        def shifted(b):
            n, got = 0, {}
            for s in turn:
                if s[0] == "shift" and s[2] == b:
                    n += 16 * (2 if s[1] == 2 else 4)
                    got[s[1]] = n
            return got

        shift_at = [shifted(b) for b in range(ROWS)]

        def x_ready_from(s, p):
            prev = None
            for t in p:
                if t == s:
                    break
                if t[2] == s[2] and t[0] in ("mix", "outer", "finish", "tail"):
                    prev = ("x_mixed" if t[0] == "mix" else "x_fed"), t
            return prev

        with nc.Block() as block:
            @block.sync
            def _(sp):
                for n in WIDTH:
                    sp.dma_start(pack[n][:, :], dram[n]).then_inc(const_in, 16)
                sp.dma_start(small[:, :], dram["small"]).then_inc(const_in, 16)

            n_consts = 16 * (len(WIDTH) + 1)

            @block.scalar
            def _(act):
                act.wait_ge(const_in, n_consts)
                act.activation(tg[:, :], W("g"), ACT.Tanh).then_inc(setup_act, 1)
                act.activation(sgn[:, :], W("sig"), ACT.Sign).then_inc(setup_act, 1)
                act.activation(wq0s[:, :], W("wq0"), ACT.Copy, scale=HD ** -0.5)
                act.activation(bq0s[:, :], W("bq0"), ACT.Copy, scale=HD ** -0.5)
                act.activation(bo2x[:, :], W("bo_f1"), ACT.Copy, scale=2.0)
                act.activation(selb[:, :], S16("sel", E), ACT.Copy)
                act.activation(pickb[:, 0:P], S16("pick1", 16), ACT.Copy)
                act.activation(pickb[:, P:2 * P], S16("pick2", 16), ACT.Copy)
                act.activation(rms1[:, :], W("rms"), ACT.Copy, bias=1.0).then_inc(setup_act, 1)

            @block.gpsimd
            def _(pool):
                pool.memset(neghalf[:, :], -0.5)
                for b in range(ROWS):
                    pool.memset(v[b][:, :, :, HD:HD + 1], 1.0)
                    pool.memset(v2[b][:, :, MD:MD + 1], 1.0)
                    pool.memset(qs[b][:, :, TERMS:8, :], 0.0)
                    pool.memset(ks[b][:, :, TERMS:8, :], 0.0).then_inc(setup_pool, 1)
                    pool.wait_ge(setup_pool, b + 1)
                    pool.memset(ks[b][:, :, TERMS, 0:2], 1.0)

            @block.vector
            def _(dve):
                for b in range(ROWS):
                    nc.vector.memset(q2T[b][MD:MD + 2, :, :], 1.0)
                    nc.vector.memset(k2T[b][MD:MD + 2, :], 1.0)
                dve.wait_ge(const_in, n_consts)
                nc.vector.tensor_copy(identb[:, :], W("ident"))
                nc.vector.tensor_copy(trib[:, :], W("tri"))
                nc.vector.tensor_copy(triTb[:, :], W("triT"))
                for n in "qk":
                    c = W("cos1").rearrange("p (t d) -> p t d", t=NT)
                    sn = W("sin1").rearrange("p (t d) -> p t d", t=NT)
                    w = W(f"{n}nw")
                    H2 = HD // 2
                    nc.vector.tensor_tensor(wc[n][:, :, :], c, w[:, None, :].to_broadcast([P, NT, HD]), ALU.mult)
                    nc.vector.scalar_tensor_tensor(out=ws[n][:, :, 0:H2], in0=sn[:, :, 0:H2], scalar=-1.0,
                                                   in1=w[:, None, H2:HD].to_broadcast([P, NT, H2]),
                                                   op0=ALU.mult, op1=ALU.mult)
                    nc.vector.tensor_tensor(ws[n][:, :, H2:HD], sn[:, :, H2:HD],
                                            w[:, None, 0:H2].to_broadcast([P, NT, H2]), ALU.mult)
                ew = W("ew").rearrange("p (n k) -> p n k", k=2)
                nc.vector.tensor_tensor(wsum[:, :], ew[:, :, 0], ew[:, :, 1], ALU.add).then_inc(setup_dve, 1)
                dve.wait_ge(setup_act, 3)
                dve.wait_ge(setup_dve, 1)
                nc.vector.tensor_scalar(wsum[:, :], wsum[:, :], tg[:, 7:8], None, ALU.mult)
                nc.vector.tensor_scalar(tbo[0][:, :], W("bo0"), tg[:, 0:1], None, ALU.mult)
                nc.vector.tensor_scalar(tbo[3][:, :], W("bo3"), tg[:, 3:4], None, ALU.mult)
                nc.vector.tensor_scalar(tgam[:, :], W("gamma"), tg[:, 6:7], None, ALU.mult)
                nc.vector.tensor_scalar(tbeta[:, :], W("beta"), tg[:, 6:7], None, ALU.mult)
                nc.vector.tensor_scalar(qw2[:, :], W("qw2"), rms1[:, 0:1], None, ALU.mult)
                nc.vector.tensor_scalar(kvw2[:, :], W("kvw2"), rms1[:, 0:1], None, ALU.mult)

        def programs(block, order, plan, first_row, in_loop):
            def at(stage, s):
                return plan.value[(stage, *s[1:])]

            def bank(use, s):
                return banks[plan.slot[(use, *s[1:])]]

            def claim(pe, use, s):
                before = plan.before[(use, *s[1:])]
                if before:
                    pe.wait_ge(sem[before[0]], plan.value[before])

            def prev_on(kind, s, back):
                same = [t for t in order if t[0] == kind]
                i = same.index(s) - back
                return same[i] if i >= 0 else None

            def heads(t):
                return t[:, :, :].rearrange("p t (h d) -> p (t h) d", d=HD)

            def rope_products(ch, n, f, r, t2, ss):
                H2 = HD // 2
                V = nc.vector
                f4, r4, t4 = (t[:, :, :].rearrange("p t (h d) -> p t h d", d=HD) for t in (f, r, t2))
                ch.link(V.tensor_tensor(heads(r), heads(f), heads(f), ALU.mult))
                ch.link(V.tensor_reduce(ss[:, :], heads(r), AX.X, ALU.add))
                V.tensor_scalar(ss[:, :], ss[:, :], 1.0 / HD, 1e-10, ALU.mult, ALU.add).then_inc(sem[f"{n}_var"], 1)
                ch.mark(V.tensor_tensor(r4, f4, wc[n][:, :, None, :].to_broadcast([P, NT, HEADS, HD]), ALU.mult))
                ch.mark(V.tensor_tensor(t4[:, :, :, 0:H2], f4[:, :, :, H2:HD], ws[n][:, :, None, 0:H2].to_broadcast([P, NT, HEADS, H2]), ALU.mult))
                ch.link(V.tensor_tensor(t4[:, :, :, H2:HD], f4[:, :, :, 0:H2], ws[n][:, :, None, H2:HD].to_broadcast([P, NT, HEADS, H2]), ALU.mult))
                V.tensor_tensor(r[:, :, :], r[:, :, :], t2[:, :, :], ALU.add).then_inc(sem[f"{n}_prod"], 1)

            def parts(src, stack, lo, hi):
                return nc.scalar.activation(stack[:, :, lo:hi, :], heads(src)[:, :, None, :].to_broadcast([P, NT * HEADS, hi - lo, HD]), ACT.Copy)

            def stack_transposes(pe, ps, src, g):
                dst = ps[:, :].bitcast(BF16)
                for jj in range(4):
                    for t in range(NT):
                        hh = t * HEADS + 2 * (4 * g + jj)
                        ins = pe.transpose(dst[:, jj * SEQ + t * P:jj * SEQ + (t + 1) * P],
                                           src[:, hh:hh + 2, :, :].rearrange("p h g d -> p (h g d)"), identb[:, :])
                return ins

            def prev_flip(n, s):
                before = [t for t in order[:order.index(s)] if t[0] == f"{n}_flip" and t[2] == s[2] and t[1] != 2]
                return before[-1] if before else None

            def half_turn(dve, ch, f, tmp, dst, cname, sname, nh):
                c = W(cname).rearrange("p (t d) -> p t d", t=NT)
                sn = W(sname).rearrange("p (t d) -> p t d", t=NT)
                H2 = MD // 2
                V = nc.vector
                shape = [P, NT, nh, H2]
                ch.mark(V.tensor_tensor(dst, f, c[:, :, None, :].to_broadcast([P, NT, nh, MD]), ALU.mult))
                ch.mark(V.tensor_tensor(tmp[:, :, :, 0:H2], f[:, :, :, H2:MD], sn[:, :, None, 0:H2].to_broadcast(shape), ALU.mult))
                ch.link(V.tensor_tensor(tmp[:, :, :, H2:MD], f[:, :, :, 0:H2], sn[:, :, None, H2:MD].to_broadcast(shape), ALU.mult))
                return V.tensor_tensor(dst, dst, tmp, ALU.add)

            @block.sync
            def _(sp):
                for s in order:
                    kind, l, b = s[:3]
                    if kind == "load":
                        row = first_row + b
                        sp.dma_start(cx[b][:, :, :], dram["ctx"][bass.ds(row, 1)].rearrange("o (t p) d -> p (o t) d", p=P)).then_inc(sem["ctx_in", b], 16)
                        sp.dma_start(msk[b][:, :, :], dram["mask"][bass.ds(row, 1)].rearrange("o (t p) k -> p (o t) k", p=P)).then_inc(sem["mask_in", b], 16)
                        sp.dma_start(x[b][:, :, :], dram["x"][bass.ds(row, 1)].rearrange("o (t p) d -> p (o t) d", p=P)).then_inc(sem["x_in", b], 16)
                        sp.dma_start(mrow8[b][MD:MD + 1, :], dram["mrow"][bass.ds(row, 1)]).then_inc(sem["row_in", b], 16)
                    if kind == "shift_flip":
                        sp.wait_ge(sem["shiftT"], at("shiftT", s))
                        if l == 2:
                            for t in range(NT):
                                sp.dma_start(q2T[b][MD + 1:MD + 2, :, t * P:(t + 1) * P], mT2[b][MQ * t:MQ * t + MQ, :]).then_inc(sem["shift_in", b], 16)
                        else:
                            for r in range(2):
                                for part in range(2):
                                    row = STK * r + KD + part
                                    n = 16 * r + 8 * part
                                    sp.dma_start(qT[b][row:row + 1, :, :], mT[b][n:n + 8, :]).then_inc(sem["shift_in", b], 16)
                    if kind == "store" or kind == "tail":
                        last = ("x_fed", s) if kind == "tail" else x_ready_from(s, order)
                        if last:
                            sp.wait_ge(sem[last[0]], at(*last))
                        row = first_row + b
                        dst = out[bass.ds(row, 1)] if in_loop else out[row:row + 1]
                        sp.dma_start(dst.rearrange("o (t p) d -> p (o t) d", p=P), x[b][:, :, :]).then_inc(sem["stored"], 16)
                sp.wait_ge(sem["stored"], 16 * ROWS)

            @block.gpsimd
            def _(pool):
                ch = Chain(pool, sem["pool"])

                def power(t, n):
                    return pool.tensor_tensor(t, t, neghalf[:, 0:n], ALU.pow)

                for s in order:
                    kind, l, b = s[:3]
                    if kind == "bias":
                        pool.wait_ge(sem["mask_in", b], 16)
                        ch.link(pool.tensor_scalar(bias[b][:, :, :], msk[b][:, :, :], 0.0, NEG, ALU.is_equal, ALU.mult))
                        adj = W("adj").rearrange("p (t k) -> p t k", t=NT)
                        pool.tensor_tensor(bias[b][:, :, :], bias[b][:, :, :], adj, ALU.add).then_inc(sem["bias"], 1)
                        pool.wait_ge(sem["bias"], at("bias", s))
                        pool.tensor_copy(bias_hi[b][:, :, :], bias[b][:, :, :]).then_inc(sem["bias_hi"], 1)
                    if kind == "load":
                        pool.wait_ge(sem["ctx_var"], at("ctx_var", s))
                        power(crms[b][:, :], NT).then_inc(sem["ctx_rms"], 1)
                    if kind == "kv" and l == 1:
                        pool.wait_ge(sem["k_var"], at("k_var", s))
                        power(kss[b][:, :], NT * HEADS).then_inc(sem["k_rms"], 1)
                    if kind == "stats":
                        pool.wait_ge(sem["var"], at("var", s))
                        power(rstd[b][:, :], NT).then_inc(sem["rstd"], 1)
                        if l == 2:
                            pool.wait_ge(sem["rstd"], at("rstd", s))
                            ch.link(pool.tensor_tensor(rms[b][:, :], rstd[b][:, :], rstd[b][:, :], ALU.mult))
                            ch.link(pool.tensor_tensor(rms[b][:, :], rms[b][:, :], mv[b][:, :, 1], ALU.mult))
                            ch.link(pool.tensor_scalar(rms[b][:, :], rms[b][:, :], 1e-6, 0.0, ALU.add, ALU.add))
                            ch.link(power(rms[b][:, :], NT))
                            pool.tensor_tensor(rstd[b][:, :], rms[b][:, :], rstd[b][:, :], ALU.mult).then_inc(sem["rms"], 1)
                        add = {0: tbo[0], 3: tbo[3], 6: tbeta}.get(l)
                        src = add if add is not None else tbeta
                        pool.tensor_tensor(xb[b][:, :, :], x[b][:, :, :], src[:, None, :].to_broadcast([P, NT, P]), ALU.add).then_inc(sem["x_bias"], 1)
                    if kind == "query" and l == 1:
                        pool.wait_ge(sem["q_var"], at("q_var", s))
                        power(qss[b][:, :], NT * HEADS).then_inc(sem["q_rms"], 1)
                    if kind == "outer" and l == 2:
                        pool.wait_ge(sem["x_normed"], at("x_normed", ("norm", 6, b)))
                        pool.tensor_tensor(yr[b][:, :, :], xn[b][:, :, :], W("bo_f2")[:, None, :].to_broadcast([P, NT, P]), ALU.add).then_inc(sem["y_res"], 1)
                        pool.wait_ge(sem["y_var"], at("y_var", s))
                        power(rstd[b][:, :], NT).then_inc(sem["y_rstd"], 1)

            @block.scalar
            def _(act):
                for s in order:
                    kind, l, b = s[:3]

                    def evac(dst, use, cols, stage, **kw):
                        act.wait_ge(sem[use], at(use, s))
                        act.activation(dst, cols, ACT.Copy, **kw).then_inc(sem[stage], 1)

                    if kind == "load":
                        evac(ctxT[b][:, :], "ctxT_ps", bank("ctxT_ps", s)[:, 0:SEQ], "ctxT")
                    if kind == "bias":
                        evac(biasT[b][:, :, :], "biasT_ps", bank("biasT_ps", s)[:, :].rearrange("p (t q) -> p t q", t=NT), "biasT")
                    for n, stack, f, r in (("k", ks, kf, kr), ("q", qs, qf, qr)):
                        (h0, h1), (m0, m1) = ((3, 6), (0, 2)) if n == "k" else ((1, 4), (0, 5))
                        if (kind == ("kv" if n == "k" else "query") and l in (0, 3)) or kind == f"{n}_turn":
                            ready = f"{n}_ready" if l == 1 else f"{n}_in"
                            act.wait_ge(sem[ready], at(ready, s))
                            before = prev_flip(n, s)
                            if before:
                                act.wait_ge(sem[f"{n}T1_ps"], at(f"{n}T1_ps", before))
                            parts(f[b], stack[b], h0, h1).then_inc(sem[f"{n}_hi"], 1)
                        if kind == f"{n}_mid":
                            act.wait_ge(sem[f"{n}_rest"], at(f"{n}_rest", s))
                            if n == "q":
                                act.activation(stack[b][:, :, 0:5:4, :], heads(r[b])[:, :, None, :].to_broadcast([P, NT * HEADS, 2, HD]), ACT.Copy)\
                                   .then_inc(sem["q_mid"], 1)
                            else:
                                parts(r[b], stack[b], m0, m1).then_inc(sem["k_mid"], 1)
                    if kind == "k_flip" and l != 2:
                        for g in range(2):
                            src = bank(f"kT{g}_ps", s)[:, :].bitcast(BF16).rearrange("p (j k) -> p j k", j=4)
                            evac(kT[b][:, 4 * g:4 * g + 4, :], f"kT{g}_ps", src, f"kT{g}")
                    if kind == "k_flip" and l == 2:
                        evac(k2T[b][0:MD, :], "kT2_ps", bank("kT2_ps", s)[0:MD, 0:SEQ], "kT0")
                    if kind == "flip":
                        evac(xT[b][:, :], "xT_ps", bank("xT_ps", s)[:, 0:SEQ], "xT")
                    if kind == "q_flip" and l != 2:
                        for g in range(2):
                            src = bank(f"qT{g}_ps", s)[:, :].bitcast(BF16).rearrange("p (j k) -> p j k", j=4)
                            evac(qT[b][:, 4 * g:4 * g + 4, :], f"qT{g}_ps", src, f"qT{g}")
                    if kind == "q_flip" and l == 2:
                        src = bank("qT2_ps", s)[0:MD, :].rearrange("p (h q) -> p h q", h=MQ)
                        act.wait_ge(sem["qT2_ps"], at("qT2_ps", s))
                        act.activation(q2T[b][0:MD, 0:2, :], src[:, 0:2, :], ACT.Copy).then_inc(sem["qT0"], 1)
                        act.activation(q2T[b][0:MD, 2:4, :], src[:, 2:4, :], ACT.Copy).then_inc(sem["qT1"], 1)
                    if kind == "shift_flip":
                        if l == 2:
                            evac(mT2[b][:, :], "shift_ps", bank("shift_ps", s)[0:8, 0:P], "shiftT")
                        else:
                            evac(mT[b][:, :], "shift_ps", bank("shift_ps", s)[0:32, 0:P].bitcast(BF16), "shiftT")
                    if kind == "attend":
                        n = plan.nth[s]
                        before = prev_on("attend", s, 4)
                        if before:
                            act.wait_ge(sem["weighed"], at("weighed", before))
                        dst = probs[n % 4]
                        if l == 0:
                            act.wait_ge(sem["biased"], at("biased", s))
                            act.activation(dst[:, :, :], dst[:, :, :], ACT.Exp).then_inc(sem["probs"], 1)
                        else:
                            act.wait_ge(sem["scores_ps"], at("scores_ps", s))
                            w = 384 if l == 1 else 512
                            src = bank("scores_ps", s)[:, :].rearrange("p (r n) -> p r n", r=2)
                            act.activation(dst[:, :, 0:w], src[:, :, 0:w], ACT.Exp,
                                           scale=1.0 if l == 2 else HD ** -0.5).then_inc(sem["probs"], 1)
                    if kind == "o_flip":
                        evac(oT[b][:, :], "oT_ps", bank("oT_ps", s)[:, 0:SEQ], "oT")
                    if kind == "route" and l == 1:
                        act.wait_ge(sem["gate_in"], at("gate_in", s))
                        act.activation(ge[b][:, :, :], lg[b][:, :, :], ACT.Exp).then_inc(sem["gate_exp"], 1)
                    if kind == "choose":
                        rows = 16 if l == 1 else 8
                        src = bank("onehotT_ps", s)[0:rows, 0:P].bitcast(BF16)
                        evac(ohT[b][0:rows, :], "onehotT_ps", src, "onehotT")
                        if l == 1:
                            evac(uT[b][:, :], "u_ps", bank("u_ps", s)[:, 0:SEQ], "u")
                        else:
                            act.wait_ge(sem["onehotT"], at("onehotT", s))
                            act.activation(ohF[b][0:rows, :], ohT[b][0:rows, :], ACT.Copy).then_inc(sem["onehotF"], 1)
                    if kind == "inner" and l == 1:
                        for i in range(2):
                            act.wait_ge(sem[f"h{i}_ps"], at(f"h{i}_ps", s))
                            for ft in range(FT):
                                ins = act.activation(h[b][:, i, ft, :], bank(f"h{i}_ps", s)[:, ft * SEQ:(ft + 1) * SEQ],
                                                     ACT.Relu, bias=W("bi")[:, ft:ft + 1])
                            ins.then_inc(sem[f"h{i}"], 1)
                    if kind == "inner" and l == 2:
                        act.wait_ge(sem["h0_ps"], at("h0_ps", s))
                        act.activation(h[b][:, 0, :, :], bank("h0_ps", s)[:, :].rearrange("p (f q) -> p f q", f=FT), ACT.Gelu).then_inc(sem["h0"], 1)
                    if kind == "tail":
                        for i in range(2):
                            act.wait_ge(sem[f"h{i}_ps"], at(f"h{i}_ps", s))
                            act.activation(h[b][:, i, :, :], bank(f"h{i}_ps", s)[:, :].rearrange("p (f q) -> p f q", f=FT), ACT.Gelu_apprx_tanh).then_inc(sem[f"h{i}"], 1)

            @block.tensor
            def _(pe):
                ident = W("ident")

                def mm(dst, lhsT, rhs, start=True, stop=True, **kw):
                    return pe.matmul(dst, lhsT, rhs, start=start, stop=stop, **kw)

                for s in order:
                    kind, l, b = s[:3]
                    if kind == "load":
                        pe.wait_ge(sem["ctx_in", b], 16)
                        claim(pe, "ctxT_ps", s)
                        for t in range(NT):
                            ins = pe.transpose(bank("ctxT_ps", s)[:, t * P:(t + 1) * P], cx[b][:, t, :], ident)
                        ins.then_inc(sem["ctxT_ps"], 1)
                    if kind == "bias":
                        pe.wait_ge(sem["bias"], at("bias", s))
                        claim(pe, "biasT_ps", s)
                        for k in range(NT):
                            for q in range(NT):
                                ins = pe.transpose(bank("biasT_ps", s)[:, k * SEQ + q * P:k * SEQ + (q + 1) * P],
                                                   bias[b][:, q, k * P:(k + 1) * P], ident)
                        ins.then_inc(sem["biasT_ps"], 1)
                    if kind == "kv":
                        load = ("load", 0, b)
                        pe.wait_ge(sem["ctxT"], at("ctxT", load))
                        claim(pe, "kv_ps", s)
                        ps = bank("kv_ps", s)
                        for t in range(NT):
                            c = ctxT[b][:, t * P:(t + 1) * P]
                            if l == 2:
                                ins = mm(ps[:, t * 2 * MD:(t + 1) * 2 * MD], c, kvw2[:, :])
                            else:
                                mm(ps[:, t * P:(t + 1) * P], c, W(f"wk{l}"))
                                ins = mm(ps[:, SEQ + t * P:SEQ + (t + 1) * P], c, W(f"wv{l}"))
                        ins.then_inc(sem["kv_ps"], 1)
                    if kind == "k_flip":
                        if l == 2:
                            pe.wait_ge(sem["k_rot"], at("k_rot", s))
                            claim(pe, "kT2_ps", s)
                            for t in range(NT):
                                ins = pe.transpose(bank("kT2_ps", s)[0:MD, t * P:(t + 1) * P], k2[b][:, t, :], ident)
                            ins.then_inc(sem["kT2_ps"], 1)
                        else:
                            pe.wait_ge(sem["k_stack"], at("k_stack", s))
                            for g in range(2):
                                claim(pe, f"kT{g}_ps", s)
                                stack_transposes(pe, bank(f"kT{g}_ps", s), ks[b], g).then_inc(sem[f"kT{g}_ps"], 1)
                    if kind == "flip":
                        pe.wait_ge(sem["x_normed"], at("x_normed", s))
                        claim(pe, "xT_ps", s)
                        for t in range(NT):
                            ins = pe.transpose(bank("xT_ps", s)[:, t * P:(t + 1) * P], xn[b][:, t, :], ident)
                        ins.then_inc(sem["xT_ps"], 1)
                    if kind == "query":
                        normed = ("norm", l, b)
                        pe.wait_ge(sem["xT"], at("xT", normed))
                        claim(pe, "q_ps", s)
                        wq = {0: wq0s[:, :], 1: W("wq1"), 2: qw2[:, :], 3: W("wq3")}[l]
                        for t in range(NT):
                            ins = mm(bank("q_ps", s)[:, t * P:(t + 1) * P], xT[b][:, t * P:(t + 1) * P], wq)
                        ins.then_inc(sem["q_ps"], 1)
                    if kind == "q_flip":
                        pe.wait_ge(sem["q_stack"], at("q_stack", s))
                        if l == 2:
                            claim(pe, "qT2_ps", s)
                            for hh in range(MQ):
                                for t in range(NT):
                                    ins = pe.transpose(bank("qT2_ps", s)[0:MD, hh * SEQ + t * P:hh * SEQ + (t + 1) * P],
                                                       q2[b][:, t, hh, :], ident)
                            ins.then_inc(sem["qT2_ps"], 1)
                        else:
                            for g in range(2):
                                claim(pe, f"qT{g}_ps", s)
                                stack_transposes(pe, bank(f"qT{g}_ps", s), qs[b], g).then_inc(sem[f"qT{g}_ps"], 1)
                    if kind == "max":
                        part = s[3]
                        if part == 0:
                            q, k = ("query", l, b), ("kv", l, b)
                            pe.wait_ge(sem["qT1"], at("qT1", q))
                            if l == 2:
                                pe.wait_ge(sem["kT0"], at("kT0", k))
                                pe.wait_ge(sem["mask_row"], at("mask_row", ("load", 0, b)))
                            else:
                                pe.wait_ge(sem["kT1"], at("kT1", k))
                            if l == 0:
                                pe.wait_ge(sem["bias_hi"], at("bias_hi", ("load", 0, b)))
                        for i in range(2):
                            claim(pe, f"max{i}_ps", s)
                            ps = bank(f"max{i}_ps", s)
                            if l == 2:
                                t = part
                                for hh in range(2):
                                    ins = mm(ps[:, hh * SEQ:(hh + 1) * SEQ], q2T[b][0:MD + 1, 2 * i + hh, t * P:(t + 1) * P],
                                             k2T[b][0:MD + 1, :])
                                ins.then_inc(sem[f"max{i}_ps"], 1)
                                continue
                            t, jp, r = part // 4, part % 4, i
                            rows = slice(STK * r, STK * r + KD)
                            ps2 = ps[:, :].rearrange("p (h k) -> p h k", h=2)
                            kn = P if l == 1 and t == 0 else SEQ
                            if l == 0:
                                mm(ps2, identb[:, :], bias_hi[b][:, t, None, :].to_broadcast([P, 2, SEQ]), skip_group_check=True)
                            for hh in range(2):
                                j = 2 * jp + hh
                                ins = mm(ps2[:, hh, 0:kn], qT[b][rows, j, t * P:(t + 1) * P], kT[b][rows, j, 0:kn],
                                         start=(l == 3 or (l == 1 and hh == 0)), skip_group_check=True)
                            if l == 1:
                                ins = mm(ps2[:, :, t * P:(t + 1) * P], identb[:, :],
                                         trib[:, None, :].to_broadcast([P, 2, P]), start=False, skip_group_check=True)
                            ins.then_inc(sem[f"max{i}_ps"], 1)
                    if kind == "shift_flip":
                        pe.wait_ge(sem["shift"], at("shift", s))
                        claim(pe, "shift_ps", s)
                        if l == 2:
                            ins = pe.transpose(bank("shift_ps", s)[0:8, 0:P], nm2[b][:, :, :].rearrange("p t h -> p (t h)"), ident)
                        else:
                            ps = bank("shift_ps", s)[:, 0:P].bitcast(BF16)
                            for t in range(NT):
                                ins = pe.transpose(ps[0:32, t * P:(t + 1) * P], mp[b][:, t, :, :, :].rearrange("p r m j -> p (r m j)"), identb[:, :])
                        ins.then_inc(sem["shift_ps"], 1)
                    if kind == "attend":
                        part = s[3]
                        if part == 0:
                            pe.wait_ge(sem["shift_in", b], shift_at[b][l])
                        claim(pe, "scores_ps", s)
                        ps = bank("scores_ps", s)
                        for r in range(2):
                            for k in range(NT):
                                if l == 2:
                                    ins = mm(ps[:, r * 512 + k * SEQ:r * 512 + (k + 1) * SEQ], k2T[b][:, k * P:(k + 1) * P],
                                             q2T[b][:, 2 * part + r, :])
                                    continue
                                rows = slice(STK * r, STK * r + KD + 2)
                                q0 = P if l == 1 and k == 1 else 0
                                ins = mm(ps[:, r * 512 + k * SEQ:r * 512 + k * SEQ + SEQ - q0],
                                         kT[b][rows, part, k * P:(k + 1) * P], qT[b][rows, part, q0:SEQ],
                                         start=(l != 1 or k == 0), skip_group_check=True)
                            if l == 1:
                                diag = ps[:, r * 512:(r + 1) * 512].rearrange("p (k q) -> p k q", k=2)[:, :, 0:P]
                                ins = mm(diag, identb[:, :], triTb[:, None, :].to_broadcast([P, 2, P]),
                                         start=False, skip_group_check=True)
                        ins.then_inc(sem["scores_ps"], 1)
                    if kind == "weigh":
                        part = s[3]
                        if part == 0:
                            pe.wait_ge(sem["v"], at("v", ("kv", l, b)))
                            mixed = [t for t in order[:order.index(s)] if t[0] == "divide"]
                            if mixed:
                                pe.wait_ge(sem["o"], at("o", mixed[-1]))
                        pe.wait_ge(sem["probs"], at("probs", s))
                        pr = probs[plan.nth[("attend", *s[1:])] % 4]
                        for r in range(2):
                            hh = 2 * part + r
                            for t in range(NT):
                                ks_ = [0] if l == 1 and t == 0 else [0, 1]
                                for k in ks_:
                                    c = k * SEQ + t * P - (P if l == 1 and k == 1 else 0)
                                    if l == 2:
                                        dst = pv[:, (t * MQ + hh) * (MD + 1):(t * MQ + hh + 1) * (MD + 1)]
                                        w = v2[b][:, k, :]
                                    else:
                                        dst = pv[:, (t * HEADS + hh) * (HD + 1):(t * HEADS + hh + 1) * (HD + 1)]
                                        w = v[b][:, k, hh, :]
                                    ins = mm(dst, pr[:, r, c:c + P], w, start=(k == 0), stop=(k == ks_[-1]))
                        ins.then_inc(sem["weighed"], 1)
                    if kind == "o_flip":
                        pe.wait_ge(sem["o"], at("o", s))
                        claim(pe, "oT_ps", s)
                        for t in range(NT):
                            ins = pe.transpose(bank("oT_ps", s)[:, t * P:(t + 1) * P], o[b][:, t, :], ident)
                        ins.then_inc(sem["oT_ps"], 1)
                    if kind == "mix":
                        pe.wait_ge(sem["oT"], at("oT", s))
                        claim(pe, "y_ps", s)
                        for t in range(NT):
                            ins = mm(bank("y_ps", s)[:, t * P:(t + 1) * P], oT[b][:, t * P:(t + 1) * P], W("ow2" if l == 2 else f"wo{l}"))
                        ins.then_inc(sem["y_ps"], 1)
                    if kind == "route":
                        pe.wait_ge(sem["xT"], at("xT", ("norm", 4 + l, b)))
                        claim(pe, "logits_ps", s)
                        for t in range(NT):
                            w = {0: sgn[:, :], 1: W("gate"), 2: W("wr")}[l]
                            ins = mm(bank("logits_ps", s)[:, t * E:(t + 1) * E], xT[b][:, t * P:(t + 1) * P], w)
                        ins.then_inc(sem["logits_ps"], 1)
                    if kind == "choose":
                        n = 16 if l == 1 else 8
                        pe.wait_ge(sem["onehot"], at("onehot", s))
                        claim(pe, "onehotT_ps", s)
                        ps = bank("onehotT_ps", s)[:, 0:P].bitcast(BF16)
                        for t in range(NT):
                            ins = pe.transpose(ps[0:n, t * P:(t + 1) * P], oh[b][:, t, :, :].rearrange("p s e -> p (s e)")[:, 0:n], identb[:, :])
                        ins.then_inc(sem["onehotT_ps"], 1)
                        if l == 1:
                            claim(pe, "u_ps", s)
                            mm(bank("u_ps", s)[:, 0:SEQ], W("loraA"), xT[b][:, :]).then_inc(sem["u_ps"], 1)
                    if kind == "spread":
                        if l == 1:
                            pe.wait_ge(sem["onehotT"], at("onehotT", s))
                            claim(pe, "pick_ps", s)
                            for i in range(2):
                                ins = mm(bank("pick_ps", s)[:, i * SEQ:(i + 1) * SEQ], pickb[:, i * P:(i + 1) * P], ohT[b][:, :])
                            ins.then_inc(sem["pick_ps"], 1)
                        else:
                            pe.wait_ge(sem["onehotT"], at("onehotT", s))
                            for i in range(2):
                                claim(pe, f"spread{i}_ps", s)
                                for e in range(4):
                                    ins = mm(bank(f"spread{i}_ps", s)[:, e * SEQ:(e + 1) * SEQ],
                                             selb[:, (4 * i + e) * P:(4 * i + e + 1) * P], ohT[b][0:E, :])
                                ins.then_inc(sem[f"spread{i}_ps"], 1)
                    r = ("spread", l, b)
                    if kind == "inner":
                        if l == 1:
                            for i in range(2):
                                if i == 0:
                                    pe.wait_ge(sem["picked"], at("picked", r))
                                claim(pe, f"h{i}_ps", s)
                                for ft in range(FT):
                                    dst = bank(f"h{i}_ps", s)[:, ft * SEQ:(ft + 1) * SEQ]
                                    mm(dst, W("wi")[:, ft * P:(ft + 1) * P], xT[b][:, :], stop=False)
                                    ins = mm(dst, W("loraB")[:, ft * P:(ft + 1) * P], um[b][:, i, :], start=False)
                                ins.then_inc(sem[f"h{i}_ps"], 1)
                        if l == 2:
                            pe.wait_ge(sem["spread1"], at("spread1", r))
                            pe.wait_ge(sem["onehotF"], at("onehotF", r))
                            claim(pe, "h0_ps", s)
                            for ft in range(FT):
                                dst = bank("h0_ps", s)[:, ft * SEQ:(ft + 1) * SEQ]
                                mm(dst, S16("b1_f2", E)[:, ft * P:(ft + 1) * P], ohF[b][0:E, :], stop=False)
                                for e in range(E):
                                    ins = mm(dst, W("w1_f2")[:, e * FF + ft * P:e * FF + (ft + 1) * P], xm[b][:, e, :], start=False, stop=(e == E - 1))
                            ins.then_inc(sem["h0_ps"], 1)
                    if kind == "outer":
                        if l == 0:
                            pe.wait_ge(sem["spread1"], at("spread1", r))
                            pe.wait_ge(sem["onehotF"], at("onehotF", r))
                            claim(pe, "f_ps", s)
                            for t in range(NT):
                                dst = bank("f_ps", s)[:, t * P:(t + 1) * P]
                                mm(dst, ohF[b][0:E, t * P:(t + 1) * P], S16("bf0", E), stop=False)
                                for e in range(E):
                                    ins = mm(dst, xm[b][:, e, t * P:(t + 1) * P], W("wf0")[:, e * P:(e + 1) * P], start=False, stop=(e == E - 1))
                            ins.then_inc(sem["f_ps"], 1)
                        if l > 0:
                            claim(pe, "f_ps", s)
                            for i in range(3 - l):
                                pe.wait_ge(sem[f"h{i}"], at(f"h{i}", s))
                            for t in range(NT):
                                for i in range(3 - l):
                                    for ft in range(FT):
                                        w = W(f"wo_f{l}")[:, ft * P:(ft + 1) * P]
                                        ins = mm(bank("f_ps", s)[:, t * P:(t + 1) * P], h[b][:, i, ft, t * P:(t + 1) * P], w,
                                                 start=(i == 0 and ft == 0), stop=(i == 2 - l and ft == FT - 1))
                            ins.then_inc(sem["f_ps"], 1)
                    if kind == "tail":
                        pe.wait_ge(sem["xT"], at("xT", ("flip", 7, b)))
                        for i in range(2):
                            claim(pe, f"h{i}_ps", s)
                            for ft in range(FT):
                                n = FT * i + ft
                                ins = mm(bank(f"h{i}_ps", s)[:, ft * SEQ:(ft + 1) * SEQ], W("w1_f3")[:, n * P:(n + 1) * P], xT[b][:, :])
                            ins.then_inc(sem[f"h{i}_ps"], 1)
                        claim(pe, "f_ps", s)
                        for i in range(2):
                            pe.wait_ge(sem[f"h{i}"], at(f"h{i}", s))
                        for t in range(NT):
                            for n in range(FT3):
                                ins = mm(bank("f_ps", s)[:, t * P:(t + 1) * P], h[b][:, n // FT, n % FT, t * P:(t + 1) * P],
                                         W("w2_f3")[:, n * P:(n + 1) * P], start=(n == 0), stop=(n == FT3 - 1))
                        ins.then_inc(sem["f_ps"], 1)

            @block.vector
            def _(dve):
                ch = Chain(dve, sem["dve"])
                V = nc.vector

                def half(ap):
                    return ap.rearrange("p (t d) -> p t d", t=NT)

                def layer_stats(src, b, m, sums):
                    for t in range(NT):
                        ch.link(V.bn_stats(sums[b][:, t, :], src[:, t, :]))
                    for t in range(NT):
                        ch.link(V.bn_aggr(m[b][:, t, :], sums[b][:, t, :]))

                for s in order:
                    kind, l, b = s[:3]
                    if kind == "load":
                        dve.wait_ge(sem["ctx_in", b], 16)
                        layer_stats(cx[b], b, cmv, cst)
                        ch.link(V.tensor_tensor(crms[b][:, :], cmv[b][:, :, 0], cmv[b][:, :, 0], ALU.mult))
                        ch.link(V.tensor_tensor(crms[b][:, :], crms[b][:, :], cmv[b][:, :, 1], ALU.add))
                        V.tensor_scalar(crms[b][:, :], crms[b][:, :], 1e-6, None, ALU.add).then_inc(sem["ctx_var"], 1)
                        dve.wait_ge(sem["row_in", b], 16)
                        V.tensor_scalar(k2T[b][MD:MD + 1, :], mrow8[b][MD:MD + 1, :], 0.0, FILL, ALU.is_equal, ALU.mult).then_inc(sem["mask_row"], 1)
                    if kind == "kv":
                        dve.wait_ge(sem["kv_ps"], at("kv_ps", s))
                        ps = bank("kv_ps", s)
                        if l == 2:
                            dve.wait_ge(sem["ctx_rms"], at("ctx_rms", ("load", 0, b)))
                            for t in range(NT):
                                V.tensor_scalar(v2[b][:, t, 0:MD], ps[:, t * 2 * MD + MD:(t + 1) * 2 * MD], crms[b][:, t:t + 1], None, ALU.mult)\
                                 .then_inc(sem["v"] if t == NT - 1 else sem["dve"], 1)
                                if t < NT - 1:
                                    ch.n += 1
                            kk = kf[b][:, :, 0:MD]
                            for t in range(NT):
                                ins = V.tensor_scalar(kk[:, t, :], ps[:, t * 2 * MD:t * 2 * MD + MD], crms[b][:, t:t + 1], None, ALU.mult)
                                if t < NT - 1:
                                    ch.mark(ins)
                            ins.then_inc(sem["k_in"], 1)
                            dve.wait_ge(sem["k_in"], at("k_in", s))
                            half_turn(dve, ch, kk[:, :, None, :], kr[b][:, :, 0:MD].unsqueeze(2), k2[b][:, :, None, :], "ck2", "sk2", 1).then_inc(sem["k_rot"], 1)
                        else:
                            vin = half(ps[:, SEQ:2 * SEQ])
                            vd = v[b][:, :, :, 0:HD]
                            if l == 1:
                                V.tensor_copy(vd, vin.rearrange("p t (h d) -> p t h d", d=HD)).then_inc(sem["v"], 1)
                                V.tensor_copy(kf[b][:, :, :], half(ps[:, 0:SEQ])).then_inc(sem["k_in"], 1)
                                dve.wait_ge(sem["k_in"], at("k_in", s))
                                rope_products(ch, "k", kf[b], kr[b], kt2[b], kss[b])
                            else:
                                bv = W(f"bv{l}").rearrange("p (h d) -> p h d", d=HD)
                                for t in range(NT):
                                    ins = V.tensor_tensor(vd[:, t], vin[:, t].rearrange("p (h d) -> p h d", d=HD), bv, ALU.add)
                                    if t < NT - 1:
                                        ch.mark(ins)
                                ins.then_inc(sem["v"], 1)
                                V.tensor_tensor(kf[b][:, :, :], half(ps[:, 0:SEQ]), W(f"bk{l}")[:, None, :].to_broadcast([P, NT, P]), ALU.add).then_inc(sem["k_in"], 1)
                    if kind == "stats":
                        prev = x_ready_from(s, order)
                        if prev:
                            dve.wait_ge(sem[prev[0]], at(*prev))
                        elif in_loop:
                            dve.wait_ge(sem["x_in", b], 16)
                        layer_stats(x[b], b, mv, st)
                        V.tensor_scalar(rstd[b][:, :], mv[b][:, :, 1], 1e-5, None, ALU.add).then_inc(sem["var"], 1)
                    if kind == "norm":
                        n = "rms" if l == 2 else "rstd"
                        dve.wait_ge(sem[n], at(n, ("stats", l, b)))
                        for t in range(NT):
                            ins = V.tensor_scalar(xn[b][:, t, :], x[b][:, t, :], mv[b][:, t, 0:1], rstd[b][:, t:t + 1], ALU.subtract, ALU.mult)
                            if t < NT - 1:
                                ch.mark(ins)
                        ins.then_inc(sem["x_normed"], 1)
                    if kind == "query":
                        dve.wait_ge(sem["q_ps"], at("q_ps", s))
                        ps = half(bank("q_ps", s)[:, 0:SEQ])
                        if l in (0, 3):
                            bq = bq0s[:, :] if l == 0 else W("bq3")
                            V.tensor_tensor(qf[b][:, :, :], ps, bq[:, None, :].to_broadcast([P, NT, P]), ALU.add).then_inc(sem["q_in"], 1)
                            dve.wait_ge(sem["q_in"], at("q_in", s))
                        else:
                            V.tensor_copy(qf[b][:, :, :], ps).then_inc(sem["q_in"], 1)
                            dve.wait_ge(sem["q_in"], at("q_in", s))
                        if l == 1:
                            rope_products(ch, "q", qf[b], qr[b], qt2[b], qss[b])
                        if l == 2:
                            q4 = qf[b][:, :, :].rearrange("p t (h d) -> p t h d", d=MD)
                            r4 = qr[b][:, :, :].rearrange("p t (h d) -> p t h d", d=MD)
                            half_turn(dve, ch, q4, r4, q2[b][:, :, :, :], "cq2", "sq2", MQ).then_inc(sem["q_stack"], 1)
                    for n, stack, f, r, ss in (("k", ks, kf, kr, kss), ("q", qs, qf, qr, qss)):
                        hi, mid, low = (3, 0, 2) if n == "k" else (1, 0, 5)
                        if kind == f"{n}_turn":
                            dve.wait_ge(sem[f"{n}_prod"], at(f"{n}_prod", s))
                            dve.wait_ge(sem[f"{n}_rms"], at(f"{n}_rms", s))
                            V.tensor_tensor(heads(f[b]), heads(r[b]), ss[b][:, :, None].to_broadcast([P, NT * HEADS, HD]), ALU.mult)\
                             .then_inc(sem[f"{n}_ready"], 1)
                        if kind == f"{n}_mid":
                            dve.wait_ge(sem[f"{n}_hi"], at(f"{n}_hi", s))
                            V.tensor_tensor(heads(r[b]), heads(f[b]), stack[b][:, :, hi, :], ALU.subtract).then_inc(sem[f"{n}_rest"], 1)
                        if kind == f"{n}_low":
                            dve.wait_ge(sem[f"{n}_mid"], at(f"{n}_mid", s))
                            V.tensor_tensor(stack[b][:, :, low, :], heads(r[b]), stack[b][:, :, mid, :], ALU.subtract).then_inc(sem[f"{n}_stack"], 1)
                    if kind == "max":
                        part = s[3]
                        for i in range(2):
                            dve.wait_ge(sem[f"max{i}_ps"], at(f"max{i}_ps", s))
                            ps = bank(f"max{i}_ps", s)[:, :].rearrange("p (h k) -> p h k", h=2)
                            if l == 2:
                                dst, kn = nm2[b][:, part, 2 * i:2 * i + 2], SEQ
                            else:
                                t, jp = part // 4, part % 4
                                dst, kn = nm[b][:, t, i, 2 * jp:2 * jp + 2], (P if l == 1 and t == 0 else SEQ)
                            V.tensor_reduce(dst, ps[:, :, 0:kn], AX.X, ALU.max, negate=True).then_inc(sem[f"max{i}"], 1)
                    if kind == "shift":
                        lastp = ("max", l, b, 7 if l != 2 else 1)
                        dve.wait_ge(sem["max0"], at("max0", lastp))
                        dve.wait_ge(sem["max1"], at("max1", lastp))
                        if l == 2:
                            V.tensor_copy(nm2[b][:, 0, 0:1], nm2[b][:, 0, 0:1]).then_inc(sem["shift"], 1)
                        else:
                            for t in range(NT):
                                ch.link(V.tensor_copy(mp[b][:, t, :, 0, :], nm[b][:, t, :, :]))
                            for t in range(NT):
                                ins = V.tensor_tensor(mp[b][:, t, :, 1, :], nm[b][:, t, :, :], mp[b][:, t, :, 0, :], ALU.subtract)
                                if t < NT - 1:
                                    ch.mark(ins)
                            ins.then_inc(sem["shift"], 1)
                    if kind == "attend" and l == 0:
                        n = plan.nth[s]
                        before = prev_on("attend", s, 4)
                        if before:
                            dve.wait_ge(sem["weighed"], at("weighed", before))
                        if s[3] == 0:
                            dve.wait_ge(sem["biasT"], at("biasT", ("load", 0, b)))
                        dve.wait_ge(sem["scores_ps"], at("scores_ps", s))
                        bt = biasT[b][:, :, :].rearrange("p k q -> p (k q)")
                        V.tensor_tensor(probs[n % 4][:, :, :], bank("scores_ps", s)[:, :].rearrange("p (r n) -> p r n", r=2),
                                        bt[:, None, :].to_broadcast([P, 2, 512]), ALU.add).then_inc(sem["biased"], 1)
                    if kind == "divide":
                        lastp = ("attend", l, b, 7 if l != 2 else 1)
                        dve.wait_ge(sem["weighed"], at("weighed", lastp))
                        nh, d = (MQ, MD) if l == 2 else (HEADS, HD)
                        n = NT * nh
                        z = pv[:, 0:n * (d + 1)].rearrange("p (n d) -> p n d", d=d + 1)
                        ch.link(V.reciprocal(rec[b][:, 0:n], z[:, :, d]))
                        V.tensor_tensor(o[b][:, :, :].rearrange("p t (h d) -> p (t h) d", d=d), z[:, :, 0:d],
                                        rec[b][:, 0:n, None].to_broadcast([P, n, d]), ALU.mult).then_inc(sem["o"], 1)
                    if kind == "mix":
                        dve.wait_ge(sem["y_ps"], at("y_ps", s))
                        res = x
                        dve.wait_ge(sem["x_bias"], at("x_bias", ("stats", l, b)))
                        if l in (0, 3):
                            res = xb
                        V.scalar_tensor_tensor(out=x[b][:, :, :], in0=half(bank("y_ps", s)[:, 0:SEQ]), scalar=tg[:, l:l + 1],
                                               in1=res[b][:, :, :], op0=ALU.mult, op1=ALU.add).then_inc(sem["x_mixed"], 1)
                    if kind == "route":
                        dve.wait_ge(sem["logits_ps"], at("logits_ps", s))
                        ps = bank("logits_ps", s)[:, 0:NT * E].rearrange("p (t e) -> p t e", t=NT)
                        vals = lg
                        if l == 1:
                            V.tensor_tensor(lg[b][:, :, :], ps, W("gateb")[:, None, :].to_broadcast([P, NT, E]), ALU.add).then_inc(sem["logits"], 1)
                            dve.wait_ge(sem["logits"], at("logits", s))
                            ch.link(V.tensor_reduce(gm[b][:, :], lg[b][:, :, :], AX.X, ALU.max))
                            V.tensor_tensor(lg[b][:, :, :], lg[b][:, :, :], gm[b][:, :, None].to_broadcast([P, NT, E]), ALU.subtract).then_inc(sem["gate_in"], 1)
                            dve.wait_ge(sem["gate_exp"], at("gate_exp", s))
                            vals = ge
                        else:
                            V.tensor_copy(lg[b][:, :, :], ps).then_inc(sem["logits"], 1)
                            dve.wait_ge(sem["logits"], at("logits", s))
                        for t in range(NT):
                            ch.link(V.max(mx[b][:, t, :], vals[b][:, t, :]))
                        for t in range(NT):
                            ch.link(V.max_index(ix[b][:, t, :], mx[b][:, t, :], vals[b][:, t, :]))
                        ch.link(V.tensor_copy(ixf[b][:, :, :], ix[b][:, :, :]))
                        ns = 2 if l == 1 else 1
                        for t in range(NT):
                            for i in range(ns):
                                ins = V.tensor_scalar(oh[b][:, t, i, :], W("iota"), ixf[b][:, t, i:i + 1], None, ALU.is_equal)
                                if (t, i) != (NT - 1, ns - 1):
                                    ch.mark(ins)
                        ins.then_inc(sem["onehot"], 1)
                        if l == 1:
                            ch.link(V.tensor_reduce(gs[b][:, :], ge[b][:, :, :], AX.X, ALU.add))
                            ch.link(V.reciprocal(gs[b][:, :], gs[b][:, :]))
                            ch.link(V.tensor_tensor(gv[b][:, :], mx[b][:, :, 0], mx[b][:, :, 1], ALU.add))
                            ch.link(V.scalar_tensor_tensor(out=gv[b][:, :], in0=gv[b][:, :], scalar=tg[:, 5:6], in1=gs[b][:, :], op0=ALU.mult, op1=ALU.mult))
                    if kind == "spread":
                        if l == 1:
                            dve.wait_ge(sem["u"], at("u", s))
                            dve.wait_ge(sem["pick_ps"], at("pick_ps", s))
                            V.tensor_tensor(um[b][:, :, :], bank("pick_ps", s)[:, :].rearrange("p (i q) -> p i q", i=2),
                                            uT[b][:, None, :].to_broadcast([P, 2, SEQ]), ALU.mult).then_inc(sem["picked"], 1)
                        else:
                            for i in range(2):
                                dve.wait_ge(sem[f"spread{i}_ps"], at(f"spread{i}_ps", s))
                                V.tensor_tensor(xm[b][:, 4 * i:4 * i + 4, :], bank(f"spread{i}_ps", s)[:, :].rearrange("p (e q) -> p e q", e=4),
                                                xT[b][:, None, :].to_broadcast([P, 4, SEQ]), ALU.mult).then_inc(sem[f"spread{i}"], 1)
                    if kind == "outer":
                        dve.wait_ge(sem["f_ps"], at("f_ps", s))
                        dve.wait_ge(sem["x_bias"], at("x_bias", ("stats", 4 + l, b)))
                        ps = half(bank("f_ps", s)[:, 0:SEQ])
                        if l == 0:
                            V.scalar_tensor_tensor(out=x[b][:, :, :], in0=ps, scalar=tg[:, 4:5], in1=x[b][:, :, :],
                                                   op0=ALU.mult, op1=ALU.add).then_inc(sem["x_fed"], 1)
                        if l == 1:
                            V.tensor_tensor(y[b][:, :, :], ps, bo2x[:, None, :].to_broadcast([P, NT, P]), ALU.add).then_inc(sem["f_in"], 1)
                            dve.wait_ge(sem["f_in"], at("f_in", s))
                            for t in range(NT):
                                ins = V.scalar_tensor_tensor(out=x[b][:, t, :], in0=y[b][:, t, :], scalar=gv[b][:, t:t + 1], in1=x[b][:, t, :],
                                                             op0=ALU.mult, op1=ALU.add)
                                if t < NT - 1:
                                    ch.mark(ins)
                            ins.then_inc(sem["x_fed"], 1)
                        if l == 2:
                            dve.wait_ge(sem["y_res"], at("y_res", s))
                            V.tensor_tensor(y[b][:, :, :], ps, yr[b][:, :, :], ALU.add).then_inc(sem["f_in"], 1)
                            dve.wait_ge(sem["f_in"], at("f_in", s))
                            layer_stats(y[b], b, mv, st)
                            V.tensor_scalar(rstd[b][:, :], mv[b][:, :, 1], 1e-12, None, ALU.add).then_inc(sem["y_var"], 1)
                    if kind == "finish":
                        if l == 2:
                            dve.wait_ge(sem["y_rstd"], at("y_rstd", s))
                            for t in range(NT):
                                ch.link(V.tensor_scalar(y[b][:, t, :], y[b][:, t, :], mv[b][:, t, 0:1], rstd[b][:, t:t + 1], ALU.subtract, ALU.mult))
                            ch.link(V.tensor_tensor(y[b][:, :, :], y[b][:, :, :], tgam[:, None, :].to_broadcast([P, NT, P]), ALU.mult))
                            V.tensor_tensor(x[b][:, :, :], y[b][:, :, :], xb[b][:, :, :], ALU.add).then_inc(sem["x_fed"], 1)
                    if kind == "tail":
                        dve.wait_ge(sem["f_ps"], at("f_ps", s))
                        dve.wait_ge(sem["x_bias"], at("x_bias", ("stats", 7, b)))
                        for t in range(NT):
                            n = b * NT + t
                            ins = V.scalar_tensor_tensor(out=x[b][:, t, :], in0=bank("f_ps", s)[:, t * P:(t + 1) * P], scalar=wsum[:, n:n + 1],
                                                         in1=x[b][:, t, :], op0=ALU.mult, op1=ALU.add)
                            if t < NT - 1:
                                ch.mark(ins)
                        ins.then_inc(sem["x_fed"], 1)

        with nc.Fori(0, TURNS) as i:
            with nc.Block() as block:
                programs(block, turn, plan, (TURNS - 1 - i) * ROWS, True)
            nc.all_engine_barrier(sems_to_clear=all_sems)

        if SUBLAYERS == 8:
            with nc.Block() as block:
                programs(block, tail, tail_plan, 0, False)



def kernel(**inputs):
    import numpy as np
    import concourse.bacc as _bacc
    from concourse import mybir as _mybir
    from concourse.bass_utils import run_bass_kernel_spmd as _run

    a = {k: np.asarray(v) for k, v in inputs.items()}
    f = np.float32

    def rows(n):
        return np.broadcast_to(a[n].reshape(1, -1), (P, a[n].size))

    def tiles(w):
        return w.reshape(-1, P, w.shape[-1]).transpose(1, 0, 2).reshape(P, -1)

    pos = np.arange(SEQ, dtype=f)

    def spread(t):
        return tiles(np.ascontiguousarray(t.astype(f)))

    inv1 = (1.0 / np.power(f(500000.0), np.arange(0, HD, 2, dtype=f) / f(HD))).astype(f)
    ang1 = np.outer(pos, inv1).astype(f)
    emb1 = np.concatenate([ang1, ang1], -1)
    ts2 = np.power(f(10000.0), f(2.0 / MD) * np.arange(MD // 2, dtype=f)).astype(f)
    angk = (pos[:, None] / ts2).astype(f)
    angq = ((pos + SEQ)[:, None] / ts2).astype(f)
    sc = MD ** -0.5
    cos2, sin2 = (lambda g: np.concatenate([np.cos(g), np.cos(g)], -1)), (lambda g: np.concatenate([-np.sin(g), np.sin(g)], -1))
    i, j = np.arange(P)[:, None], np.arange(P)[None, :]
    tri = np.where(j <= i, 0.0, NEG).astype(f)
    ex = {
        "ident": np.eye(P, dtype=f), "tri": tri, "triT": np.ascontiguousarray(tri.T),
        "iota": np.broadcast_to(np.arange(E, dtype=f), (P, E)),
        "g": np.broadcast_to(np.concatenate([a["g_xattn"], a["g_ffn"]])[None], (P, 8)),
        "adj": tiles(a["L0_xattn_adj"]),
        "sig": a["L0_ffn_tile_sigs"].T, "wf0": a["L0_ffn_W"].transpose(1, 0, 2).reshape(P, -1),
        "qnw": rows("L1_xattn_q_norm_w"), "knw": rows("L1_xattn_k_norm_w"),
        "cos1": spread(np.cos(emb1)), "sin1": spread(np.sin(emb1)),
        "wi": a["L1_ffn_wi"].T, "bi": a["L1_ffn_bi"].reshape(FT, P).T, "wo_f1": tiles(a["L1_ffn_wo"].T), "bo_f1": rows("L1_ffn_bo"),
        "loraA": a["L1_ffn_lora_A"].reshape(P, P).T, "loraB": a["L1_ffn_lora_B"].transpose(0, 2, 1).reshape(P, FF),
        "gate": a["L1_ffn_gate_w"].T, "gateb": rows("L1_ffn_gate_b"),
        "rms": a["L2_xattn_rms_scale"].reshape(P, 1), "qw2": a["L2_xattn_q_w"].transpose(1, 0, 2).reshape(P, P),
        "kvw2": a["L2_xattn_kv_w"][:, 0].transpose(1, 0, 2).reshape(P, 2 * MD), "ow2": a["L2_xattn_out_w"].reshape(P, P),
        "cq2": spread(cos2(angq) * sc), "sq2": spread(sin2(angq) * sc), "ck2": spread(cos2(angk)), "sk2": spread(sin2(angk)),
        "wr": a["L2_ffn_Wr"].T, "w1_f2": a["L2_ffn_W1"].transpose(1, 0, 2).reshape(P, -1), "wo_f2": tiles(a["L2_ffn_Wo"]),
        "bo_f2": rows("L2_ffn_bo"), "gamma": rows("L2_ffn_gamma"), "beta": rows("L2_ffn_beta"),
        "w1_f3": a["L3_ffn_w1"], "w2_f3": tiles(a["L3_ffn_w2"]), "ew": tiles(a["L3_ffn_expert_weights"]),
    }
    for l in (0, 1, 3):
        for n in "qkvo":
            ex[f"w{n}{l}"] = a[f"L{l}_xattn_W{n}"].T
            if l != 1:
                ex[f"b{n}{l}"] = rows(f"L{l}_xattn_b{n}")
    arrays = {n: np.concatenate([ex[m] for m, _ in parts], axis=1) for n, parts in PACKS.items()}
    sel = np.zeros((16, E, P), f)
    for e in range(E):
        sel[e, e, :] = 1.0
    pick = np.zeros((2, 16, P), f)
    for c in range(2):
        for e in range(E):
            pick[c, c * E + e, e * RANK:(e + 1) * RANK] = 1.0
    small = np.zeros((16, SMALL_W), f)
    for n, w, r in (("sel", sel.reshape(16, -1), 16), ("pick1", pick[0], 16), ("pick2", pick[1], 16),
                    ("bf0", a["L0_ffn_b"], E), ("b1_f2", a["L2_ffn_b1"], E)):
        c, k = SMALL_COLS[n]
        small[0:r, c:c + k] = w
    arrays |= {"small": small, "x": a["x"], "ctx": a["ctx_1024"], "mask": a["mask_Bx1xSxS2_ik1"][:, 0],
               "mrow": a["mask_BxS2_bk0"]}
    arrays = {n: np.ascontiguousarray(v) for n, v in arrays.items()}

    nc = _bacc.Bacc("TRN2", target_bir_lowering=False, num_devices=1)
    dram = {n: nc.dram_tensor(f"in_{n}", v.shape, _mybir.dt.from_np(v.dtype), kind="ExternalInput").ap() for n, v in arrays.items()}
    out = nc.dram_tensor("out", (BATCH, SEQ, P), _mybir.dt.float32, kind="ExternalOutput").ap()
    build(nc, dram, out)
    r = _run(nc, [{f"in_{n}": v for n, v in arrays.items()}], core_ids=[0])
    return r.results[0]["out"]
```

```python
from contextlib import ExitStack

import concourse.bass as bass
from concourse import mybir

F32 = mybir.dt.float32
BF16 = mybir.dt.bfloat16
I32 = mybir.dt.int32
U32 = mybir.dt.uint32
U8 = mybir.dt.uint8
ALU = mybir.AluOpType
ACT = mybir.ActivationFunctionType
AX = mybir.AxisListType

P = 128
BATCH = 8
SEQ = 256
NT = SEQ // P
ROWS = 4
TURNS = BATCH // ROWS
HEADS = 16
HD = P // HEADS
MQ, MD = 4, 32
E = 8
RANK = 16
FF = 512
FT = FF // P
FF3 = 1024
FT3 = FF3 // P
STK = 64
TERMS = 6
KD = TERMS * HD
NEG = -1.0e30
FILL = -2.3819763e+38
SUBLAYERS = 8
TAIL_ROWS = 2
GROUP = 8
STACKS, WIDES, PROBS = 3, 2, 3


def columns(parts):
    at, out = 0, {}
    for name, n in parts:
        out[name] = (at, n)
        at += n
    return out, at


PACKS = {
    "c0": [("ident", P), ("tri", P), ("triT", P), ("iota", E), ("g", 8),
           ("wq0", P), ("wk0", P), ("wv0", P), ("wo0", P), ("bq0", P), ("bk0", P), ("bv0", P), ("bo0", P),
           ("adj", NT * SEQ)],
    "c1": [("sig", E), ("wf0", E * P),
           ("wq1", P), ("wk1", P), ("wv1", P), ("wo1", P), ("qnw", HD), ("knw", HD),
           ("cos1", NT * HD), ("sin1", NT * HD)],
    "c2": [("wi", FF), ("bi", FT), ("wo_f1", FF), ("bo_f1", P), ("loraA", P), ("loraB", FF), ("gate", E),
           ("gateb", E),
           ("rms", 1), ("qw2", P), ("kvw2", 2 * MD), ("ow2", P),
           ("cq2", NT * MD), ("sq2", NT * MD), ("ck2", NT * MD), ("sk2", NT * MD)],
    "c3": [("wr", E), ("w1_f2", E * FF), ("wo_f2", FF), ("bo_f2", P), ("gamma", P), ("beta", P)],
    "c4": [("wq3", P), ("wk3", P), ("wv3", P), ("wo3", P), ("bq3", P), ("bk3", P), ("bv3", P), ("bo3", P),
           ("ew", 2 * NT * TAIL_ROWS)],
}
SMALL = [("bf0", P), ("b1_f2", FF), ("part", 3)]
PICKS = [("sel", E * P), ("pick1", P), ("pick2", P)]
SPREADS = [("o", P // 2), ("r", P // 2), ("o2", P // 2), ("r2", P // 2)]
LATE_PACKS = ["c1", "c2", "c3", "c4"]
WHERE = {}
WIDTH = {}
for _pack, _parts in PACKS.items():
    _cols, WIDTH[_pack] = columns(_parts)
    WHERE.update({_n: (_pack, *_c) for _n, _c in _cols.items()})
SMALL_COLS, SMALL_W = columns(SMALL)
PICK_COLS, PICK_W = columns(PICKS)
SPREAD_COLS, SPREAD_W = columns(SPREADS)
SROWS = {l: MQ // 2 * (MD + 1) if l == 2 else GROUP * (HD + 1) for l in range(4)}



def row_steps(b):
    def keys(l):
        if 2 * l >= SUBLAYERS or l > 3:
            return [None] * 5
        steps = [("kv", l, b), ("k_turn", l, b) if l == 1 else None]
        return steps + ([("k_mid", l, b), ("k_low", l, b)] if l != 2 else [None, None]) + [("k_flip", l, b)]

    out = [("load", 0, b)] + keys(0)
    for l in range(4):
        parts_a, parts_b = (8, 8) if l != 2 else (2, 2)
        if 2 * l < SUBLAYERS:
            out += [("stats", l, b), ("norm", l, b), ("flip", l, b), ("query", l, b)]
            out += [("q_turn", l, b)] if l == 1 else [("bias", 0, b)] if l == 0 else []
            out += [("q_mid", l, b), ("q_low", l, b)] if l != 2 else []
            out += [("q_flip", l, b)]
            out += [("max", l, b, p) for p in range(parts_a)]
            out += [("shift", l, b), ("shift_flip", l, b)]
            for p in range(parts_b + AHEAD):
                out += [("attend", l, b, p)] if p < parts_b else []
                out += [("weigh", l, b, p - AHEAD)] if p >= AHEAD else []
            out += [("divide", l, b), ("o_flip", l, b), ("mix", l, b)]
        k = keys(l + 1)
        if 2 * l + 1 < SUBLAYERS and l < 3:
            out += [k[0], ("stats", 4 + l, b), k[1], ("norm", 4 + l, b), ("flip", 4 + l, b), k[2], ("route", l, b), k[3],
                    ("choose", l, b), k[4], ("spread", l, b), ("inner", l, b), ("outer", l, b)]
            out += [("finish", l, b)] if l == 2 else []
        else:
            out += k
    return [t for t in out if t] + [("store", 0, b)]


AHEAD = 2
COST = {"load": [("PE", .5), ("ACT", .4), ("DVE", 1.8), ("POOL", .7)],
        "bias": [("POOL", 5.5), ("PE", 1.2), ("ACT", .6)], "kv": [("PE", 1.7), ("DVE", 1), ("ACT", 1)],
        ("kv", 1): [("PE", 1.7), ("DVE", 3.2), ("POOL", 5.7)], ("kv", 2): [("PE", .9), ("DVE", 2.8)],
        "k_turn": [("DVE", .5), ("ACT", 1)], "k_mid": [("DVE", .4), ("ACT", .8)], "k_low": [("DVE", .4)],
        "k_flip": [("PE", 1.7), ("ACT", .8)], "stats": [("DVE", 1.6), ("POOL", 1.2)],
        ("stats", 2): [("DVE", 1.6), ("POOL", 3.5)], "norm": [("DVE", .8)], "flip": [("PE", .45), ("ACT", .4)],
        "query": [("PE", .9), ("DVE", .5), ("ACT", 1)], ("query", 1): [("PE", .9), ("DVE", 3), ("POOL", 5.7)],
        ("query", 2): [("PE", .9), ("DVE", 2)], "q_turn": [("DVE", .5), ("ACT", 1)],
        "q_mid": [("DVE", .4), ("ACT", .8)], "q_low": [("DVE", .4)], "q_flip": [("PE", 1.7), ("ACT", .8)],
        ("q_flip", 2): [("PE", 1.7), ("ACT", 1.4)], "max": [("PE", 1), ("DVE", 1.1)],
        ("max", 0): [("PE", 1.5), ("DVE", 1.3)], ("max", 2): [("PE", 3.4), ("DVE", 1.3)], "shift": [("DVE", .8)],
        "shift_flip": [("PE", .3), ("ACT", .4), ("SP", 2.5)], "attend": [("PE", .9), ("ACT", 1)],
        ("attend", 0): [("PE", .9), ("DVE", 1.2), ("ACT", 1)], ("attend", 2): [("PE", 3.4), ("ACT", 1)],
        "weigh": [("PE", 1.7)], ("weigh", 1): [("PE", 1.3)], ("weigh", 2): [("PE", 3.4)], "divide": [("ACT", .7)],
        "o_flip": [("PE", 1.7), ("DVE", 1.8)], "mix": [("PE", .9), ("DVE", .5)], "route": [("PE", .5), ("DVE", 2.5)],
        ("route", 1): [("PE", .5), ("DVE", 1), ("ACT", .4), ("DVE", 3)], "choose": [("PE", .3), ("ACT", .8)],
        "spread": [("PE", 1.2), ("DVE", 2.6)], ("spread", 1): [("PE", .3), ("DVE", .8)], "inner": [],
        ("inner", 1): [("PE", 5.3), ("ACT", 3.5), ("POOL", 2)], ("inner", 2): [("PE", 17.1), ("ACT", 2.5)],
        "outer": [("PE", 5.6), ("DVE", .5)], ("outer", 1): [("PE", 1.7), ("DVE", 1.5)],
        ("outer", 2): [("PE", 1.7), ("DVE", 2), ("POOL", .8)], "finish": [("DVE", 2)], "store": []}
LAG = 8
RANKED = 0.5
HOP = 0.15


SHARED = {"pv": (1, [("attend", l) for l in range(4)], [("divide", l) for l in range(4)]),
          "wide": (WIDES, [("load", 0), ("spread", 0), ("inner", 1), ("spread", 2)],
                   [("bias", 0)] + [("outer", l) for l in range(3)]),
          "stack": (STACKS, [("kv", 0), ("k_turn", 1), ("kv", 3), ("query", 0), ("q_turn", 1), ("query", 3)],
                    [(f"{n}_flip", l) for n in "kq" for l in (0, 1, 3)])}


def turn_order():
    rows, at, out = [row_steps(b) for b in range(ROWS)], [0] * ROWS, []
    holders = {name: [] for name in SHARED}
    free, done = {}, {}

    def can_go(s):
        for name, (n, takes, _) in SHARED.items():
            held = holders[name]
            if s[:2] in takes and not (s[0] == "attend" and s[3]) and len(held) >= n and not held[-n][1]:
                return False
        return True

    def chain(s):
        return ("keys" if s[0][0] == "k" else "row", s[2])

    def start(s, engine=True):
        b = s[2]
        t = done.get(chain(s), LAG * b)
        if s[0] == "weigh":
            t = done["part", *s[1:]]
        if s[0] == "shift":
            t = done["maxima", b]
        if s[0] in ("max", "kv"):
            t = max(t, done.get(("keys" if s[0] == "max" else "row", b), 0))
        phases = COST.get(s[:2], COST[s[0]])
        return max(t, free.get(phases[0][0], 0)) if phases and engine else t

    while any(at[b] < len(rows[b]) for b in range(ROWS)):
        b = min((b for b in range(ROWS) if at[b] < len(rows[b]) and can_go(rows[b][at[b]])),
                key=lambda b: RANKED * start(rows[b][at[b]]) + start(rows[b][at[b]], False))
        s = rows[b][at[b]]
        for name, (n, takes, gives) in SHARED.items():
            if s[:2] in takes and not (s[0] == "attend" and s[3]):
                holders[name].append([b, False])
            if s[:2] in gives:
                next(h for h in holders[name] if h[0] == b and not h[1])[1] = True
        out.append(s)
        at[b] += 1
        t = first = start(s)
        for n, (eng, us) in enumerate(COST.get(s[:2], COST[s[0]])):
            t = max(t, free.get(eng, 0)) + us
            if eng != "SP":
                free[eng] = t
            t += HOP
            if n == 0:
                first = t
        done[chain(s)] = first if s[0] in ("max", "attend") else t
        if s[0] == "max":
            done["maxima", b] = t
        if s[0] == "attend":
            done["part", *s[1:]] = t
    first = next((s for s in out if s[:2] == ("kv", 1)), out[-1])
    out.insert(out.index(first), ("fold", 0, 0))
    return out


def psum_uses(s):
    kind, l, b = s[:3]
    wide = l != 2
    uses = {
        "load": [("ctxT_ps", "one", "ctxT")],
        "bias": [("biasT_ps", "one", "biasT")],
        "kv": [("kv_ps", "one", "k_in")],
        "k_flip": [("kT0_ps", "one", "kT0"), ("kT1_ps", "one", "kT1")] if wide else [("kT2_ps", "one", "kT0")],
        "flip": [("xT_ps", "one", "xT")],
        "query": [("q_ps", "one", "q_in")],
        "q_flip": [("qT0_ps", "one", "qT0"), ("qT1_ps", "one", "qT1")] if wide else [("qT2_ps", "two", "qT1")],
        "max": [("max0_ps", "one", "max0"), ("max1_ps", "one", "max1")],
        "shift_flip": [("shift_ps", "one", "shiftT")],
        "attend": [("scores_ps", "two", "biased" if l == 0 else "probs")],
        "o_flip": [("oT_ps", "one", "oT")],
        "mix": [("y_ps", "one", "x_mixed")],
        "route": [("logits_ps", "one", "logits")],
        "choose": [("onehotT_ps", "one", "onehotT")] + ([("u_ps", "one", "u")] if l == 1 else []),
        "spread": [("pick_ps", "one", "picked")] if l == 1 else
                  [("spread0_ps", "two", "spread0"), ("spread1_ps", "two", "spread1")],
        "inner": [[], [("h0_ps", "two", "h1")], [("h0_ps", "two", "h0")]][l] if l < 3 else [],
        "outer": [("f_ps", "one", "f_in" if l else "x_fed")],
        "tail": [("h0_ps", "two", "h0"), ("h1_ps", "two", "h1"), ("f_ps", "one", "x_fed")],
    }
    return uses.get(kind, [])


def stages(s):
    kind, l, b = s[:3]
    wide = l != 2
    more = {
        "fold": ["folded_act", "folded_dve"],
        "load": ["ctxT", "ctx_var", "ctx_rms"],
        "bias": ["bias", "bias_hi", "biasT"],
        "kv": ["k_in", "v"] + (["k_var", "k_rms", "k_prod"] if l == 1 else ["k_hi"] if wide else ["k_rot", "mask_row"]),
        "k_turn": ["k_ready", "k_hi"],
        "k_mid": ["k_rest", "k_mid"],
        "k_low": ["k_stack"],
        "k_flip": ["kT0", "kT1"] if wide else ["kT0"],
        "stats": ["var", "rstd"] + (["rms"] if l == 2 else []) + ["x_bias"],
        "norm": ["x_normed"],
        "flip": ["xT"],
        "query": ["q_in"] + (["q_var", "q_rms", "q_prod"] if l == 1 else ["q_hi"] if wide else ["q_stack"]),
        "q_turn": ["q_ready", "q_hi"],
        "q_mid": ["q_rest", "q_mid"],
        "q_low": ["q_stack"],
        "q_flip": ["qT0", "qT1"],
        "max": ["max0", "max1"],
        "shift": ["shift"],
        "shift_flip": ["shiftT"],
        "attend": (["biased"] if l == 0 else []) + ["probs"] + (["v_placed"] if s[3:] == (0,) else []),
        "weigh": ["weighed"],
        "divide": ["sums"],
        "o_flip": ["oT"],
        "mix": ["x_mixed"],
        "route": ["logits", "onehot"] + (["gate_in", "gate_exp"] if l == 1 else []),
        "choose": ["onehotT"] + (["u"] if l == 1 else []),
        "spread": ["picked"] if l == 1 else ["spread0", "spread1"],
        "inner": [[], ["h1_ps", "h0", "h1", "h_sum"], ["h0"]][l] if l < 3 else [],
        "outer": (["f_in"] if l else []) + (["y_res", "y_var", "y_rstd"] if l == 2 else ["x_fed"]),
        "finish": ["x_fed"],
        "tail": ["h0", "h1", "x_fed"],
        "store": [],
    }[kind]
    return [u[0] for u in psum_uses(s)] + more


def buffer_uses(s):
    kind, l = s[:2]
    if kind == "attend":
        return [("probs_in", "probs", "weighed")]
    if (kind, l) in SHARED["wide"][1]:
        return [("mask", "wide", "biasT_ps")] if kind == "load" else [("wide", "wide", "f_ps")]
    if (kind, l) in SHARED["stack"][1]:
        n = kind[0]
        return [(f"{n}s", "stack", f"{n}T1_ps")]
    return [("wide", "wide", "f_ps")] if kind == "tail" else []


class Plan:

    def __init__(self, order, slots):
        self.value, self.slot, self.before, self.nth = {}, {}, {}, {}
        count, at, last, steps = {}, {ring: 0 for ring in slots}, {}, {}
        for s in order:
            for stage in stages(s):
                count[stage] = count.get(stage, 0) + 1
                self.value[(stage, *s[1:])] = count[stage]
            for use, ring, reader in psum_uses(s) + buffer_uses(s):
                slot = (ring, at[ring] % slots[ring])
                key = (use, *s[1:])
                at[ring] += 1
                self.slot[key] = slot
                self.before[key] = last.get(slot)
                last[slot] = (reader, *s[1:])
            steps[s[0]] = steps.get(s[0], 0) + 1
            self.nth[s] = steps[s[0]] - 1
        self.names = sorted(count)


def build(nc, dram, out):
    turn = turn_order()
    rings = {"one": 3, "two": 2, "probs": PROBS, "wide": WIDES, "stack": STACKS}
    plan = Plan(turn, rings)
    tail = [("stats", 7, b) for b in range(TAIL_ROWS)] + [("norm", 7, b) for b in range(TAIL_ROWS)] + \
           [("flip", 7, b) for b in range(TAIL_ROWS)] + \
           [("tail", 3, b) for b in range(TAIL_ROWS)]
    tail_plan = Plan(tail, rings)

    with ExitStack() as ctx:
        def sb(name, shape, dt=F32):
            return ctx.enter_context(nc.sbuf_tensor(name, shape, dt))

        def each(name, shape, dt=F32):
            return [sb(f"{name}_row{b}", shape, dt) for b in range(ROWS)]

        pack = {n: sb(n, [P, w]) for n, w in WIDTH.items()}
        small_parts = sb("small_parts", [3 * E, P + FF], BF16)
        spreads = sb("spreads", [GROUP * (HD + 1), SPREAD_W])

        def W(name):
            n, a, w = WHERE[name]
            return pack[n][:, a:a + w]

        def biases(name):
            a, w = SMALL_COLS[name]
            return small_parts[:, a:a + w]

        identb = sb("identb", [P, P], BF16)
        trib = sb("trib", [P, P], BF16)
        triTb = sb("triTb", [P, P], BF16)
        selb = sb("selb", [E, E * P], BF16)
        pickb = sb("pickb", [16, 2 * P], BF16)
        wq0s = sb("wq0s", [P, P])
        bq0s = sb("bq0s", [P, P])
        sgn = sb("sgn", [P, E])
        wc = {"q": sb("wcq", [P, NT, HD]), "k": sb("wck", [P, NT, HD])}
        ws = {"q": sb("wsq", [P, NT, HD]), "k": sb("wsk", [P, NT, HD])}
        qw2 = sb("qw2s", [P, P])
        kvw2 = sb("kvw2s", [P, 2 * MD])
        rms1 = sb("rms1", [P, 1])
        tg = sb("tg", [P, 8])
        tbo = {0: sb("tbo0", [P, P]), 3: sb("tbo3", [P, P])}
        tgam = sb("tgam", [P, P])
        tbeta = sb("tbeta", [P, P])
        bo2x = sb("bo2x", [P, P])
        wsum = sb("wsum", [P, TAIL_ROWS * NT])
        neghalf = sb("neghalf", [P, NT * HEADS])

        x = each("x", [P, NT, P])
        ctxT = each("ctxT", [P, SEQ])
        xn = each("xn", [P, NT, P])
        xT = each("xT", [P, SEQ])
        xb = each("xb", [P, NT, P])
        biasT = each("biasT", [P, NT, SEQ])
        brief = each("brief", [P, NT, P])
        qf = each("qf", [P, NT, P])
        qr = each("qr", [P, NT, P])
        qT = each("qT", [P, 8, SEQ], BF16)
        kT = each("kT", [P, 8, SEQ], BF16)
        v = each("v", [P, NT, P])
        mrow8 = each("mrow8", [MD + 1, SEQ], U8)
        cst = each("cst", [P, NT, 6])
        cmv = each("cmv", [P, NT, 2])
        crms = each("crms", [P, NT])
        st = each("st", [P, NT, 6])
        mv = each("mv", [P, NT, 2])
        rstd = each("rstd", [P, NT])
        rms = each("rms", [P, NT])
        qss = each("qss", [P, NT * HEADS])
        kss = each("kss", [P, NT * HEADS])
        nm = each("nm", [P, NT, 2, 8])
        mp = each("mp", [P, NT, 2, 2, 8], BF16)
        mT = each("mT", [32, SEQ], BF16)
        k2 = each("k2", [P, NT, MD])
        v2 = each("v2", [P, NT, MD])
        nm2 = each("nm2", [P, NT, MQ])
        mT2 = each("mT2", [8, P])
        lg = each("lg", [P, NT, E])
        ge = each("ge", [P, NT, E])
        gm = each("gm", [P, NT])
        gs = each("gs", [P, NT])
        gv = each("gv", [P, NT])
        mx = each("mx", [P, NT, 8])
        ix = each("ix", [P, NT, 8], U32)
        ixf = each("ixf", [P, NT, 8])
        oh = each("oh", [P, NT, 3, E], BF16)
        ohT = each("ohT", [3 * E, SEQ], BF16)
        cx = xn
        oT = xT
        kf, kr, y, yr = qf, qr, qf, qr
        bias_hi = [t[:, :, :].rearrange("p t d -> p (t d)").bitcast(BF16).rearrange("p (t k) -> p t k", t=NT) for t in brief]
        qt2, kt2 = brief, brief
        q2 = [t[:, :, :].rearrange("p t (h d) -> p t h d", h=MQ) for t in brief]
        uT = [t[:, :, :].rearrange("p t d -> p (t d)") for t in qf]
        um = biasT
        weighed_sb = biasT
        q2T = [t[0:MD + 2, :, :].rearrange("p j q -> p (j q)").bitcast(F32).rearrange("p (h q) -> p h q", h=MQ) for t in qT]
        k2T = [t[0:MD + 2, 0:2, :].rearrange("p j q -> p (j q)").bitcast(F32) for t in kT]

        stacks = [sb(f"stack{i}", [P, NT * HEADS, 8, HD], BF16) for i in range(STACKS)]
        wides = [sb(f"wide{i}", [P, E, SEQ]) for i in range(WIDES)]
        probs = [sb(f"probs{i}", [P, 2, 512]) for i in range(PROBS)]
        vpad = sb("vpad", [P, NT, 2, GROUP * GROUP * (HD + 1) + GROUP * (HD + 1)])
        v2pad = sb("v2pad", [P, NT, 2 * 3 * (MD + 1)])
        picks = probs[0][0:16, :, :].rearrange("p r n -> p (r n)"), probs[1][0:16, :, :].rearrange("p r n -> p (r n)")
        small, rest = (t[0:3 * E, :, :].rearrange("p r n -> p (r n)") for t in (probs[2], probs[1]))
        late = stacks[0][:, :, :, :].rearrange("p n g d -> p (n g d)").bitcast(F32), \
            stacks[1][:, :, :, :].rearrange("p n g d -> p (n g d)").bitcast(F32)

        banks = {("one", i): ctx.enter_context(nc.psum_tensor(f"one{i}", [P, 512], F32)) for i in range(rings["one"])}
        banks |= {("two", i): ctx.enter_context(nc.psum_tensor(f"two{i}", [P, 1024], F32)) for i in range(rings["two"])}
        pv = ctx.enter_context(nc.psum_tensor("pv", [P, 512], F32))

        const_in = ctx.enter_context(nc.semaphore("const_in"))
        early_in = ctx.enter_context(nc.semaphore("early_in"))
        setup_act = ctx.enter_context(nc.semaphore("setup_act"))
        setup_dve = ctx.enter_context(nc.semaphore("setup_dve"))
        setup_pool = ctx.enter_context(nc.semaphore("setup_pool"))
        sem = {}
        for name in plan.names:
            sem[name] = ctx.enter_context(nc.semaphore(name))
        sem["late_in"] = ctx.enter_context(nc.semaphore("late_in"))
        for b in range(ROWS):
            for name in ("x_in", "ctx_in", "mask_in", "row_in", "shift_in"):
                sem[name, b] = ctx.enter_context(nc.semaphore(f"{name}{b}"))
        sem["stored"] = ctx.enter_context(nc.semaphore("stored"))
        sem["dve"] = ctx.enter_context(nc.semaphore("dve_done"))
        sem["act"] = ctx.enter_context(nc.semaphore("act_done"))
        sem["pool"] = ctx.enter_context(nc.semaphore("pool_done"))
        nums = [s.num for s in sem.values()]
        all_sems = range(min(nums), max(nums) + 1)

        class Chain:

            def __init__(self, eng, s):
                self.eng, self.s, self.n = eng, s, 0

            def mark(self, ins):
                ins.then_inc(self.s, 1)
                self.n += 1

            def link(self, ins):
                self.mark(ins)
                self.eng.wait_ge(self.s, self.n)

        def shifted(b):
            n, got = 0, {}
            for s in turn:
                if s[0] == "shift" and s[2] == b:
                    n += 16 * (2 if s[1] == 2 else 4)
                    got[s[1]] = n
            return got

        shift_at = [shifted(b) for b in range(ROWS)]

        def x_ready_from(s, p):
            prev = None
            for t in p:
                if t == s:
                    break
                if t[2] == s[2] and t[0] in ("mix", "outer", "finish", "tail"):
                    prev = ("x_mixed" if t[0] == "mix" else "x_fed"), t
            return prev

        with nc.Block() as block:
            @block.sync
            def _(sp):
                sp.dma_start(pack["c0"][:, :], dram["c0"]).then_inc(early_in, 16)
                sp.dma_start(picks[0], dram["picks"][:, 0:E * P]).then_inc(early_in, 16)
                sp.dma_start(picks[1][:, 0:2 * P], dram["picks"][:, E * P:PICK_W]).then_inc(early_in, 16)
                sp.dma_start(spreads[:, :], dram["spreads"]).then_inc(early_in, 16)
                sp.dma_start(small[:, 0:SMALL_W], dram["small"]).then_inc(early_in, 16)

            @block.scalar
            def _(act):
                act.wait_ge(early_in, 16 * 5)
                act.activation(tg[:, :], W("g"), ACT.Tanh).then_inc(setup_act, 1)
                act.activation(wq0s[:, :], W("wq0"), ACT.Copy, scale=HD ** -0.5)
                act.activation(bq0s[:, :], W("bq0"), ACT.Copy, scale=HD ** -0.5)
                act.activation(selb[:, :], picks[0][0:E, :], ACT.Copy)
                act.activation(pickb[:, :], picks[1][:, 0:2 * P], ACT.Copy)
                for n in LATE_PACKS:
                    act.dma_start(pack[n][:, :], dram[n]).then_inc(const_in, 16)

            @block.gpsimd
            def _(pool):
                pool.memset(neghalf[:, :], -0.5)
                vp = vpad[:, :, :, :].rearrange("p t g (j w) -> p (t g) j w", w=GROUP * (HD + 1) + HD + 1)
                v2p = v2pad[:, :, :].rearrange("p t (j w) -> p t j w", j=2)
                pool.memset(vpad[:, :, :, :], 0.0)
                pool.memset(v2pad[:, :, :], 0.0)
                for i in range(STACKS):
                    last = pool.memset(stacks[i][:, :, TERMS:8, :], 0.0)
                last.then_inc(setup_pool, 1)
                pool.wait_ge(setup_pool, 1)
                pool.memset(vp[:, :, :, HD:HD + 1], 1.0)
                pool.memset(v2p[:, :, :, MD:MD + 1], 1.0)
                for i in range(STACKS):
                    pool.memset(stacks[i][:, :, TERMS, 0:2], 1.0)

            @block.vector
            def _(dve):
                dve.wait_ge(early_in, 16 * 5)
                nc.vector.tensor_copy(identb[:, :], W("ident"))
                nc.vector.tensor_copy(trib[:, :], W("tri"))
                nc.vector.tensor_copy(triTb[:, :], W("triT"))
                V, n = nc.vector, P + FF
                full, part = small[:, 0:n], small[:, n:n + 3]
                half, left = small[:, 660:660 + n // 2].bitcast(BF16), rest[:, 300:300 + n]
                V.tensor_copy(half, full).then_inc(setup_dve, 1)
                dve.wait_ge(setup_dve, 1)
                V.tensor_tensor(left, full, half, ALU.subtract).then_inc(setup_dve, 1)
                V.tensor_scalar(small_parts[:, :], half, part[:, 0:1], None, ALU.mult).then_inc(setup_dve, 1)
                dve.wait_ge(setup_dve, 3)
                V.tensor_copy(half, left).then_inc(setup_dve, 1)
                dve.wait_ge(setup_dve, 4)
                V.tensor_tensor(left, left, half, ALU.subtract).then_inc(setup_dve, 1)
                V.scalar_tensor_tensor(out=small_parts[:, :], in0=half, scalar=part[:, 1:2], in1=small_parts[:, :],
                                       op0=ALU.mult, op1=ALU.add).then_inc(setup_dve, 1)
                dve.wait_ge(setup_dve, 6)
                V.scalar_tensor_tensor(out=small_parts[:, :], in0=left, scalar=part[:, 2:3], in1=small_parts[:, :],
                                       op0=ALU.mult, op1=ALU.add)
                dve.wait_ge(setup_act, 1)
                nc.vector.tensor_scalar(tbo[0][:, :], W("bo0"), tg[:, 0:1], None, ALU.mult)

        n_late = 16 * len(LATE_PACKS)

        def programs(block, order, plan, first_row, in_loop):
            def at(stage, s):
                return plan.value[(stage, *s[1:])]

            def bank(use, s):
                return banks[plan.slot[(use, *s[1:])]]

            def claim(pe, use, s):
                before = plan.before[(use, *s[1:])]
                if before:
                    pe.wait_ge(sem[before[0]], plan.value[before])

            def prev_on(kind, s, back):
                same = [t for t in order if t[0] == kind]
                i = same.index(s) - back
                return same[i] if i >= 0 else None

            def heads(t):
                return t[:, :, :].rearrange("p t (h d) -> p (t h) d", d=HD)

            def rope_products(ch, n, f, r, t2, ss):
                H2 = HD // 2
                V = nc.vector
                f4, r4, t4 = (t[:, :, :].rearrange("p t (h d) -> p t h d", d=HD) for t in (f, r, t2))
                ch.link(V.tensor_tensor(heads(r), heads(f), heads(f), ALU.mult))
                ch.link(V.tensor_reduce(ss[:, :], heads(r), AX.X, ALU.add))
                V.tensor_scalar(ss[:, :], ss[:, :], 1.0 / HD, 1e-10, ALU.mult, ALU.add).then_inc(sem[f"{n}_var"], 1)
                ch.mark(V.tensor_tensor(r4, f4, wc[n][:, :, None, :].to_broadcast([P, NT, HEADS, HD]), ALU.mult))
                ch.mark(V.tensor_tensor(t4[:, :, :, 0:H2], f4[:, :, :, H2:HD], ws[n][:, :, None, 0:H2].to_broadcast([P, NT, HEADS, H2]), ALU.mult))
                ch.link(V.tensor_tensor(t4[:, :, :, H2:HD], f4[:, :, :, 0:H2], ws[n][:, :, None, H2:HD].to_broadcast([P, NT, HEADS, H2]), ALU.mult))
                V.tensor_tensor(r[:, :, :], r[:, :, :], t2[:, :, :], ALU.add).then_inc(sem[f"{n}_prod"], 1)

            def parts(src, stack, lo, hi):
                return nc.scalar.activation(stack[:, :, lo:hi, :], heads(src)[:, :, None, :].to_broadcast([P, NT * HEADS, hi - lo, HD]), ACT.Copy)

            def stack_transposes(pe, ps, src, g):
                dst = ps[:, :].bitcast(BF16)
                for jj in range(4):
                    for t in range(NT):
                        hh = t * HEADS + 2 * (4 * g + jj)
                        ins = pe.transpose(dst[:, jj * SEQ + t * P:jj * SEQ + (t + 1) * P],
                                           src[:, hh:hh + 2, :, :].rearrange("p h g d -> p (h g d)"), identb[:, :])
                return ins

            def held(ring, use, s):
                return ring[plan.slot[(use, *s[1:])][1]]

            def half_turn(dve, ch, f, tmp, dst, cname, sname, nh):
                c = W(cname).rearrange("p (t d) -> p t d", t=NT)
                sn = W(sname).rearrange("p (t d) -> p t d", t=NT)
                H2 = MD // 2
                V = nc.vector
                shape = [P, NT, nh, H2]
                ch.mark(V.tensor_tensor(dst, f, c[:, :, None, :].to_broadcast([P, NT, nh, MD]), ALU.mult))
                ch.mark(V.tensor_tensor(tmp[:, :, :, 0:H2], f[:, :, :, H2:MD], sn[:, :, None, 0:H2].to_broadcast(shape), ALU.mult))
                ch.link(V.tensor_tensor(tmp[:, :, :, H2:MD], f[:, :, :, 0:H2], sn[:, :, None, H2:MD].to_broadcast(shape), ALU.mult))
                return V.tensor_tensor(dst, dst, tmp, ALU.add)

            @block.sync
            def _(sp):
                if not in_loop:
                    for i in range(2):
                        sp.dma_start(late[i], dram["late"][:, i * FF3:(i + 1) * FF3]).then_inc(sem["late_in"], 16)
                for s in order:
                    kind, l, b = s[:3]
                    if kind == "load":
                        row = first_row + b
                        sp.dma_start(cx[b][:, :, :], dram["ctx"][bass.ds(row, 1)].rearrange("o (t p) d -> p (o t) d", p=P)).then_inc(sem["ctx_in", b], 16)
                        msk = held(wides, "mask", s)[:, 0:NT, :].bitcast(I32)
                        claim(sp, "mask", s)
                        sp.dma_start(msk, dram["mask"][bass.ds(row, 1)].rearrange("o (t p) k -> p (o t) k", p=P)).then_inc(sem["mask_in", b], 16)
                        sp.dma_start(x[b][:, :, :], dram["x"][bass.ds(row, 1)].rearrange("o (t p) d -> p (o t) d", p=P)).then_inc(sem["x_in", b], 16)
                        sp.dma_start(mrow8[b][MD:MD + 1, :], dram["mrow"][bass.ds(row, 1)]).then_inc(sem["row_in", b], 16)
                    if kind == "shift_flip":
                        sp.wait_ge(sem["shiftT"], at("shiftT", s))
                        if l == 2:
                            for t in range(NT):
                                sp.dma_start(q2T[b][MD + 1:MD + 2, :, t * P:(t + 1) * P], mT2[b][MQ * t:MQ * t + MQ, :]).then_inc(sem["shift_in", b], 16)
                        else:
                            for r in range(2):
                                for part in range(2):
                                    row = STK * r + KD + part
                                    n = 16 * r + 8 * part
                                    sp.dma_start(qT[b][row:row + 1, :, :], mT[b][n:n + 8, :]).then_inc(sem["shift_in", b], 16)
                    if kind == "store" or kind == "tail":
                        last = ("x_fed", s) if kind == "tail" else x_ready_from(s, order)
                        if last:
                            sp.wait_ge(sem[last[0]], at(*last))
                        row = first_row + b
                        dst = out[bass.ds(row, 1)] if in_loop else out[row:row + 1]
                        sp.dma_start(dst.rearrange("o (t p) d -> p (o t) d", p=P), x[b][:, :, :]).then_inc(sem["stored"], 16)
                sp.wait_ge(sem["stored"], 16 * len([s for s in order if s[0] in ("store", "tail")]))

            @block.gpsimd
            def _(pool):
                ch = Chain(pool, sem["pool"])

                def power(t, n):
                    return pool.tensor_tensor(t, t, neghalf[:, 0:n], ALU.pow)

                for s in order:
                    kind, l, b = s[:3]
                    if kind == "fold":
                        pool.wait_ge(const_in, n_late)
                        pool.wait_ge(sem["folded_dve"], at("folded_dve", s))
                    if kind == "bias":
                        pool.wait_ge(sem["mask_in", b], 16)
                        wide = held(wides, "mask", s)
                        msk, bias = wide[:, 0:NT, :].bitcast(I32), wide[:, NT:2 * NT, :]
                        ch.link(pool.tensor_scalar(bias, msk, 0.0, NEG, ALU.is_equal, ALU.mult))
                        adj = W("adj").rearrange("p (t k) -> p t k", t=NT)
                        pool.tensor_tensor(bias, bias, adj, ALU.add).then_inc(sem["bias"], 1)
                        pool.wait_ge(sem["bias"], at("bias", s))
                        pool.tensor_copy(bias_hi[b], bias).then_inc(sem["bias_hi"], 1)
                    if kind == "load":
                        pool.wait_ge(sem["ctx_var"], at("ctx_var", s))
                        power(crms[b][:, :], NT).then_inc(sem["ctx_rms"], 1)
                    if kind == "kv" and l == 1:
                        pool.wait_ge(sem["k_var"], at("k_var", s))
                        power(kss[b][:, :], NT * HEADS).then_inc(sem["k_rms"], 1)
                    if kind == "stats":
                        pool.wait_ge(sem["var"], at("var", s))
                        power(rstd[b][:, :], NT).then_inc(sem["rstd"], 1)
                        if l == 2:
                            pool.wait_ge(sem["rstd"], at("rstd", s))
                            ch.link(pool.tensor_tensor(rms[b][:, :], rstd[b][:, :], rstd[b][:, :], ALU.mult))
                            ch.link(pool.tensor_tensor(rms[b][:, :], rms[b][:, :], mv[b][:, :, 1], ALU.mult))
                            ch.link(pool.tensor_scalar(rms[b][:, :], rms[b][:, :], 1e-6, 0.0, ALU.add, ALU.add))
                            ch.link(power(rms[b][:, :], NT))
                            pool.tensor_tensor(rstd[b][:, :], rms[b][:, :], rstd[b][:, :], ALU.mult).then_inc(sem["rms"], 1)
                        add = {0: tbo[0], 3: tbo[3], 6: tbeta}.get(l)
                        src = add if add is not None else tbeta
                        pool.tensor_tensor(xb[b][:, :, :], x[b][:, :, :], src[:, None, :].to_broadcast([P, NT, P]), ALU.add).then_inc(sem["x_bias"], 1)
                    if kind == "query" and l == 1:
                        pool.wait_ge(sem["q_var"], at("q_var", s))
                        power(qss[b][:, :], NT * HEADS).then_inc(sem["q_rms"], 1)
                    if kind == "inner" and l == 1:
                        pool.wait_ge(sem["h1"], at("h1", s))
                        wide = held(wides, "wide", s)
                        pool.tensor_tensor(wide[:, 0:FT, :], wide[:, 0:FT, :], wide[:, FT:E, :], ALU.add).then_inc(sem["h_sum"], 1)
                    if kind == "outer" and l == 2:
                        pool.wait_ge(sem["x_normed"], at("x_normed", ("norm", 6, b)))
                        pool.wait_ge(sem["k_stack"], at("k_stack", ("k_low", 3, b)))
                        pool.tensor_tensor(yr[b][:, :, :], xn[b][:, :, :], W("bo_f2")[:, None, :].to_broadcast([P, NT, P]), ALU.add).then_inc(sem["y_res"], 1)
                        pool.wait_ge(sem["y_var"], at("y_var", s))
                        power(rstd[b][:, :], NT).then_inc(sem["y_rstd"], 1)

            @block.scalar
            def _(act):
                for s in order:
                    kind, l, b = s[:3]

                    def evac(dst, use, cols, stage, **kw):
                        act.wait_ge(sem[use], at(use, s))
                        act.activation(dst, cols, ACT.Copy, **kw).then_inc(sem[stage], 1)

                    if kind == "fold":
                        act.wait_ge(const_in, n_late)
                        act.activation(sgn[:, :], W("sig"), ACT.Sign)
                        act.activation(bo2x[:, :], W("bo_f1"), ACT.Copy, scale=2.0)
                        act.activation(rms1[:, :], W("rms"), ACT.Copy, bias=1.0).then_inc(sem["folded_act"], 1)
                    if kind == "load":
                        evac(ctxT[b][:, :], "ctxT_ps", bank("ctxT_ps", s)[:, 0:SEQ], "ctxT")
                    if kind == "bias":
                        evac(biasT[b][:, :, :], "biasT_ps", bank("biasT_ps", s)[:, :].rearrange("p (t q) -> p t q", t=NT), "biasT")
                    for n in "kq" if l != 2 else "":
                        (h0, h1), (m0, m1) = ((3, 6), (0, 2)) if n == "k" else ((1, 4), (0, 5))
                        takes = kind == (f"{n}_turn" if l == 1 else {"k": "kv", "q": "query"}[n])
                        if takes:
                            ready = f"{n}_ready" if l == 1 else f"{n}_in"
                            act.wait_ge(sem[ready], at(ready, s))
                            claim(act, f"{n}s", s)
                            parts(qf[b], held(stacks, f"{n}s", s), h0, h1).then_inc(sem[f"{n}_hi"], 1)
                        if kind == f"{n}_mid":
                            act.wait_ge(sem[f"{n}_rest"], at(f"{n}_rest", s))
                            if n == "q":
                                act.activation(held(stacks, "qs", s)[:, :, 0:5:4, :], heads(qr[b])[:, :, None, :].to_broadcast([P, NT * HEADS, 2, HD]), ACT.Copy)\
                                   .then_inc(sem["q_mid"], 1)
                            else:
                                parts(qr[b], held(stacks, "ks", s), m0, m1).then_inc(sem["k_mid"], 1)
                    if kind == "k_flip" and l != 2:
                        for g in range(2):
                            src = bank(f"kT{g}_ps", s)[:, :].bitcast(BF16).rearrange("p (j k) -> p j k", j=4)
                            evac(kT[b][:, 4 * g:4 * g + 4, :], f"kT{g}_ps", src, f"kT{g}")
                    if kind == "k_flip" and l == 2:
                        evac(k2T[b][0:MD, :], "kT2_ps", bank("kT2_ps", s)[0:MD, 0:SEQ], "kT0")
                    if kind == "flip":
                        evac(xT[b][:, :], "xT_ps", bank("xT_ps", s)[:, 0:SEQ], "xT")
                    if kind == "q_flip" and l != 2:
                        for g in range(2):
                            src = bank(f"qT{g}_ps", s)[:, :].bitcast(BF16).rearrange("p (j k) -> p j k", j=4)
                            evac(qT[b][:, 4 * g:4 * g + 4, :], f"qT{g}_ps", src, f"qT{g}")
                    if kind == "q_flip" and l == 2:
                        src = bank("qT2_ps", s)[0:MD, :].rearrange("p (h q) -> p h q", h=MQ)
                        act.wait_ge(sem["qT2_ps"], at("qT2_ps", s))
                        act.activation(q2T[b][0:MD, 0:2, :], src[:, 0:2, :], ACT.Copy).then_inc(sem["qT0"], 1)
                        act.activation(q2T[b][0:MD, 2:4, :], src[:, 2:4, :], ACT.Copy).then_inc(sem["qT1"], 1)
                    if kind == "shift_flip":
                        if l == 2:
                            evac(mT2[b][:, :], "shift_ps", bank("shift_ps", s)[0:8, 0:P], "shiftT")
                        else:
                            evac(mT[b][:, :], "shift_ps", bank("shift_ps", s)[0:32, 0:P].bitcast(BF16), "shiftT")
                    if kind == "attend":
                        if s[3] == 0:
                            act.wait_ge(sem["v"], at("v", ("kv", l, b)))
                            ended = [t for t in order[:order.index(s)] if t[0] == "divide"]
                            if ended:
                                act.wait_ge(sem["sums"], at("sums", ended[-1]))
                            if l == 2:
                                to = v2pad[:, :, :].rearrange("p t (j w) -> p t j w", j=2)
                                ins = act.activation(to[:, :, :, 0:MD], v2[b][:, :, None, :].to_broadcast([P, NT, 2, MD]), ACT.Copy)
                            else:
                                for t in range(NT):
                                    to = vpad[:, t].rearrange("p g (j w) -> p (g j) w", j=GROUP)
                                    ins = act.activation(to[:, :, 0:HD], v[b][:, t, :].rearrange("p (h d) -> p h d", d=HD), ACT.Copy)
                            ins.then_inc(sem["v_placed"], 1)
                        dst = held(probs, "probs_in", s)
                        if l != 0:
                            claim(act, "probs_in", s)
                        if l == 0:
                            act.wait_ge(sem["biased"], at("biased", s))
                            act.activation(dst[:, :, :], dst[:, :, :], ACT.Exp).then_inc(sem["probs"], 1)
                        else:
                            act.wait_ge(sem["scores_ps"], at("scores_ps", s))
                            w = 384 if l == 1 else 512
                            src = bank("scores_ps", s)[:, :].rearrange("p (r n) -> p r n", r=2)
                            act.activation(dst[:, :, 0:w], src[:, :, 0:w], ACT.Exp,
                                           scale=1.0 if l == 2 else HD ** -0.5).then_inc(sem["probs"], 1)
                    if kind == "divide":
                        act.wait_ge(sem["weighed"], at("weighed", ("attend", l, b, 7 if l != 2 else 1)))
                        rows = SROWS[l]
                        act.activation(weighed_sb[b][0:rows, :, :], pv[0:rows, :].rearrange("p (g q) -> p g q", g=2), ACT.Copy).then_inc(sem["sums"], 1)
                    if kind == "route" and l == 1:
                        act.wait_ge(sem["gate_in"], at("gate_in", s))
                        act.activation(ge[b][:, :, :], lg[b][:, :, :], ACT.Exp).then_inc(sem["gate_exp"], 1)
                    if kind == "choose":
                        rows = E * (2 if l == 1 else 3)
                        src = bank("onehotT_ps", s)[0:rows, 0:P].bitcast(BF16)
                        evac(ohT[b][0:rows, :], "onehotT_ps", src, "onehotT")
                        if l == 1:
                            evac(uT[b][:, :], "u_ps", bank("u_ps", s)[:, 0:SEQ], "u")
                    if kind in ("inner", "tail") and l > 0:
                        h = held(wides, "wide", s)[:, :, :].rearrange("p (i f) q -> p i f q", i=2)
                    if (kind, l) == ("inner", 1) or kind == "tail":
                        claim(act, "wide", s)
                    if kind == "inner" and l == 1:
                        for i in range(2):
                            act.wait_ge(sem[f"h{i}_ps"], at(f"h{i}_ps", s))
                            for ft in range(FT):
                                ins = act.activation(h[:, i, ft, :], bank("h0_ps", s)[:, ft * SEQ:(ft + 1) * SEQ],
                                                     ACT.Relu, bias=W("bi")[:, ft:ft + 1])
                            ins.then_inc(sem[f"h{i}"], 1)
                    if kind == "inner" and l == 2:
                        act.wait_ge(sem["h0_ps"], at("h0_ps", s))
                        act.activation(h[:, 0, :, :], bank("h0_ps", s)[:, :].rearrange("p (f q) -> p f q", f=FT), ACT.Gelu).then_inc(sem["h0"], 1)
                    if kind == "tail":
                        for i in range(2):
                            act.wait_ge(sem[f"h{i}_ps"], at(f"h{i}_ps", s))
                            act.activation(h[:, i, :, :], bank(f"h{i}_ps", s)[:, :].rearrange("p (f q) -> p f q", f=FT), ACT.Gelu_apprx_tanh).then_inc(sem[f"h{i}"], 1)

            @block.tensor
            def _(pe):
                ident = W("ident")

                def mm(dst, lhsT, rhs, start=True, stop=True, **kw):
                    return pe.matmul(dst, lhsT, rhs, start=start, stop=stop, **kw)

                for s in order:
                    kind, l, b = s[:3]
                    if kind == "fold":
                        pe.wait_ge(const_in, n_late)
                        pe.wait_ge(sem["folded_act"], at("folded_act", s))
                        pe.wait_ge(sem["folded_dve"], at("folded_dve", s))
                    if kind == "load":
                        pe.wait_ge(sem["ctx_in", b], 16)
                        claim(pe, "ctxT_ps", s)
                        for t in range(NT):
                            ins = pe.transpose(bank("ctxT_ps", s)[:, t * P:(t + 1) * P], cx[b][:, t, :], ident)
                        ins.then_inc(sem["ctxT_ps"], 1)
                    if kind == "bias":
                        pe.wait_ge(sem["bias"], at("bias", s))
                        claim(pe, "biasT_ps", s)
                        for k in range(NT):
                            for q in range(NT):
                                ins = pe.transpose(bank("biasT_ps", s)[:, k * SEQ + q * P:k * SEQ + (q + 1) * P],
                                                   held(wides, "mask", s)[:, NT + q, k * P:(k + 1) * P], ident)
                        pe.wait_ge(sem["bias_hi"], at("bias_hi", s))
                        pe.transpose(bank("biasT_ps", s)[:, 0:P], held(wides, "mask", s)[:, NT, 0:P], ident).then_inc(sem["biasT_ps"], 1)
                    if kind == "kv":
                        load = ("load", 0, b)
                        pe.wait_ge(sem["ctxT"], at("ctxT", load))
                        claim(pe, "kv_ps", s)
                        ps = bank("kv_ps", s)
                        for t in range(NT):
                            c = ctxT[b][:, t * P:(t + 1) * P]
                            if l == 2:
                                ins = mm(ps[:, t * 2 * MD:(t + 1) * 2 * MD], c, kvw2[:, :])
                            else:
                                mm(ps[:, t * P:(t + 1) * P], c, W(f"wk{l}"))
                                ins = mm(ps[:, SEQ + t * P:SEQ + (t + 1) * P], c, W(f"wv{l}"))
                        ins.then_inc(sem["kv_ps"], 1)
                    if kind == "k_flip":
                        if l == 2:
                            pe.wait_ge(sem["k_rot"], at("k_rot", s))
                            claim(pe, "kT2_ps", s)
                            for t in range(NT):
                                ins = pe.transpose(bank("kT2_ps", s)[0:MD, t * P:(t + 1) * P], k2[b][:, t, :], ident)
                            ins.then_inc(sem["kT2_ps"], 1)
                        else:
                            pe.wait_ge(sem["k_stack"], at("k_stack", s))
                            for g in range(2):
                                claim(pe, f"kT{g}_ps", s)
                                stack_transposes(pe, bank(f"kT{g}_ps", s), held(stacks, "ks", s), g).then_inc(sem[f"kT{g}_ps"], 1)
                    if kind == "flip":
                        pe.wait_ge(sem["x_normed"], at("x_normed", s))
                        claim(pe, "xT_ps", s)
                        for t in range(NT):
                            ins = pe.transpose(bank("xT_ps", s)[:, t * P:(t + 1) * P], xn[b][:, t, :], ident)
                        ins.then_inc(sem["xT_ps"], 1)
                    if kind == "query":
                        normed = ("norm", l, b)
                        pe.wait_ge(sem["xT"], at("xT", normed))
                        claim(pe, "q_ps", s)
                        wq = {0: wq0s[:, :], 1: W("wq1"), 2: qw2[:, :], 3: W("wq3")}[l]
                        for t in range(NT):
                            ins = mm(bank("q_ps", s)[:, t * P:(t + 1) * P], xT[b][:, t * P:(t + 1) * P], wq)
                        ins.then_inc(sem["q_ps"], 1)
                    if kind == "q_flip":
                        pe.wait_ge(sem["q_stack"], at("q_stack", s))
                        if l == 2:
                            claim(pe, "qT2_ps", s)
                            for hh in range(MQ):
                                for t in range(NT):
                                    ins = pe.transpose(bank("qT2_ps", s)[0:MD, hh * SEQ + t * P:hh * SEQ + (t + 1) * P],
                                                       q2[b][:, t, hh, :], ident)
                            ins.then_inc(sem["qT2_ps"], 1)
                        else:
                            for g in range(2):
                                claim(pe, f"qT{g}_ps", s)
                                stack_transposes(pe, bank(f"qT{g}_ps", s), held(stacks, "qs", s), g).then_inc(sem[f"qT{g}_ps"], 1)
                    if kind == "max":
                        part = s[3]
                        if part == 0:
                            q, k = ("query", l, b), ("kv", l, b)
                            pe.wait_ge(sem["qT1"], at("qT1", q))
                            if l == 2:
                                pe.wait_ge(sem["kT0"], at("kT0", k))
                                pe.wait_ge(sem["mask_row"], at("mask_row", k))
                            else:
                                pe.wait_ge(sem["kT1"], at("kT1", k))
                            if l == 0:
                                pe.wait_ge(sem["bias_hi"], at("bias_hi", ("load", 0, b)))
                        for i in range(2):
                            claim(pe, f"max{i}_ps", s)
                            ps = bank(f"max{i}_ps", s)
                            if l == 2:
                                t = part
                                for hh in range(2):
                                    ins = mm(ps[:, hh * SEQ:(hh + 1) * SEQ], q2T[b][0:MD + 1, 2 * i + hh, t * P:(t + 1) * P],
                                             k2T[b][0:MD + 1, :])
                                ins.then_inc(sem[f"max{i}_ps"], 1)
                                continue
                            t, jp, r = part // 4, part % 4, i
                            rows = slice(STK * r, STK * r + KD)
                            ps2 = ps[:, :].rearrange("p (h k) -> p h k", h=2)
                            kn = P if l == 1 and t == 0 else SEQ
                            if l == 0:
                                mm(ps2, identb[:, :], bias_hi[b][:, t, None, :].to_broadcast([P, 2, SEQ]), skip_group_check=True)
                            for hh in range(2):
                                j = 2 * jp + hh
                                ins = mm(ps2[:, hh, 0:kn], qT[b][rows, j, t * P:(t + 1) * P], kT[b][rows, j, 0:kn],
                                         start=(l == 3 or (l == 1 and hh == 0)), skip_group_check=True)
                            if l == 1:
                                ins = mm(ps2[:, :, t * P:(t + 1) * P], identb[:, :],
                                         trib[:, None, :].to_broadcast([P, 2, P]), start=False, skip_group_check=True)
                            ins.then_inc(sem[f"max{i}_ps"], 1)
                    if kind == "shift_flip":
                        pe.wait_ge(sem["shift"], at("shift", s))
                        claim(pe, "shift_ps", s)
                        if l == 2:
                            ins = pe.transpose(bank("shift_ps", s)[0:8, 0:P], nm2[b][:, :, :].rearrange("p t h -> p (t h)"), ident)
                        else:
                            ps = bank("shift_ps", s)[:, 0:P].bitcast(BF16)
                            for t in range(NT):
                                ins = pe.transpose(ps[0:32, t * P:(t + 1) * P], mp[b][:, t, :, :, :].rearrange("p r m j -> p (r m j)"), identb[:, :])
                        ins.then_inc(sem["shift_ps"], 1)
                    if kind == "attend":
                        part = s[3]
                        if part == 0:
                            pe.wait_ge(sem["shift_in", b], shift_at[b][l])
                        claim(pe, "scores_ps", s)
                        ps = bank("scores_ps", s)
                        for r in range(2):
                            for k in range(NT):
                                if l == 2:
                                    ins = mm(ps[:, r * 512 + k * SEQ:r * 512 + (k + 1) * SEQ], k2T[b][:, k * P:(k + 1) * P],
                                             q2T[b][:, 2 * part + r, :])
                                    continue
                                rows = slice(STK * r, STK * r + KD + 2)
                                q0 = P if l == 1 and k == 1 else 0
                                ins = mm(ps[:, r * 512 + k * SEQ:r * 512 + k * SEQ + SEQ - q0],
                                         kT[b][rows, part, k * P:(k + 1) * P], qT[b][rows, part, q0:SEQ],
                                         start=(l != 1 or k == 0), skip_group_check=True)
                            if l == 1:
                                diag = ps[:, r * 512:(r + 1) * 512].rearrange("p (k q) -> p k q", k=2)[:, :, 0:P]
                                ins = mm(diag, identb[:, :], triTb[:, None, :].to_broadcast([P, 2, P]),
                                         start=False, skip_group_check=True)
                        ins.then_inc(sem["scores_ps"], 1)
                    if kind == "weigh":
                        part = s[3]
                        if part == 0:
                            pe.wait_ge(sem["v_placed"], at("v_placed", ("attend", l, b, 0)))
                            ended = [t for t in order[:order.index(s)] if t[0] == "divide"]
                            if ended:
                                pe.wait_ge(sem["sums"], at("sums", ended[-1]))
                        pe.wait_ge(sem["probs"], at("probs", ("attend", *s[1:])))
                        pr = held(probs, "probs_in", s)
                        per = 2 if l == 2 else GROUP
                        for r in range(2):
                            hh = 2 * part + r
                            g, j = hh // per, hh % per
                            rows = SROWS[l]
                            for k in range(NT):
                                w = (v2pad[:, k, :] if l == 2 else vpad[:, k, g, :])[:, j * rows:(j + 1) * rows]
                                q0 = P if l == 1 and k == 1 else 0
                                ins = mm(pv[0:rows, g * SEQ + q0:(g + 1) * SEQ], w, pr[:, r, k * SEQ:k * SEQ + SEQ - q0],
                                         start=(j == 0 and k == 0), stop=(j == per - 1 and k == NT - 1), skip_group_check=True)
                        ins.then_inc(sem["weighed"], 1)
                    if kind == "o_flip":
                        pe.wait_ge(sem["sums"], at("sums", s))
                        claim(pe, "oT_ps", s)
                        rows = SROWS[l]
                        for i, n in enumerate(("o2", "r2") if l == 2 else ("o", "r")):
                            a, w = SPREAD_COLS[n]
                            for g in range(2):
                                ins = mm(bank("oT_ps", s)[g * w:(g + 1) * w, i * SEQ:(i + 1) * SEQ], spreads[0:rows, a:a + w],
                                         weighed_sb[b][0:rows, g, :])
                        ins.then_inc(sem["oT_ps"], 1)
                    if kind == "mix":
                        pe.wait_ge(sem["oT"], at("oT", s))
                        claim(pe, "y_ps", s)
                        for t in range(NT):
                            ins = mm(bank("y_ps", s)[:, t * P:(t + 1) * P], oT[b][:, t * P:(t + 1) * P], W("ow2" if l == 2 else f"wo{l}"))
                        ins.then_inc(sem["y_ps"], 1)
                    if kind == "route":
                        pe.wait_ge(sem["xT"], at("xT", ("norm", 4 + l, b)))
                        claim(pe, "logits_ps", s)
                        for t in range(NT):
                            w = {0: sgn[:, :], 1: W("gate"), 2: W("wr")}[l]
                            ins = mm(bank("logits_ps", s)[:, t * E:(t + 1) * E], xT[b][:, t * P:(t + 1) * P], w)
                        ins.then_inc(sem["logits_ps"], 1)
                    if kind == "choose":
                        n = E * (2 if l == 1 else 3)
                        pe.wait_ge(sem["onehot"], at("onehot", s))
                        claim(pe, "onehotT_ps", s)
                        ps = bank("onehotT_ps", s)[:, 0:P].bitcast(BF16)
                        for t in range(NT):
                            ins = pe.transpose(ps[0:n, t * P:(t + 1) * P], oh[b][:, t, :, :].rearrange("p s e -> p (s e)")[:, 0:n], identb[:, :])
                        ins.then_inc(sem["onehotT_ps"], 1)
                        if l == 1:
                            claim(pe, "u_ps", s)
                            mm(bank("u_ps", s)[:, 0:SEQ], W("loraA"), xT[b][:, :]).then_inc(sem["u_ps"], 1)
                    if kind == "spread":
                        if l == 1:
                            pe.wait_ge(sem["onehotT"], at("onehotT", s))
                            claim(pe, "pick_ps", s)
                            for i in range(2):
                                ins = mm(bank("pick_ps", s)[:, i * SEQ:(i + 1) * SEQ], pickb[:, i * P:(i + 1) * P], ohT[b][0:2 * E, :])
                            ins.then_inc(sem["pick_ps"], 1)
                        else:
                            pe.wait_ge(sem["onehotT"], at("onehotT", s))
                            for i in range(2):
                                claim(pe, f"spread{i}_ps", s)
                                for e in range(4):
                                    ins = mm(bank(f"spread{i}_ps", s)[:, e * SEQ:(e + 1) * SEQ],
                                             selb[:, (4 * i + e) * P:(4 * i + e + 1) * P], ohT[b][0:E, :])
                                ins.then_inc(sem[f"spread{i}_ps"], 1)
                    r = ("spread", l, b)
                    if kind == "inner":
                        if l == 1:
                            for i in range(2):
                                if i == 0:
                                    pe.wait_ge(sem["picked"], at("picked", r))
                                    claim(pe, "h0_ps", s)
                                else:
                                    pe.wait_ge(sem["h0"], at("h0", s))
                                for ft in range(FT):
                                    dst = bank("h0_ps", s)[:, ft * SEQ:(ft + 1) * SEQ]
                                    if i == 0:
                                        mm(dst, W("wi")[:, ft * P:(ft + 1) * P], xT[b][:, :], start=(ft % 2 == 0), stop=False,
                                           skip_group_check=True)
                                    ins = mm(dst, W("loraB")[:, ft * P:(ft + 1) * P], um[b][:, i, :], start=False, stop=True, skip_group_check=True)
                                ins.then_inc(sem[f"h{i}_ps"], 1)
                        if l == 2:
                            pe.wait_ge(sem["spread1"], at("spread1", r))
                            claim(pe, "h0_ps", s)
                            for ft in range(FT):
                                dst = bank("h0_ps", s)[:, ft * SEQ:(ft + 1) * SEQ]
                                mm(dst, biases("b1_f2")[:, ft * P:(ft + 1) * P], ohT[b][0:3 * E, :], stop=False)
                                for e in range(E):
                                    ins = mm(dst, W("w1_f2")[:, e * FF + ft * P:e * FF + (ft + 1) * P], held(wides, "wide", s)[:, e, :], start=False, stop=(e == E - 1))
                            ins.then_inc(sem["h0_ps"], 1)
                    if kind == "outer":
                        if l == 0:
                            pe.wait_ge(sem["spread1"], at("spread1", r))
                            claim(pe, "f_ps", s)
                            for t in range(NT):
                                dst = bank("f_ps", s)[:, t * P:(t + 1) * P]
                                mm(dst, ohT[b][0:3 * E, t * P:(t + 1) * P], biases("bf0"), stop=False)
                                for e in range(E):
                                    ins = mm(dst, held(wides, "wide", s)[:, e, t * P:(t + 1) * P], W("wf0")[:, e * P:(e + 1) * P], start=False, stop=(e == E - 1))
                            ins.then_inc(sem["f_ps"], 1)
                        if l > 0:
                            claim(pe, "f_ps", s)
                            n = "h_sum" if l == 1 else "h0"
                            pe.wait_ge(sem[n], at(n, s))
                            for t in range(NT):
                                for ft in range(FT):
                                    ins = mm(bank("f_ps", s)[:, t * P:(t + 1) * P], held(wides, "wide", s)[:, ft, t * P:(t + 1) * P],
                                             W(f"wo_f{l}")[:, ft * P:(ft + 1) * P], start=(ft == 0), stop=(ft == FT - 1))
                            ins.then_inc(sem["f_ps"], 1)
                    if kind == "tail":
                        pe.wait_ge(sem["xT"], at("xT", ("flip", 7, b)))
                        pe.wait_ge(sem["late_in"], 32)
                        for i in range(2):
                            claim(pe, f"h{i}_ps", s)
                            for ft in range(FT):
                                n = FT * i + ft
                                ins = mm(bank(f"h{i}_ps", s)[:, ft * SEQ:(ft + 1) * SEQ], late[0][:, n * P:(n + 1) * P], xT[b][:, :])
                            ins.then_inc(sem[f"h{i}_ps"], 1)
                        claim(pe, "f_ps", s)
                        for i in range(2):
                            pe.wait_ge(sem[f"h{i}"], at(f"h{i}", s))
                        for t in range(NT):
                            for n in range(FT3):
                                ins = mm(bank("f_ps", s)[:, t * P:(t + 1) * P], held(wides, "wide", s)[:, n, t * P:(t + 1) * P],
                                         late[1][:, n * P:(n + 1) * P], start=(n == 0), stop=(n == FT3 - 1))
                        ins.then_inc(sem["f_ps"], 1)

            @block.vector
            def _(dve):
                ch = Chain(dve, sem["dve"])
                V = nc.vector

                def half(ap):
                    return ap.rearrange("p (t d) -> p t d", t=NT)

                def layer_stats(src, b, m, sums):
                    for t in range(NT):
                        ch.link(V.bn_stats(sums[b][:, t, :], src[:, t, :]))
                    for t in range(NT):
                        ch.link(V.bn_aggr(m[b][:, t, :], sums[b][:, t, :]))

                for s in order:
                    kind, l, b = s[:3]
                    if kind == "fold":
                        dve.wait_ge(const_in, n_late)
                        for n in "qk":
                            c = W("cos1").rearrange("p (t d) -> p t d", t=NT)
                            sn = W("sin1").rearrange("p (t d) -> p t d", t=NT)
                            w = W(f"{n}nw")
                            H2 = HD // 2
                            V.tensor_tensor(wc[n][:, :, :], c, w[:, None, :].to_broadcast([P, NT, HD]), ALU.mult)
                            V.scalar_tensor_tensor(out=ws[n][:, :, 0:H2], in0=sn[:, :, 0:H2], scalar=-1.0,
                                                           in1=w[:, None, H2:HD].to_broadcast([P, NT, H2]),
                                                           op0=ALU.mult, op1=ALU.mult)
                            V.tensor_tensor(ws[n][:, :, H2:HD], sn[:, :, H2:HD],
                                                    w[:, None, 0:H2].to_broadcast([P, NT, H2]), ALU.mult)
                        ew = W("ew").rearrange("p (n k) -> p n k", k=2)
                        ch.link(V.tensor_tensor(wsum[:, :], ew[:, :, 0], ew[:, :, 1], ALU.add))
                        dve.wait_ge(sem["folded_act"], at("folded_act", s))
                        V.tensor_scalar(wsum[:, :], wsum[:, :], tg[:, 7:8], None, ALU.mult)
                        V.tensor_scalar(tbo[3][:, :], W("bo3"), tg[:, 3:4], None, ALU.mult)
                        V.tensor_scalar(tgam[:, :], W("gamma"), tg[:, 6:7], None, ALU.mult)
                        V.tensor_scalar(tbeta[:, :], W("beta"), tg[:, 6:7], None, ALU.mult)
                        V.tensor_scalar(qw2[:, :], W("qw2"), rms1[:, 0:1], None, ALU.mult)
                        V.tensor_scalar(kvw2[:, :], W("kvw2"), rms1[:, 0:1], None, ALU.mult).then_inc(sem["folded_dve"], 1)
                    if kind == "load":
                        dve.wait_ge(sem["ctx_in", b], 16)
                        layer_stats(cx[b], b, cmv, cst)
                        ch.link(V.tensor_tensor(crms[b][:, :], cmv[b][:, :, 0], cmv[b][:, :, 0], ALU.mult))
                        ch.link(V.tensor_tensor(crms[b][:, :], crms[b][:, :], cmv[b][:, :, 1], ALU.add))
                        V.tensor_scalar(crms[b][:, :], crms[b][:, :], 1e-6, None, ALU.add).then_inc(sem["ctx_var"], 1)
                    if kind == "kv":
                        dve.wait_ge(sem["kv_ps"], at("kv_ps", s))
                        ps = bank("kv_ps", s)
                        if l == 2:
                            dve.wait_ge(sem["ctx_rms"], at("ctx_rms", ("load", 0, b)))
                            for t in range(NT):
                                V.tensor_scalar(v2[b][:, t, :], ps[:, t * 2 * MD + MD:(t + 1) * 2 * MD], crms[b][:, t:t + 1], None, ALU.mult)\
                                 .then_inc(sem["v"] if t == NT - 1 else sem["dve"], 1)
                                if t < NT - 1:
                                    ch.n += 1
                            kk = kf[b][:, :, 0:MD]
                            for t in range(NT):
                                ins = V.tensor_scalar(kk[:, t, :], ps[:, t * 2 * MD:t * 2 * MD + MD], crms[b][:, t:t + 1], None, ALU.mult)
                                if t < NT - 1:
                                    ch.mark(ins)
                            ins.then_inc(sem["k_in"], 1)
                            dve.wait_ge(sem["k_in"], at("k_in", s))
                            half_turn(dve, ch, kk[:, :, None, :], kr[b][:, :, 0:MD].unsqueeze(2), k2[b][:, :, None, :], "ck2", "sk2", 1).then_inc(sem["k_rot"], 1)
                            dve.wait_ge(sem["row_in", b], 16)
                            ch.link(V.memset(k2T[b][MD:MD + 2, :], 1.0))
                            V.tensor_scalar(k2T[b][MD:MD + 1, :], mrow8[b][MD:MD + 1, :], 0.0, FILL, ALU.is_equal, ALU.mult).then_inc(sem["mask_row"], 1)
                        else:
                            vin = half(ps[:, SEQ:2 * SEQ])
                            vd = v[b]
                            if l == 1:
                                V.tensor_copy(vd[:, :, :], vin).then_inc(sem["v"], 1)
                                V.tensor_copy(kf[b][:, :, :], half(ps[:, 0:SEQ])).then_inc(sem["k_in"], 1)
                                dve.wait_ge(sem["k_in"], at("k_in", s))
                                rope_products(ch, "k", kf[b], kr[b], kt2[b], kss[b])
                            else:
                                V.tensor_tensor(vd[:, :, :], vin, W(f"bv{l}")[:, None, :].to_broadcast([P, NT, P]), ALU.add).then_inc(sem["v"], 1)
                                V.tensor_tensor(kf[b][:, :, :], half(ps[:, 0:SEQ]), W(f"bk{l}")[:, None, :].to_broadcast([P, NT, P]), ALU.add).then_inc(sem["k_in"], 1)
                    if kind == "stats":
                        prev = x_ready_from(s, order)
                        if prev:
                            dve.wait_ge(sem[prev[0]], at(*prev))
                        elif in_loop:
                            dve.wait_ge(sem["x_in", b], 16)
                        layer_stats(x[b], b, mv, st)
                        V.tensor_scalar(rstd[b][:, :], mv[b][:, :, 1], 1e-5, None, ALU.add).then_inc(sem["var"], 1)
                    if kind == "norm":
                        n = "rms" if l == 2 else "rstd"
                        dve.wait_ge(sem[n], at(n, ("stats", l, b)))
                        for t in range(NT):
                            ins = V.tensor_scalar(xn[b][:, t, :], x[b][:, t, :], mv[b][:, t, 0:1], rstd[b][:, t:t + 1], ALU.subtract, ALU.mult)
                            if t < NT - 1:
                                ch.mark(ins)
                        ins.then_inc(sem["x_normed"], 1)
                    if kind == "query":
                        dve.wait_ge(sem["q_ps"], at("q_ps", s))
                        ps = half(bank("q_ps", s)[:, 0:SEQ])
                        if l in (0, 3):
                            bq = bq0s[:, :] if l == 0 else W("bq3")
                            V.tensor_tensor(qf[b][:, :, :], ps, bq[:, None, :].to_broadcast([P, NT, P]), ALU.add).then_inc(sem["q_in"], 1)
                            dve.wait_ge(sem["q_in"], at("q_in", s))
                        else:
                            V.tensor_copy(qf[b][:, :, :], ps).then_inc(sem["q_in"], 1)
                            dve.wait_ge(sem["q_in"], at("q_in", s))
                        if l == 1:
                            rope_products(ch, "q", qf[b], qr[b], qt2[b], qss[b])
                        if l == 2:
                            q4 = qf[b][:, :, :].rearrange("p t (h d) -> p t h d", d=MD)
                            r4 = qr[b][:, :, :].rearrange("p t (h d) -> p t h d", d=MD)
                            ch.mark(V.memset(q2T[b][MD:MD + 2, :, :], 1.0))
                            half_turn(dve, ch, q4, r4, q2[b], "cq2", "sq2", MQ).then_inc(sem["q_stack"], 1)
                    for n in "kq" if l != 2 else "":
                        f, r, ss = qf, qr, {"k": kss, "q": qss}[n]
                        hi, mid, low = (3, 0, 2) if n == "k" else (1, 0, 5)
                        if kind == f"{n}_turn":
                            dve.wait_ge(sem[f"{n}_prod"], at(f"{n}_prod", s))
                            dve.wait_ge(sem[f"{n}_rms"], at(f"{n}_rms", s))
                            V.tensor_tensor(heads(f[b]), heads(r[b]), ss[b][:, :, None].to_broadcast([P, NT * HEADS, HD]), ALU.mult)\
                             .then_inc(sem[f"{n}_ready"], 1)
                        if kind == f"{n}_mid":
                            dve.wait_ge(sem[f"{n}_hi"], at(f"{n}_hi", s))
                            V.tensor_tensor(heads(r[b]), heads(f[b]), held(stacks, f"{n}s", s)[:, :, hi, :], ALU.subtract).then_inc(sem[f"{n}_rest"], 1)
                        if kind == f"{n}_low":
                            dve.wait_ge(sem[f"{n}_mid"], at(f"{n}_mid", s))
                            stack = held(stacks, f"{n}s", s)
                            V.tensor_tensor(stack[:, :, low, :], heads(r[b]), stack[:, :, mid, :], ALU.subtract).then_inc(sem[f"{n}_stack"], 1)
                    if kind == "max":
                        part = s[3]
                        for i in range(2):
                            dve.wait_ge(sem[f"max{i}_ps"], at(f"max{i}_ps", s))
                            ps = bank(f"max{i}_ps", s)[:, :].rearrange("p (h k) -> p h k", h=2)
                            if l == 2:
                                dst, kn = nm2[b][:, part, 2 * i:2 * i + 2], SEQ
                            else:
                                t, jp = part // 4, part % 4
                                dst, kn = nm[b][:, t, i, 2 * jp:2 * jp + 2], (P if l == 1 and t == 0 else SEQ)
                            V.tensor_reduce(dst, ps[:, :, 0:kn], AX.X, ALU.max, negate=True).then_inc(sem[f"max{i}"], 1)
                    if kind == "shift":
                        lastp = ("max", l, b, 7 if l != 2 else 1)
                        dve.wait_ge(sem["max0"], at("max0", lastp))
                        dve.wait_ge(sem["max1"], at("max1", lastp))
                        if l == 2:
                            V.tensor_copy(nm2[b][:, 0, 0:1], nm2[b][:, 0, 0:1]).then_inc(sem["shift"], 1)
                        else:
                            for t in range(NT):
                                ch.link(V.tensor_copy(mp[b][:, t, :, 0, :], nm[b][:, t, :, :]))
                            for t in range(NT):
                                ins = V.tensor_tensor(mp[b][:, t, :, 1, :], nm[b][:, t, :, :], mp[b][:, t, :, 0, :], ALU.subtract)
                                if t < NT - 1:
                                    ch.mark(ins)
                            ins.then_inc(sem["shift"], 1)
                    if kind == "attend" and l == 0:
                        claim(dve, "probs_in", s)
                        if s[3] == 0:
                            dve.wait_ge(sem["biasT"], at("biasT", ("load", 0, b)))
                        dve.wait_ge(sem["scores_ps"], at("scores_ps", s))
                        bt = biasT[b][:, :, :].rearrange("p k q -> p (k q)")
                        V.tensor_tensor(held(probs, "probs_in", s)[:, :, :], bank("scores_ps", s)[:, :].rearrange("p (r n) -> p r n", r=2),
                                        bt[:, None, :].to_broadcast([P, 2, 512]), ALU.add).then_inc(sem["biased"], 1)
                    if kind == "o_flip":
                        dve.wait_ge(sem["oT_ps"], at("oT_ps", s))
                        ps = bank("oT_ps", s)
                        over = qf[b][:, :, :].rearrange("p t d -> p (t d)")
                        ch.link(V.reciprocal(over, ps[:, SEQ:2 * SEQ]))
                        V.tensor_tensor(oT[b][:, :], ps[:, 0:SEQ], over, ALU.mult).then_inc(sem["oT"], 1)
                    if kind == "mix":
                        dve.wait_ge(sem["y_ps"], at("y_ps", s))
                        res = x
                        dve.wait_ge(sem["x_bias"], at("x_bias", ("stats", l, b)))
                        if l in (0, 3):
                            res = xb
                        V.scalar_tensor_tensor(out=x[b][:, :, :], in0=half(bank("y_ps", s)[:, 0:SEQ]), scalar=tg[:, l:l + 1],
                                               in1=res[b][:, :, :], op0=ALU.mult, op1=ALU.add).then_inc(sem["x_mixed"], 1)
                    if kind == "route":
                        dve.wait_ge(sem["logits_ps"], at("logits_ps", s))
                        ps = bank("logits_ps", s)[:, 0:NT * E].rearrange("p (t e) -> p t e", t=NT)
                        vals = lg
                        if l == 1:
                            V.tensor_tensor(lg[b][:, :, :], ps, W("gateb")[:, None, :].to_broadcast([P, NT, E]), ALU.add).then_inc(sem["logits"], 1)
                            dve.wait_ge(sem["logits"], at("logits", s))
                            ch.link(V.tensor_reduce(gm[b][:, :], lg[b][:, :, :], AX.X, ALU.max))
                            V.tensor_tensor(lg[b][:, :, :], lg[b][:, :, :], gm[b][:, :, None].to_broadcast([P, NT, E]), ALU.subtract).then_inc(sem["gate_in"], 1)
                            dve.wait_ge(sem["gate_exp"], at("gate_exp", s))
                            vals = ge
                        else:
                            V.tensor_copy(lg[b][:, :, :], ps).then_inc(sem["logits"], 1)
                            dve.wait_ge(sem["logits"], at("logits", s))
                        for t in range(NT):
                            ch.link(V.max(mx[b][:, t, :], vals[b][:, t, :]))
                        for t in range(NT):
                            ch.link(V.max_index(ix[b][:, t, :], mx[b][:, t, :], vals[b][:, t, :]))
                        ch.link(V.tensor_copy(ixf[b][:, :, :], ix[b][:, :, :]))
                        ns = 2 if l == 1 else 1
                        for t in range(NT):
                            for i in range(ns):
                                if l == 1:
                                    ins = V.tensor_scalar(oh[b][:, t, i, :], W("iota"), ixf[b][:, t, i:i + 1], None, ALU.is_equal)
                                else:
                                    ins = V.tensor_scalar(oh[b][:, t, :, :], W("iota")[:, None, :].to_broadcast([P, 3, E]),
                                                          ixf[b][:, t, 0:1], None, ALU.is_equal)
                                if (t, i) != (NT - 1, ns - 1):
                                    ch.mark(ins)
                        ins.then_inc(sem["onehot"], 1)
                        if l == 1:
                            ch.link(V.tensor_reduce(gs[b][:, :], ge[b][:, :, :], AX.X, ALU.add))
                            ch.link(V.reciprocal(gs[b][:, :], gs[b][:, :]))
                            ch.link(V.tensor_tensor(gv[b][:, :], mx[b][:, :, 0], mx[b][:, :, 1], ALU.add))
                            ch.link(V.scalar_tensor_tensor(out=gv[b][:, :], in0=gv[b][:, :], scalar=tg[:, 5:6], in1=gs[b][:, :], op0=ALU.mult, op1=ALU.mult))
                    if kind == "spread":
                        if l == 1:
                            dve.wait_ge(sem["u"], at("u", s))
                            dve.wait_ge(sem["pick_ps"], at("pick_ps", s))
                            V.tensor_tensor(um[b][:, :, :], bank("pick_ps", s)[:, :].rearrange("p (i q) -> p i q", i=2),
                                            uT[b][:, None, :].to_broadcast([P, 2, SEQ]), ALU.mult).then_inc(sem["picked"], 1)
                        else:
                            for i in range(2):
                                dve.wait_ge(sem[f"spread{i}_ps"], at(f"spread{i}_ps", s))
                                if i == 0:
                                    claim(dve, "wide", s)
                                V.tensor_tensor(held(wides, "wide", s)[:, 4 * i:4 * i + 4, :], bank(f"spread{i}_ps", s)[:, :].rearrange("p (e q) -> p e q", e=4),
                                                xT[b][:, None, :].to_broadcast([P, 4, SEQ]), ALU.mult).then_inc(sem[f"spread{i}"], 1)
                    if kind == "outer":
                        dve.wait_ge(sem["f_ps"], at("f_ps", s))
                        dve.wait_ge(sem["x_bias"], at("x_bias", ("stats", 4 + l, b)))
                        ps = half(bank("f_ps", s)[:, 0:SEQ])
                        if l == 0:
                            V.scalar_tensor_tensor(out=x[b][:, :, :], in0=ps, scalar=tg[:, 4:5], in1=x[b][:, :, :],
                                                   op0=ALU.mult, op1=ALU.add).then_inc(sem["x_fed"], 1)
                        if l == 1:
                            V.tensor_tensor(y[b][:, :, :], ps, bo2x[:, None, :].to_broadcast([P, NT, P]), ALU.add).then_inc(sem["f_in"], 1)
                            dve.wait_ge(sem["f_in"], at("f_in", s))
                            for t in range(NT):
                                ins = V.scalar_tensor_tensor(out=x[b][:, t, :], in0=y[b][:, t, :], scalar=gv[b][:, t:t + 1], in1=x[b][:, t, :],
                                                             op0=ALU.mult, op1=ALU.add)
                                if t < NT - 1:
                                    ch.mark(ins)
                            ins.then_inc(sem["x_fed"], 1)
                        if l == 2:
                            dve.wait_ge(sem["y_res"], at("y_res", s))
                            V.tensor_tensor(y[b][:, :, :], ps, yr[b][:, :, :], ALU.add).then_inc(sem["f_in"], 1)
                            dve.wait_ge(sem["f_in"], at("f_in", s))
                            layer_stats(y[b], b, mv, st)
                            V.tensor_scalar(rstd[b][:, :], mv[b][:, :, 1], 1e-12, None, ALU.add).then_inc(sem["y_var"], 1)
                    if kind == "finish":
                        if l == 2:
                            dve.wait_ge(sem["y_rstd"], at("y_rstd", s))
                            for t in range(NT):
                                ch.link(V.tensor_scalar(y[b][:, t, :], y[b][:, t, :], mv[b][:, t, 0:1], rstd[b][:, t:t + 1], ALU.subtract, ALU.mult))
                            ch.link(V.tensor_tensor(y[b][:, :, :], y[b][:, :, :], tgam[:, None, :].to_broadcast([P, NT, P]), ALU.mult))
                            V.tensor_tensor(x[b][:, :, :], y[b][:, :, :], xb[b][:, :, :], ALU.add).then_inc(sem["x_fed"], 1)
                    if kind == "tail":
                        dve.wait_ge(sem["f_ps"], at("f_ps", s))
                        dve.wait_ge(sem["x_bias"], at("x_bias", ("stats", 7, b)))
                        for t in range(NT):
                            n = b * NT + t
                            ins = V.scalar_tensor_tensor(out=x[b][:, t, :], in0=bank("f_ps", s)[:, t * P:(t + 1) * P], scalar=wsum[:, n:n + 1],
                                                         in1=x[b][:, t, :], op0=ALU.mult, op1=ALU.add)
                            if t < NT - 1:
                                ch.mark(ins)
                        ins.then_inc(sem["x_fed"], 1)

        with nc.Fori(0, TURNS) as i:
            with nc.Block() as block:
                programs(block, turn, plan, (TURNS - 1 - i) * ROWS, True)
            nc.all_engine_barrier(sems_to_clear=all_sems)

        if SUBLAYERS == 8:
            with nc.Block() as block:
                programs(block, tail, tail_plan, 0, False)



def kernel(**inputs):
    import numpy as np
    import concourse.bacc as _bacc
    from concourse import mybir as _mybir
    from concourse.bass_utils import run_bass_kernel_spmd as _run

    a = {k: np.asarray(v) for k, v in inputs.items()}
    f = np.float32

    def rows(n):
        return np.broadcast_to(a[n].reshape(1, -1), (P, a[n].size))

    def tiles(w):
        return w.reshape(-1, P, w.shape[-1]).transpose(1, 0, 2).reshape(P, -1)

    pos = np.arange(SEQ, dtype=f)

    def spread(t):
        return tiles(np.ascontiguousarray(t.astype(f)))

    inv1 = (1.0 / np.power(f(500000.0), np.arange(0, HD, 2, dtype=f) / f(HD))).astype(f)
    ang1 = np.outer(pos, inv1).astype(f)
    emb1 = np.concatenate([ang1, ang1], -1)
    ts2 = np.power(f(10000.0), f(2.0 / MD) * np.arange(MD // 2, dtype=f)).astype(f)
    angk = (pos[:, None] / ts2).astype(f)
    angq = ((pos + SEQ)[:, None] / ts2).astype(f)
    sc = MD ** -0.5
    cos2, sin2 = (lambda g: np.concatenate([np.cos(g), np.cos(g)], -1)), (lambda g: np.concatenate([-np.sin(g), np.sin(g)], -1))
    i, j = np.arange(P)[:, None], np.arange(P)[None, :]
    tri = np.where(j <= i, 0.0, NEG).astype(f)
    ex = {
        "ident": np.eye(P, dtype=f), "tri": tri, "triT": np.ascontiguousarray(tri.T),
        "iota": np.broadcast_to(np.arange(E, dtype=f), (P, E)),
        "g": np.broadcast_to(np.concatenate([a["g_xattn"], a["g_ffn"]])[None], (P, 8)),
        "adj": tiles(a["L0_xattn_adj"]),
        "sig": a["L0_ffn_tile_sigs"].T, "wf0": a["L0_ffn_W"].transpose(1, 0, 2).reshape(P, -1),
        "qnw": rows("L1_xattn_q_norm_w"), "knw": rows("L1_xattn_k_norm_w"),
        "cos1": spread(np.cos(emb1)), "sin1": spread(np.sin(emb1)),
        "wi": a["L1_ffn_wi"].T, "bi": a["L1_ffn_bi"].reshape(FT, P).T, "wo_f1": tiles(a["L1_ffn_wo"].T), "bo_f1": rows("L1_ffn_bo"),
        "loraA": a["L1_ffn_lora_A"].reshape(P, P).T, "loraB": a["L1_ffn_lora_B"].transpose(0, 2, 1).reshape(P, FF),
        "gate": a["L1_ffn_gate_w"].T, "gateb": rows("L1_ffn_gate_b"),
        "rms": a["L2_xattn_rms_scale"].reshape(P, 1), "qw2": a["L2_xattn_q_w"].transpose(1, 0, 2).reshape(P, P),
        "kvw2": a["L2_xattn_kv_w"][:, 0].transpose(1, 0, 2).reshape(P, 2 * MD), "ow2": a["L2_xattn_out_w"].reshape(P, P),
        "cq2": spread(cos2(angq) * sc), "sq2": spread(sin2(angq) * sc), "ck2": spread(cos2(angk)), "sk2": spread(sin2(angk)),
        "wr": a["L2_ffn_Wr"].T, "w1_f2": a["L2_ffn_W1"].transpose(1, 0, 2).reshape(P, -1), "wo_f2": tiles(a["L2_ffn_Wo"]),
        "bo_f2": rows("L2_ffn_bo"), "gamma": rows("L2_ffn_gamma"), "beta": rows("L2_ffn_beta"),
        "ew": tiles(a["L3_ffn_expert_weights"]),
    }
    for l in (0, 1, 3):
        for n in "qkvo":
            ex[f"w{n}{l}"] = a[f"L{l}_xattn_W{n}"].T
            if l != 1:
                ex[f"b{n}{l}"] = rows(f"L{l}_xattn_b{n}")
    arrays = {n: np.concatenate([ex[m] for m, _ in parts], axis=1) for n, parts in PACKS.items()}
    sel = np.zeros((16, E, P), f)
    for e in range(E):
        sel[e, e, :] = 1.0
    pick = np.zeros((2, 16, P), f)
    for c in range(2):
        for e in range(E):
            pick[c, c * E + e, e * RANK:(e + 1) * RANK] = 1.0
            pick[1, e, e * RANK:(e + 1) * RANK] = -1.0
    spreads = np.zeros((GROUP * (HD + 1), SPREAD_W), f)
    for n, m, d in (("", GROUP, HD), ("2", MQ // 2, MD)):
        for j in range(m):
            for i in range(d):
                spreads[j * (d + 1) + i, SPREAD_COLS["o" + n][0] + j * d + i] = 1.0
                spreads[j * (d + 1) + d, SPREAD_COLS["r" + n][0] + j * d + i] = 1.0
    arrays |= {"small": np.concatenate([np.tile(a["L0_ffn_b"], (3, 1)), np.tile(a["L2_ffn_b1"], (3, 1)), np.repeat(np.eye(3, dtype=f), E, 0)], axis=1), "spreads": spreads,
               "picks": np.concatenate([sel.reshape(16, -1), pick[0], pick[1]], axis=1),
               "late": np.concatenate([a["L3_ffn_w1"], tiles(a["L3_ffn_w2"])], axis=1), "x": a["x"], "ctx": a["ctx_1024"], "mask": a["mask_Bx1xSxS2_ik1"][:, 0],
               "mrow": a["mask_BxS2_bk0"]}
    arrays = {n: np.ascontiguousarray(v) for n, v in arrays.items()}

    nc = _bacc.Bacc("TRN2", target_bir_lowering=False, num_devices=1)
    dram = {n: nc.dram_tensor(f"in_{n}", v.shape, _mybir.dt.from_np(v.dtype), kind="ExternalInput").ap() for n, v in arrays.items()}
    out = nc.dram_tensor("out", (BATCH, SEQ, P), _mybir.dt.float32, kind="ExternalOutput").ap()
    build(nc, dram, out)
    r = _run(nc, [{f"in_{n}": v for n, v in arrays.items()}], core_ids=[0])
    return r.results[0]["out"]
```
